# Optimizing a Trainium2 kernel written in Bass

```python
import numpy as np
import jax
import jax.numpy as jnp

def _softmax(x, axis=-1):
    return jax.nn.softmax(x, axis=axis)

def _gelu(x):
    return jax.nn.gelu(x, approximate=True)

def _silu(x):
    return jax.nn.silu(x)

def _sigmoid(x):
    return jax.nn.sigmoid(x)

def _layernorm(x, axis=-1, eps=1e-05):
    m = jnp.mean(x, axis=axis, keepdims=True)
    v = jnp.var(x, axis=axis, keepdims=True)
    return (x - m) / jnp.sqrt(v + eps)

def _scatter_add(tgt, idx, src, axis=0):
    return tgt.at[idx].add(src)

def _segment_sum(src, seg, n):
    return jax.ops.segment_sum(src, seg, n)
kernel_name = 'mk_decoder_postln_d2_seqx_r4_847a3f'

def setup_inputs(seed: int=0):
    np.random.seed(seed)
    _w = jnp.asarray

    def _rec_inputs():
        import jax
        import jax.numpy as jnp
        _rk = jax.random.key(seed)
        x = -0.0002928 + 1 * jax.random.normal(jax.random.fold_in(_rk, 1), (16, 128, 512), jnp.float32)
        _lenS = 128 - jax.random.randint(jax.random.fold_in(_rk, 7), (16,), 0, max(1, 128 // 4) + 1, jnp.int32)
        _lenS2 = 128 - jax.random.randint(jax.random.fold_in(_rk, 8), (16,), 0, max(1, 128 // 4) + 1, jnp.int32)
        _ctx_512P = jax.random.normal(jax.random.fold_in(_rk, 11), (16, 16, 128), jnp.float32)
        _ctx_512c = jax.random.dirichlet(jax.random.fold_in(_rk, 511), 0.3 * jnp.ones((16,), jnp.float32), (16, 128))
        _ctx_512t = jnp.einsum('bsk,bkd->bsd', _ctx_512c, _ctx_512P)
        _ctx_512t = _ctx_512t * jax.lax.rsqrt(jnp.mean(jnp.square(_ctx_512t)) + 1e-12) * 0.953939
        ctx_512 = 0.000227908 + 0.99994 * (_ctx_512t + 0.3 * jax.random.normal(jax.random.fold_in(_rk, 611), (16, 128, 128), jnp.float32))
        return (x, ctx_512)
    x, ctx_512 = _rec_inputs()

    def _L0_attn_setup():
        import jax, jax.numpy as jnp
        import numpy as np
        DIM = 512
        H = 16
        KV = 4
        D = DIM // H
        G = H // KV
        ROPE_MAX = 512

        def _rope_cache():
            inv_freq = 1.0 / 10000.0 ** (jnp.arange(0, D, 2, dtype=jnp.float32) / D)
            t = jnp.arange(ROPE_MAX, dtype=jnp.float32)
            freqs = jnp.einsum('i,j->ij', t, inv_freq)
            emb = jnp.concatenate([freqs, freqs], axis=-1)
            return (jnp.cos(emb)[None, None], jnp.sin(emb)[None, None])

        def _rotate_half(x):
            x1, x2 = jnp.split(x, 2, axis=-1)
            return jnp.concatenate([-x2, x1], axis=-1)
        key = jax.random.key(seed)
        ks = jax.random.split(key, 9)
        s = 0.02
        return {'x': jax.random.normal(ks[0], (2, 512, DIM), dtype=jnp.float32), 'wq': jax.random.normal(ks[1], (DIM, DIM), dtype=jnp.float32) * s, 'bq': jax.random.normal(ks[2], (DIM,), dtype=jnp.float32) * s, 'wk': jax.random.normal(ks[3], (D * KV, DIM), dtype=jnp.float32) * s, 'bk': jax.random.normal(ks[4], (D * KV,), dtype=jnp.float32) * s, 'wv': jax.random.normal(ks[5], (D * KV, DIM), dtype=jnp.float32) * s, 'bv': jax.random.normal(ks[6], (D * KV,), dtype=jnp.float32) * s, 'wo': jax.random.normal(ks[7], (DIM, DIM), dtype=jnp.float32) * s, 'bo': jax.random.normal(ks[8], (DIM,), dtype=jnp.float32) * s}
    _L0_attn_all = _L0_attn_setup()
    _L0_attn_in = {k: v for k, v in _L0_attn_all.items() if k in ('wq', 'bq', 'wk', 'bk', 'wv', 'bv', 'wo', 'bo')}
    del _L0_attn_all

    def _L0_xattn_setup():
        import jax, jax.numpy as jnp
        import numpy as np
        B, S, L = (2, 256, 256)
        DIM_Q, H, K, D_C, D_CQ, R = (512, 16, 128, 128, 384, 64)

        def _rope_tables(seq_len, dim, dtype):
            inv_freq = 1.0 / 10000.0 ** (jnp.arange(0, dim, 2, dtype=dtype) / dim)
            t = jnp.arange(seq_len, dtype=dtype)
            freqs = t[:, None] * inv_freq[None, :]
            sin = jnp.repeat(jnp.sin(freqs), 2, axis=-1)
            cos = jnp.repeat(jnp.cos(freqs), 2, axis=-1)
            return (sin, cos)

        def _rotate_half(x):
            h = x.shape[-1] // 2
            return jnp.concatenate([-x[..., h:], x[..., :h]], axis=-1)
        key = jax.random.key(seed)
        ks = jax.random.split(key, 8)
        s_in = 1.0 / np.sqrt(DIM_Q)
        s_k = 1.0 / np.sqrt(K)
        s_cq = 1.0 / np.sqrt(D_CQ)
        s_c = 1.0 / np.sqrt(D_C)
        return {'hidden_q': jax.random.normal(ks[0], (B, S, DIM_Q), jnp.float32), 'kv_c': jax.random.normal(ks[1], (B, L, D_C), jnp.float32), 'Wq': jax.random.normal(ks[2], (H * K, DIM_Q), jnp.float32) * s_in, 'w_kc_q': jax.random.normal(ks[3], (H, K, D_CQ), jnp.float32) * s_k, 'w_kc_kv': jax.random.normal(ks[4], (H, K, D_C), jnp.float32) * s_k, 'W_qr': jax.random.normal(ks[5], (H, D_CQ, R), jnp.float32) * s_cq / np.sqrt(R), 'W_kr': jax.random.normal(ks[6], (H, D_C, R), jnp.float32) * s_c, 'Wo': jax.random.normal(ks[7], (DIM_Q, H * K), jnp.float32) * s_k}
    _L0_xattn_all = _L0_xattn_setup()
    _L0_xattn_in = {k: v for k, v in _L0_xattn_all.items() if k in ('Wq', 'w_kc_q', 'w_kc_kv', 'W_qr', 'W_kr', 'Wo')}
    del _L0_xattn_all

    def _L0_ffn_setup():
        import jax, jax.numpy as jnp
        import numpy as np
        EPS = 1e-08

        def _quantize(w):
            gamma = jnp.mean(jnp.abs(w))
            return jnp.clip(jnp.round(w / (gamma + EPS)), -1.0, 1.0)

        def _bitlinear(x, w):
            return jnp.matmul(x, _quantize(w).T)
        key = jax.random.key(seed)
        k1, k2, k3, k4 = jax.random.split(key, 4)
        d, h = (512, 1408)
        x = jax.random.normal(k1, (4, 512, d), dtype=jnp.float32)
        w1 = jax.random.normal(k2, (h, d), dtype=jnp.float32)
        w2 = jax.random.normal(k3, (h, d), dtype=jnp.float32)
        w3 = jax.random.normal(k4, (d, h), dtype=jnp.float32)
        return {'x': x, 'w1': w1, 'w2': w2, 'w3': w3}
    _L0_ffn_all = _L0_ffn_setup()
    _L0_ffn_in = {k: v for k, v in _L0_ffn_all.items() if k in ('w1', 'w2', 'w3')}
    del _L0_ffn_all

    def _L1_attn_setup():
        import math
        import jax, jax.numpy as jnp
        import numpy as np
        BLOCK = 64

        def build_slope_tensor(n_heads):

            def p2(n):
                start = 2.0 ** (-2.0 ** (-(math.log2(n) - 3)))
                return [start * start ** i for i in range(n)]
            if math.log2(n_heads).is_integer():
                s = p2(n_heads)
            else:
                closest = 2 ** math.floor(math.log2(n_heads))
                s = p2(closest) + p2(2 * closest)[0::2][:n_heads - closest]
            return jnp.asarray(np.array(s, dtype=np.float32))

        def lightning_attn(q, k, v, slopes, block=BLOCK):
            B, H, N, d = q.shape
            nc = N // block
            i = jnp.arange(block, dtype=q.dtype)
            diff = i[:, None] - i[None, :]
            intra_decay = jnp.where(diff >= 0, jnp.exp(-slopes[:, None, None] * diff), 0.0)
            q_decay = jnp.exp(-slopes[:, None] * i[None, :])
            k_decay = jnp.exp(-slopes[:, None] * (block - i[None, :]))
            blk_decay = jnp.exp(-slopes * block)

            def to_chunks(t):
                return t.reshape(B, H, nc, block, d).transpose(2, 0, 1, 3, 4)
            qc, kc, vc = (to_chunks(q), to_chunks(k), to_chunks(v))

            def body(S, xs):
                qb, kb, vb = xs
                scores = jnp.einsum('bhid,bhjd->bhij', qb, kb) * intra_decay[None]
                o_intra = jnp.einsum('bhij,bhjd->bhid', scores, vb)
                o_inter = jnp.einsum('bhid,bhde->bhie', qb * q_decay[None, :, :, None], S)
                S_new = blk_decay[None, :, None, None] * S + jnp.einsum('bhjd,bhje->bhde', kb * k_decay[None, :, :, None], vb)
                return (S_new, o_intra + o_inter)
            S0 = jnp.zeros((B, H, d, d), dtype=q.dtype)
            _, o = jax.lax.scan(body, S0, (qc, kc, vc))
            return o.transpose(1, 2, 0, 3, 4).reshape(B, H, N, d)
        key = jax.random.key(seed)
        k1, k2, k3 = jax.random.split(key, 3)
        dim, num_heads = (512, 16)
        B, N = (2, 1024)
        x = jax.random.normal(k1, (B, N, dim), dtype=jnp.float32)
        Wqkv = jax.random.normal(k2, (dim, 3 * dim), dtype=jnp.float32) / math.sqrt(dim)
        bqkv = jnp.zeros((3 * dim,), dtype=jnp.float32)
        Wout = jax.random.normal(k3, (dim, dim), dtype=jnp.float32) / math.sqrt(dim)
        bout = jnp.zeros((dim,), dtype=jnp.float32)
        slopes = build_slope_tensor(num_heads)
        return {'x': x, 'Wqkv': Wqkv, 'bqkv': bqkv, 'Wout': Wout, 'bout': bout, 'slopes': slopes}
    _L1_attn_all = _L1_attn_setup()
    _L1_attn_in = {k: v for k, v in _L1_attn_all.items() if k in ('Wqkv', 'bqkv', 'Wout', 'bout', 'slopes')}
    del _L1_attn_all

    def _L1_xattn_setup():
        import jax, jax.numpy as jnp
        import numpy as np
        B, S, H, NH, L = (2, 512, 512, 16, 128)
        HD = H // NH
        key = jax.random.key(seed)
        k1, k2, k3, k4, k5 = jax.random.split(key, 5)
        scale = 0.02
        return {'q': jax.random.normal(k1, (B, S, H), dtype=jnp.float32), 'latent_kv': jax.random.normal(k2, (B, S, L), dtype=jnp.float32), 'Wq': jax.random.normal(k3, (H, H), dtype=jnp.float32) * scale, 'Wkv_expand': jax.random.normal(k4, (2 * H, L), dtype=jnp.float32) * scale, 'Wout': jax.random.normal(k5, (H, H), dtype=jnp.float32) * scale}
    _L1_xattn_all = _L1_xattn_setup()
    _L1_xattn_in = {k: v for k, v in _L1_xattn_all.items() if k in ('Wq', 'Wkv_expand', 'Wout')}
    del _L1_xattn_all

    def _L1_ffn_setup():
        import jax, jax.numpy as jnp
        import numpy as np
        TOP_K = 2
        key = jax.random.key(seed)
        ks = jax.random.split(key, 6)
        B, S, H, F, E = (1, 512, 512, 352, 8)
        Fs = 2 * F
        std = jnp.float32(0.02)
        return {'hidden_states': jax.random.normal(ks[0], (B, S, H), jnp.float32), 'gate_weight': jax.random.normal(ks[1], (E, H), jnp.float32) * std, 'gate_up_weights': jax.random.normal(ks[2], (E, 2 * F, H), jnp.float32) * std, 'down_weights': jax.random.normal(ks[3], (E, H, F), jnp.float32) * std, 'shared_gate_up': jax.random.normal(ks[4], (2 * Fs, H), jnp.float32) * std, 'shared_down': jax.random.normal(ks[5], (H, Fs), jnp.float32) * std}
    _L1_ffn_all = _L1_ffn_setup()
    _L1_ffn_in = {k: v for k, v in _L1_ffn_all.items() if k in ('gate_weight', 'gate_up_weights', 'down_weights', 'shared_gate_up', 'shared_down')}
    del _L1_ffn_all
    return {'x': x, 'ctx_512': ctx_512, 'L0_attn_wq': _L0_attn_in['wq'], 'L0_attn_bq': _L0_attn_in['bq'], 'L0_attn_wk': _L0_attn_in['wk'], 'L0_attn_bk': _L0_attn_in['bk'], 'L0_attn_wv': _L0_attn_in['wv'], 'L0_attn_bv': _L0_attn_in['bv'], 'L0_attn_wo': _L0_attn_in['wo'], 'L0_attn_bo': _L0_attn_in['bo'], 'L0_xattn_Wq': _L0_xattn_in['Wq'], 'L0_xattn_w_kc_q': _L0_xattn_in['w_kc_q'], 'L0_xattn_w_kc_kv': _L0_xattn_in['w_kc_kv'], 'L0_xattn_W_qr': _L0_xattn_in['W_qr'], 'L0_xattn_W_kr': _L0_xattn_in['W_kr'], 'L0_xattn_Wo': _L0_xattn_in['Wo'], 'L0_ffn_w1': _L0_ffn_in['w1'], 'L0_ffn_w2': _L0_ffn_in['w2'], 'L0_ffn_w3': _L0_ffn_in['w3'], 'L1_attn_Wqkv': _L1_attn_in['Wqkv'], 'L1_attn_bqkv': _L1_attn_in['bqkv'], 'L1_attn_Wout': _L1_attn_in['Wout'], 'L1_attn_bout': _L1_attn_in['bout'], 'L1_attn_slopes': _L1_attn_in['slopes'], 'L1_xattn_Wq': _L1_xattn_in['Wq'], 'L1_xattn_Wkv_expand': _L1_xattn_in['Wkv_expand'], 'L1_xattn_Wout': _L1_xattn_in['Wout'], 'L1_ffn_gate_weight': _L1_ffn_in['gate_weight'], 'L1_ffn_gate_up_weights': _L1_ffn_in['gate_up_weights'], 'L1_ffn_down_weights': _L1_ffn_in['down_weights'], 'L1_ffn_shared_gate_up': _L1_ffn_in['shared_gate_up'], 'L1_ffn_shared_down': _L1_ffn_in['shared_down']}

def reference(x, ctx_512, L0_attn_wq, L0_attn_bq, L0_attn_wk, L0_attn_bk, L0_attn_wv, L0_attn_bv, L0_attn_wo, L0_attn_bo, L0_xattn_Wq, L0_xattn_w_kc_q, L0_xattn_w_kc_kv, L0_xattn_W_qr, L0_xattn_W_kr, L0_xattn_Wo, L0_ffn_w1, L0_ffn_w2, L0_ffn_w3, L1_attn_Wqkv, L1_attn_bqkv, L1_attn_Wout, L1_attn_bout, L1_attn_slopes, L1_xattn_Wq, L1_xattn_Wkv_expand, L1_xattn_Wout, L1_ffn_gate_weight, L1_ffn_gate_up_weights, L1_ffn_down_weights, L1_ffn_shared_gate_up, L1_ffn_shared_down):
    import jax
    import jax.numpy as jnp

    def _L0_attn_ref(x, wq, bq, wk, bk, wv, bv, wo, bo):
        import jax, jax.numpy as jnp
        import numpy as np
        DIM = 512
        H = 16
        KV = 4
        D = DIM // H
        G = H // KV
        ROPE_MAX = 512

        def _rope_cache():
            inv_freq = 1.0 / 10000.0 ** (jnp.arange(0, D, 2, dtype=jnp.float32) / D)
            t = jnp.arange(ROPE_MAX, dtype=jnp.float32)
            freqs = jnp.einsum('i,j->ij', t, inv_freq)
            emb = jnp.concatenate([freqs, freqs], axis=-1)
            return (jnp.cos(emb)[None, None], jnp.sin(emb)[None, None])

        def _rotate_half(x):
            x1, x2 = jnp.split(x, 2, axis=-1)
            return jnp.concatenate([-x2, x1], axis=-1)
        B, T, C = x.shape
        scale = D ** (-0.5)
        q = (x @ wq.T + bq).reshape(B, T, H, D)
        k = (x @ wk.T + bk).reshape(B, T, KV, D)
        v = (x @ wv.T + bv).reshape(B, T, KV, D)
        cos, sin = _rope_cache()
        cos_q, sin_q = (cos[..., :H, :], sin[..., :H, :])
        q = q * cos_q + _rotate_half(q) * sin_q
        cos_k, sin_k = (cos_q[..., :KV, :], sin_q[..., :KV, :])
        k = k * cos_k + _rotate_half(k) * sin_k
        qg = q.reshape(B, T, KV, G, D)
        scores = jnp.einsum('btkgd,bskd->bkgts', qg, k) * scale
        mask = jnp.tril(jnp.ones((T, T), dtype=scores.dtype))
        scores = scores + mask[None, None, None]
        p = jax.nn.softmax(scores, axis=-1)
        out = jnp.einsum('bkgts,bskd->btkgd', p, v).reshape(B, T, C)
        return out @ wo.T + bo

    def _L0_xattn_ref(hidden_q, kv_c, Wq, w_kc_q, w_kc_kv, W_qr, W_kr, Wo):
        import jax, jax.numpy as jnp
        import numpy as np
        B, S, L = (2, 256, 256)
        DIM_Q, H, K, D_C, D_CQ, R = (512, 16, 128, 128, 384, 64)

        def _rope_tables(seq_len, dim, dtype):
            inv_freq = 1.0 / 10000.0 ** (jnp.arange(0, dim, 2, dtype=dtype) / dim)
            t = jnp.arange(seq_len, dtype=dtype)
            freqs = t[:, None] * inv_freq[None, :]
            sin = jnp.repeat(jnp.sin(freqs), 2, axis=-1)
            cos = jnp.repeat(jnp.cos(freqs), 2, axis=-1)
            return (sin, cos)

        def _rotate_half(x):
            h = x.shape[-1] // 2
            return jnp.concatenate([-x[..., h:], x[..., :h]], axis=-1)
        b, s, _ = hidden_q.shape
        l = kv_c.shape[1]
        q_hk = (hidden_q @ Wq.T).reshape(b, s, H, K)
        q_big = jnp.einsum('bshk,hkq->bshq', q_hk, w_kc_q)
        sin, cos = _rope_tables(l, D_C, kv_c.dtype)
        kv_rope = kv_c * cos[None] + _rotate_half(kv_c) * sin[None]
        q_r = jnp.einsum('bshq,hqr->bhsr', q_big, W_qr)
        k_r = jnp.einsum('bld,hdr->bhlr', kv_rope, W_kr)
        scores = jnp.einsum('bhsr,bhlr->bhsl', q_r, k_r)
        attn = jax.nn.softmax(scores, axis=-1)
        ctx_c = jnp.einsum('bhsl,bld->bhsd', attn, kv_rope)
        ctx_lat = jnp.einsum('bhsd,hkd->bshk', ctx_c, w_kc_kv)
        out = ctx_lat.reshape(b, s, H * K) @ Wo.T
        return out

    def _L0_ffn_ref(x, w1, w2, w3):
        import jax, jax.numpy as jnp
        import numpy as np
        EPS = 1e-08

        def _quantize(w):
            gamma = jnp.mean(jnp.abs(w))
            return jnp.clip(jnp.round(w / (gamma + EPS)), -1.0, 1.0)

        def _bitlinear(x, w):
            return jnp.matmul(x, _quantize(w).T)
        x1 = _bitlinear(x, w1)
        x2 = _bitlinear(x, w2)
        hidden = jax.nn.sigmoid(x1) * x2
        return _bitlinear(hidden, w3)

    def _L1_attn_ref(x, Wqkv, bqkv, Wout, bout, slopes):
        import math
        import jax, jax.numpy as jnp
        import numpy as np
        BLOCK = 64

        def build_slope_tensor(n_heads):

            def p2(n):
                start = 2.0 ** (-2.0 ** (-(math.log2(n) - 3)))
                return [start * start ** i for i in range(n)]
            if math.log2(n_heads).is_integer():
                s = p2(n_heads)
            else:
                closest = 2 ** math.floor(math.log2(n_heads))
                s = p2(closest) + p2(2 * closest)[0::2][:n_heads - closest]
            return jnp.asarray(np.array(s, dtype=np.float32))

        def lightning_attn(q, k, v, slopes, block=BLOCK):
            B, H, N, d = q.shape
            nc = N // block
            i = jnp.arange(block, dtype=q.dtype)
            diff = i[:, None] - i[None, :]
            intra_decay = jnp.where(diff >= 0, jnp.exp(-slopes[:, None, None] * diff), 0.0)
            q_decay = jnp.exp(-slopes[:, None] * i[None, :])
            k_decay = jnp.exp(-slopes[:, None] * (block - i[None, :]))
            blk_decay = jnp.exp(-slopes * block)

            def to_chunks(t):
                return t.reshape(B, H, nc, block, d).transpose(2, 0, 1, 3, 4)
            qc, kc, vc = (to_chunks(q), to_chunks(k), to_chunks(v))

            def body(S, xs):
                qb, kb, vb = xs
                scores = jnp.einsum('bhid,bhjd->bhij', qb, kb) * intra_decay[None]
                o_intra = jnp.einsum('bhij,bhjd->bhid', scores, vb)
                o_inter = jnp.einsum('bhid,bhde->bhie', qb * q_decay[None, :, :, None], S)
                S_new = blk_decay[None, :, None, None] * S + jnp.einsum('bhjd,bhje->bhde', kb * k_decay[None, :, :, None], vb)
                return (S_new, o_intra + o_inter)
            S0 = jnp.zeros((B, H, d, d), dtype=q.dtype)
            _, o = jax.lax.scan(body, S0, (qc, kc, vc))
            return o.transpose(1, 2, 0, 3, 4).reshape(B, H, N, d)
        B, N, C = x.shape
        H = slopes.shape[0]
        hd = C // H
        qkv = (x @ Wqkv + bqkv).reshape(B, N, 3, H, hd)
        qkv = qkv.transpose(2, 0, 3, 1, 4)
        q, k, v = (qkv[0], qkv[1], qkv[2])
        attn = lightning_attn(q, k, v, slopes)
        out = attn.transpose(0, 2, 1, 3).reshape(B, N, C)
        return out @ Wout + bout

    def _L1_xattn_ref(q, latent_kv, Wq, Wkv_expand, Wout):
        import jax, jax.numpy as jnp
        import numpy as np
        B, S, H, NH, L = (2, 512, 512, 16, 128)
        HD = H // NH
        b, sq, _ = q.shape
        sk = latent_kv.shape[1]
        qp = q @ Wq.T
        kv = latent_kv @ Wkv_expand.T
        k, v = jnp.split(kv, 2, axis=-1)
        qh = qp.reshape(b, sq, NH, HD).transpose(0, 2, 1, 3)
        kh = k.reshape(b, sk, NH, HD).transpose(0, 2, 1, 3)
        vh = v.reshape(b, sk, NH, HD).transpose(0, 2, 1, 3)
        inv_sqrt_d = 1.0 / jnp.sqrt(jnp.float32(HD))
        scores = jnp.einsum('bhqd,bhkd->bhqk', qh, kh) * inv_sqrt_d
        causal = jnp.tril(jnp.ones((sq, sk), dtype=bool))
        scores = jnp.where(causal, scores, jnp.finfo(scores.dtype).min)
        attn = jax.nn.softmax(scores, axis=-1)
        out = jnp.einsum('bhqk,bhkd->bhqd', attn, vh)
        out = out.transpose(0, 2, 1, 3).reshape(b, sq, H)
        return out @ Wout.T

    def _L1_ffn_ref(hidden_states, gate_weight, gate_up_weights, down_weights, shared_gate_up, shared_down):
        import jax, jax.numpy as jnp
        import numpy as np
        TOP_K = 2
        B, S, H = hidden_states.shape
        E, twoF, _ = gate_up_weights.shape
        F = twoF // 2
        T = B * S
        x = hidden_states.reshape(T, H)
        logits = x @ gate_weight.T
        scores = jax.nn.softmax(logits, axis=-1)
        topk_w, topk_idx = jax.lax.top_k(scores, TOP_K)
        combine = jnp.zeros((T, E), x.dtype).at[jnp.arange(T)[:, None], topk_idx].add(topk_w)
        gu = jnp.einsum('th,efh->tef', x, gate_up_weights)
        act = jax.nn.silu(gu[..., :F]) * gu[..., F:]
        y = jnp.einsum('tef,te,ehf->th', act, combine, down_weights)
        Fs = shared_gate_up.shape[0] // 2
        sgu = x @ shared_gate_up.T
        sact = jax.nn.silu(sgu[:, :Fs]) * sgu[:, Fs:]
        y = y + sact @ shared_down.T
        return y.reshape(B, S, H)
    x = _layernorm(x + _L0_attn_ref(x, L0_attn_wq, L0_attn_bq, L0_attn_wk, L0_attn_bk, L0_attn_wv, L0_attn_bv, L0_attn_wo, L0_attn_bo), axis=-1)
    x = _layernorm(x + _L0_xattn_ref(x, ctx_512, L0_xattn_Wq, L0_xattn_w_kc_q, L0_xattn_w_kc_kv, L0_xattn_W_qr, L0_xattn_W_kr, L0_xattn_Wo), axis=-1)
    x = _layernorm(x + _L0_ffn_ref(x, L0_ffn_w1, L0_ffn_w2, L0_ffn_w3), axis=-1)
    x = _layernorm(x + _L1_attn_ref(x, L1_attn_Wqkv, L1_attn_bqkv, L1_attn_Wout, L1_attn_bout, L1_attn_slopes), axis=-1)
    x = _layernorm(x + _L1_xattn_ref(x, ctx_512, L1_xattn_Wq, L1_xattn_Wkv_expand, L1_xattn_Wout), axis=-1)
    x = _layernorm(x + _L1_ffn_ref(x, L1_ffn_gate_weight, L1_ffn_gate_up_weights, L1_ffn_down_weights, L1_ffn_shared_gate_up, L1_ffn_shared_down), axis=-1)
    return x

_drawn_inputs = setup_inputs


def setup_inputs(seed=0):
    import zlib

    import numpy as np

    out = dict(_drawn_inputs(seed))
    spreads = {'L1_attn_bqkv': (0.0, 0.1), 'L1_attn_bout': (0.0, 0.8)}
    factors = {'L0_attn_wq': 7.78,
     'L0_attn_bq': 8.0,
     'L0_attn_wk': 7.237,
     'L0_attn_bk': 64.0,
     'L0_attn_bv': 3.073,
     'L1_xattn_Wq': 8.0,
     'L1_ffn_gate_weight': 5.1,
     'L1_ffn_gate_up_weights': 4.457,
     'L1_ffn_down_weights': 4.225,
     'L1_ffn_shared_gate_up': 2.922,
     'L1_ffn_shared_down': 2.928}
    for name, (base, spread) in spreads.items():
        noise = np.random.default_rng([zlib.crc32(name.encode()), seed]).standard_normal(out[name].shape)
        drawn = base * np.exp(spread * noise) if base else spread * noise
        out[name] = jnp.asarray(drawn.astype(out[name].dtype))
    for name, factor in factors.items():
        out[name] = (out[name] * factor).astype(out[name].dtype)
    return out
```

```python
import concourse.bass as bass
from concourse import mybir
from contextlib import ExitStack

F32 = mybir.dt.float32
F32R = mybir.dt.float32r
U32 = mybir.dt.uint32
ALU = mybir.AluOpType
ACT = mybir.ActivationFunctionType
AX = mybir.AxisListType.X

P = 128
B = 16
DM = 512
C = DM // P
GT = 4
G = B // GT
N = GT * P
H = 16
D = DM // H
KV = 4
XH = 16
XR = 64
XQ = 384
F0 = 1408
NF0 = F0 // P
E = 8
F1 = 352
NE = E + 2
FT = [128, 128, 96]
EPS = 1e-5


class Shared:
    pass


class Stats:

    def __init__(self, sb, i):
        self.six, self.mv = sb(f"six{i}", [P, 6]), sb(f"mv{i}", [P, 2])
        self.ve, self.rs, self.spare = sb(f"ve{i}", [P, 1]), sb(f"rs{i}", [P, 1]), sb(f"spare{i}", [P, 2])


class Transposer:

    def __init__(self, S, xth, xtl, sem):
        self.S, self.xth, self.xtl = S, xth, xtl
        self.full, self.hi, self.lo = sem("xt_full"), sem("xt_hi"), sem("xt_lo")

    def on_pe(self, pe):
        S = self.S
        for t in range(B):
            if t >= 2:
                pe.wait_ge(self.lo, t - 1)
            for c in range(C):
                m = pe.transpose(S.bank[t % 2][:, c * P:(c + 1) * P], S.X[:, t, c * P:(c + 1) * P], S.ident[:, :])
            m.then_inc(self.full, 1)

    def on_act(self, act, t):
        act.wait_ge(self.full, t + 1)
        act.activation(self.xth[:, :, t * P:(t + 1) * P], four(self.S.bank[t % 2]), ACT.Copy).then_inc(self.hi, 1)

    def on_dve(self, dve, t):
        dve.wait_ge(self.hi, t + 1)
        cols = slice(t * P, (t + 1) * P)
        dve.tensor_tensor(self.xtl[:, :, cols], four(self.S.bank[t % 2]), f32(self.xth[:, :, cols]),
                          ALU.subtract).then_inc(self.lo, 1)


class Chain:

    def __init__(self, eng, sem):
        self.eng, self.sem, self.base, self.k = eng, sem, 0, 0

    def mark(self, ins):
        ins.then_inc(self.sem, 1)
        self.k += 1
        return self.base + self.k

    def link(self, ins):
        self.eng.wait_ge(self.sem, self.mark(ins))

    def wait(self, value):
        self.eng.wait_ge(self.sem, value)

    def turn(self, start, g, per):
        self.base, self.k = start + g * per, 0


def over_groups(eng, chains, per, body):
    starts = [c.base + c.k for c in chains]
    with eng.Fori(0, G - 1) as g:
        for c, s, p in zip(chains, starts, per):
            c.turn(s, g, p)
        body(g, False)
        for c, p in zip(chains, per):
            assert c.k == p, (c.k, p)
    for c, s, p in zip(chains, starts, per):
        c.turn(s, G - 1, p)
    body(G - 1, True)


def products(pe, out, wh, wl, xh, xl, first, last, **kw):
    pe.matmul(out, wh, xh, start=first, stop=False, **kw)
    pe.matmul(out, wh, xl, start=False, stop=False, **kw)
    return pe.matmul(out, wl, xh, start=False, stop=last, **kw)


class Phase:

    def __init__(self, nc, name):
        self.nc, self.name, self.ctx, self.sems = nc, name, ExitStack(), []

    def __enter__(self):
        return self

    def sb(self, name, shape, dt=F32):
        return self.ctx.enter_context(self.nc.sbuf_tensor(f"{self.name}_{name}", shape, dt))

    def sem(self, name):
        self.sems.append(self.ctx.enter_context(self.nc.semaphore(f"{self.name}_{name}")))
        return self.sems[-1]

    def __exit__(self, *exc):
        if exc[0] is None:
            with self.nc.Block() as block:
                @block.sync
                def _(sp):
                    for s in self.sems:
                        sp.sem_clear(s)
        self.ctx.__exit__(*exc)


def four(bank):
    return bank[:, :].rearrange("p (c n) -> p c n", n=P)


def f32(ap):
    return ap.bitcast(F32)


def norm_stats(dve, ch, row, st, S):
    dve.tensor_copy(st.spare[:, 0:1], S.mhalf[:, :])
    ch.link(dve.bn_stats(out=st.six[:, :], in_=row))
    dve.tensor_copy(st.spare[:, 1:2], S.mhalf[:, :])
    ch.link(dve.bn_aggr(out=st.mv[:, :], in_=st.six[:, :]))
    return dve.tensor_scalar(st.ve[:, :], st.mv[:, 1:2], EPS, None, ALU.add)


def attention_phase(nc, S, kind, w):
    nk = 1 if kind == "gqa" else C
    kc = 1 if kind == "causal" else C
    nv = KV if kind == "gqa" else H
    vw = nv * D
    soft = kind != "decay"
    bias = kind != "causal"
    scale = D ** -0.5
    U = 4 * GT
    OW = D + 1
    with Phase(nc, kind) as phase:
        sb, sem = phase.sb, phase.sem

        ws = sb("ws", [P, 2, C * DM])
        xs = sb("xs", [P, GT, DM])
        xgh, xgl = sb("xgh", [P, C, N], F32R), sb("xgl", [P, C, N], F32R)
        wqh, wql = sb("wqh", [P, C, DM], F32R), sb("wql", [P, C, DM], F32R)
        wkh, wkl = sb("wkh", [P, kc, nk * P], F32R), sb("wkl", [P, kc, nk * P], F32R)
        wvh, wvl = sb("wvh", [P, kc, vw], F32R), sb("wvl", [P, kc, vw], F32R)
        woh, wol = sb("woh", [P, C, DM], F32R), sb("wol", [P, C, DM], F32R)
        qt, kt = sb("qt", [P, C, N]), sb("kt", [P, nk, N])
        v1 = sb("v1", [P, GT, nv, OW])
        pt = sb("pt", [P, 2, 4, P])
        on = sb("on", [P, 2, DM])
        oth, otl = sb("oth", [P, C, P], F32R), sb("otl", [P, C, P], F32R)
        rec = sb("rec", [P, H])
        st = [Stats(sb, i) for i in range(2)]
        if soft:
            pr = sb("pr", [P, 2, 4, P])
            nm, nb = sb("nm", [P, 2, 4]), sb("nb", [P, 2, 4])
        if kind == "causal":
            sm = sb("sm", [P, 2, 4, P])
            cs = sb("cs", [P, GT, P])
            cgh, cgl = sb("cgh", [P, N], F32R), sb("cgl", [P, N], F32R)
        if bias:
            bqk = sb("bqk", [P, 8])
            bvr = sb("bvr", [P, vw])
            bor = sb("bor", [1, DM])
            boh, bol = sb("boh", [1, DM], F32R), sb("bol", [1, DM], F32R)
        if kind == "gqa":
            rope = sb("rope", [P, 2, C * P + P])
            rt = sb("rt", [P, 2, DM])
            bsw, brp = sb("bsw", [P, 8]), sb("brp", [P, 2, 8])
            bt = sb("bt", [P, 8])
            tw, junk = sb("tw", [P, NF0, 3, P]), sb("junk", [P, NF0, P])
        if kind == "decay":
            dec = sb("dec", [P, 4, 4, P])
            slp, nslp = sb("slp", [P, H]), sb("nslp", [P, H])
        pp, sc, tp, ob = S.bank[0:2], S.bank[2:4], S.bank[4:6], S.bank[6:8]

        ws_in = [sem(f"ws_in{i}") for i in range(2)]
        ws_hi, ws_lo, ws_rope = sem("ws_hi"), sem("ws_lo"), sem("ws_rope")
        const_in, ones_set, bias_hi, const_ok = sem("const_in"), sem("ones_set"), sem("bias_hi"), sem("const_ok")
        x_in, xs_in = sem("x_in"), sem("xs_in")
        pp_full, pp_hi, pp_free = sem("pp_full"), sem("pp_hi"), sem("pp_free")
        sc_full, max_done, exp_done = sem("sc_full"), sem("max_done"), sem("exp_done")
        pt_full, pt_done, pv_done = sem("pt_full"), sem("pt_done"), sem("pv_done")
        o_norm = sem("o_norm")
        ve_done, rs_done = sem("ve_done"), sem("rs_done")
        dve_chain, act_chain = sem("dve_chain"), sem("act_chain")
        bias_lo = sem("bias_lo")
        tw_in, tw_summed = sem("tw_in"), sem("tw_summed")

        pieces = [(w["q"], wqh, wql), (w["k"], wkh, wkl), (w["v"], wvh, wvl), (w["o"], woh, wol)]
        flat = lambda t: t[:, :, :].rearrange("p c n -> p (c n)")

        head = [("x", i) for i in range(GT)] + ([("c", 0)] if kind == "causal" else [])
        proj = [("q", j) for j in range(C)] + [("k", j) for j in range(nk)] + [("v", i) for i in range(GT)]
        STEPS = U + 8
        own = {i: [] for i in range(STEPS)}
        nxt = {i: [] for i in range(STEPS)}
        for b in range(GT):
            own[4 * b + 8].append(("ot", b))
            own[4 * b + 10].append(("out", b))
        for n, e in enumerate(head):
            nxt[1 + 2 * n].append(e)
        for n, e in enumerate(proj):
            nxt[19 + e[1] // 2 if e[0] == "v" else 16 + n // 3].append(e)
        LAG = 3 if soft else 1

        def stages(last):
            out, k = [], 0
            for i in range(STEPS):
                for e in ([] if last else nxt[i]) + own[i]:
                    out.append((i, e, k))
                    k += 1
            return out

        def at_step(i, last):
            return [(e, k) for j, e, k in stages(last) if j == i]

        PRO = len(head) + len(proj)
        PER = PRO + 2 * GT
        HI = ("x", "c", "ot")
        PRO_HI, PER_HI = len(head), len(head) + GT
        LAST_X = max(k for _, e, k in stages(False) if e in head)

        def his_before(k, last):
            return sum(e[0] in HI for _, e, n in stages(last) if n < k)

        def heads_of(u):
            r = u % 4
            for j in range(4):
                yield j, j, (0 if kind == "gqa" else j), slice(D * r, D * r + D), \
                    (4 * r + j if kind == "gqa" else 4 * j + r), (r if kind == "gqa" else 4 * j + r)

        loads_n = 3 * bias + 3 * (kind == "gqa") + (kind == "decay")
        if kind == "causal":
            cgh_v = cgh[:, :].rearrange("p (c n) -> p c n", n=P)
            cgl_v = cgl[:, :].rearrange("p (c n) -> p c n", n=P)
        else:
            cgh_v = cgl_v = None

        blocks = ExitStack()
        block = blocks.enter_context(nc.Block())

        @block.sync
        def _(sp):
            x_src = S.x_dram if kind == "gqa" else S.X

            def stage(g):
                sp.dma_start(xs[:, :, :], x_src[:, bass.ds(g * GT, GT), :]).then_inc(xs_in, 16)
                if kind == "causal":
                    sp.dma_start(cs[:, :, :], S.ctx_dram[:, bass.ds(g * GT, GT), :]).then_inc(xs_in, 16)

            stage(0)
            for p, (src, hi, lo) in enumerate(pieces):
                if p >= 2:
                    sp.wait_ge(ws_lo, p - 1)
                n = src.shape[1] * src.shape[2]
                sp.dma_start(ws[:, p % 2, 0:n], src.rearrange("p c n -> p (c n)")).then_inc(ws_in[p % 2], 16)
            sp.wait_ge(pp_full, len(head))
            stage(1)
            if kind == "gqa":
                sp.dma_start(S.X[:, :, :], S.x_dram).then_inc(x_in, 16)
            with sp.Fori(2, G) as g:
                sp.wait_ge(pp_full, g * PER + (PRO - 2 * PER + LAST_X + 1))
                stage(g)

        @block.gpsimd
        def _(pool):
            pool.memset(v1[:, :, :, :], 1.0).then_inc(const_ok, 1)
            with pool.Fori(0, B // 2) as n:
                for i in range(2):
                    pool.wait_ge(ve_done, n * 2 + (i + 1))
                    pool.tensor_tensor(out=st[i].rs[:, :], in0=st[i].ve[:, :], in1=S.mhalf[:, :],
                                       op=ALU.pow).then_inc(rs_done, 1)

        @block.scalar
        def _(act):
            ac = Chain(act, act_chain)
            loads = []
            if bias:
                loads += [(bqk[:, :], w["bqk"]), (bvr[:, :], w["bv"]), (bor[:, :], w["bo"])]
            if kind == "gqa":
                loads += [(rope[:, :, :], S.rope_rows), (bsw[:, :], w["bqk_swapped"]), (brp[:, :, :], S.rope_cols)]
            if kind == "decay":
                loads += [(slp[:, :], w["slopes"])]
            for dst, src in loads:
                act.dma_start(dst, src).then_inc(const_in, 16)
            for p, (src, hi, lo) in enumerate(pieces):
                n = src.shape[1] * src.shape[2]
                if kind == "gqa" and p < 2:
                    act.wait_ge(ws_rope, p + 1)
                else:
                    act.wait_ge(ws_in[p % 2], 16 * (p // 2 + 1))
                act.activation(flat(hi), ws[:, p % 2, 0:n], ACT.Copy).then_inc(ws_hi, 1)
                if p == 0 and loads:
                    act.wait_ge(const_in, 16 * len(loads))
                    if bias:
                        act.activation(boh[:, :], bor[:, :], ACT.Copy).then_inc(bias_hi, 1)
                    if kind == "decay":
                        ac.link(act.activation(nslp[:, :], slp[:, :], ACT.Copy, scale=-1.0))
                        for r in range(4):
                            for j in range(4):
                                a = act.activation(dec[:, r, j, :], S.dist[:, :], ACT.Exp,
                                                   scale=nslp[:, 4 * j + r:4 * j + r + 1])
                        a.then_inc(bias_hi, 1)

            def hi_part(e, bank, k):
                what, i = e
                if what not in HI:
                    return
                act.wait_ge(pp_full, k + 1)
                dst = {"x": xgh[:, :, i * P:(i + 1) * P], "c": cgh_v, "ot": oth[:, :, :]}[what]
                act.activation(dst, four(bank), ACT.Copy).then_inc(pp_hi, 1)

            def ternary_quarter(g):
                act.dma_start(tw[:, :, :, :], S.ternary[:, :, :, bass.ds(g * P, P)]).then_inc(tw_in, 16)

            def magnitudes(g, m):
                if m == 0:
                    act.wait_ge(tw_in, g * 16 + 16)
                act.wait_ge(tw_summed, g * 3 + m) if m or not isinstance(g, int) else None
                act.activation(junk[:, :, :], tw[:, :, m, :], ACT.Abs,
                               accum_out=S.tern_part[:, bass.ds(g * 3 + m, 1)]).then_inc(tw_summed, 1)

            for k, e in enumerate(head + proj):
                hi_part(e, pp[k % 2], k)
            if kind == "gqa":
                ternary_quarter(0)

            def body(g, last):
                for i in range(STEPS):
                    if kind == "gqa" and i in (6, 10, 14):
                        magnitudes(g, (i - 6) // 4)
                    if kind == "gqa" and i == 18 and not last:
                        act.wait_ge(tw_summed, g * 3 + 3)
                        ternary_quarter(g + 1)
                    if soft and i < U:
                        act.wait_ge(max_done, g * U + (i + 1))
                        if i >= 2:
                            act.wait_ge(pt_full, g * U + (i - 1))
                        for j in range(4):
                            src = sm[:, i % 2, j, :] if kind == "causal" else sc[i % 2][:, j * P:(j + 1) * P]
                            a = act.activation(pr[:, i % 2, j, :], src, ACT.Exp,
                                               bias=nb[:, i % 2, j:j + 1], scale=scale)
                        a.then_inc(exp_done, 1)
                    for e, k in at_step(i, last):
                        hi_part(e, pp[k % 2], g * PER + (PRO + k))

            over_groups(act, [], [], body)

        @block.vector
        def _(dve):
            ch = Chain(dve, dve_chain)
            if loads_n:
                dve.wait_ge(const_in, 16 * loads_n)
            if kind == "gqa":
                for p in range(2):
                    dve.wait_ge(ws_in[p], 16)
                    n = DM if p == 0 else P
                    t0 = 0 if p == 0 else DM
                    for c in range(C):
                        row = ws[:, p, c * n:(c + 1) * n]
                        dst = rt[:, 1, 0:n]
                        w2 = row.rearrange("p (h s e) -> p h s e", s=2, e=D // 2)
                        sn = rope[:, 1, t0:t0 + n].rearrange("p (h s e) -> p h s e", s=2, e=D // 2)
                        d2 = dst.rearrange("p (h s e) -> p h s e", s=2, e=D // 2)
                        for s in range(2):
                            a = dve.tensor_tensor(d2[:, :, s, :], w2[:, :, 1 - s, :], sn[:, :, s, :], ALU.mult)
                        ch.link(a)
                        ch.link(dve.tensor_tensor(rt[:, 0, 0:n], row, rope[:, 0, t0:t0 + n], ALU.mult))
                        a = dve.tensor_tensor(row, rt[:, 0, 0:n], rt[:, 1, 0:n], ALU.add)
                        if c < C - 1:
                            ch.link(a)
                    a.then_inc(ws_rope, 1)
                    dve.wait_ge(ws_rope, p + 1)
                ch.link(dve.tensor_tensor(bt[:, :], bqk[:, :], brp[:, 0, :], ALU.mult))
                ch.link(dve.tensor_tensor(bsw[:, :], bsw[:, :], brp[:, 1, :], ALU.mult))
                ch.link(dve.tensor_tensor(bqk[:, :], bsw[:, :], bt[:, :], ALU.add))
            for p, (src, hi, lo) in enumerate(pieces):
                n = src.shape[1] * src.shape[2]
                dve.wait_ge(ws_hi, p + 1)
                dve.wait_ge(ws_in[p % 2], 16 * (p // 2 + 1))
                dve.tensor_tensor(flat(lo), ws[:, p % 2, 0:n], f32(flat(hi)), ALU.subtract).then_inc(ws_lo, 1)
            if bias:
                dve.wait_ge(bias_hi, 1)
                dve.tensor_tensor(bol[:, :], bor[:, :], f32(boh[:, :]), ALU.subtract).then_inc(bias_lo, 1)
            if kind == "decay":
                dve.wait_ge(bias_hi, 2)
                for r in range(4):
                    a = dve.tensor_tensor(dec[:, r, :, :], dec[:, r, :, :], S.upper4, ALU.mult)
                ch.link(a)
            dve.wait_ge(const_ok, 1)

            def lo_part(e, bank, k, hi_k, g):
                what, i = e
                dve.wait_ge(pp_full, k + 1)
                if what in HI:
                    dve.wait_ge(pp_hi, hi_k + 1)
                    hi = {"x": xgh[:, :, i * P:(i + 1) * P], "c": cgh_v, "ot": oth[:, :, :]}[what]
                    lo = {"x": xgl[:, :, i * P:(i + 1) * P], "c": cgl_v, "ot": otl[:, :, :]}[what]
                    a = dve.tensor_tensor(lo, four(bank), f32(hi), ALU.subtract)
                elif what in "qk":
                    dst = (qt if what == "q" else kt)[:, i, :]
                    if bias:
                        col = i if what == "q" else 4 + i
                        a = dve.tensor_scalar(dst, bank[:, :], bqk[:, col:col + 1], None, ALU.add)
                    else:
                        a = dve.tensor_copy(dst, bank[:, :])
                elif what == "v":
                    dst = v1[:, i, :, 0:D]
                    src = bank[:, 0:vw].rearrange("p (h d) -> p h d", d=D)
                    if bias:
                        a = dve.tensor_tensor(dst, src, bvr[:, :].rearrange("p (h d) -> p h d", d=D), ALU.add)
                    else:
                        a = dve.tensor_copy(dst, src)
                else:
                    if kind == "gqa" and i == 0 and not dve_state["x"]:
                        dve.wait_ge(x_in, 16)
                    row = S.X[:, g * GT + i, :]
                    a = dve.tensor_tensor(row, row, bank[:, :], ALU.add)
                a.then_inc(pp_free, 1)
                if what == "out":
                    s = st[i % 2]
                    dve.wait_ge(pp_free, k + 1)
                    norm_stats(dve, ch, S.X[:, g * GT + i, :], s, S).then_inc(ve_done, 1)

            dve_state = {"x": False}
            n_hi = 0
            for k, e in enumerate(head + proj):
                lo_part(e, pp[k % 2], k, n_hi, 0)
                n_hi += e[0] in HI

            def normalize(b, g):
                s = st[b % 2]
                row = S.X[:, g * GT + b, :]
                dve.wait_ge(rs_done, g * GT + (b + 1))
                dve.tensor_scalar(row, row, s.mv[:, 0:1], s.rs[:, 0:1], ALU.subtract, ALU.mult)

            def body(g, last):
                for i in range(STEPS):
                    if i < U:
                        dve.wait_ge(sc_full, g * U + (i + 1))
                        if soft:
                            if i >= 2:
                                dve.wait_ge(exp_done, g * U + (i - 1))
                            src = four(sc[i % 2])
                            if kind == "causal":
                                ch.link(dve.tensor_tensor(sm[:, i % 2, :, :], src, S.causal4, ALU.add))
                                src = sm[:, i % 2, :, :]
                            ch.link(dve.tensor_reduce(nm[:, i % 2, :], src, AX, ALU.max))
                            dve.tensor_scalar(nb[:, i % 2, :], nm[:, i % 2, :], -scale, None,
                                              ALU.mult).then_inc(max_done, 1)
                        else:
                            if i >= 2:
                                dve.wait_ge(pv_done, g * U + (i - 1))
                            dve.tensor_tensor(pt[:, i % 2, :, :], four(sc[i % 2]), dec[:, i % 4, :, :],
                                              ALU.mult).then_inc(pt_done, 1)
                    if soft and 0 <= i - 2 < U:
                        u = i - 2
                        dve.wait_ge(pt_full, g * U + (u + 1))
                        if u >= 2:
                            dve.wait_ge(pv_done, g * U + (u - 1))
                        if kind == "gqa":
                            a = dve.tensor_tensor(pt[:, u % 2, :, :], four(tp[u % 2]), S.lower4, ALU.mult)
                        else:
                            a = dve.tensor_copy(pt[:, u % 2, :, :], four(tp[u % 2]))
                        a.then_inc(pt_done, 1)
                    u = i - LAG
                    if 0 <= u < U and u % 4 == 3:
                        b = u // 4
                        dve.wait_ge(pv_done, g * U + (u + 1))
                        if soft:
                            for q in range(2):
                                o = ob[q][:, 0:8 * OW].rearrange("p (h e) -> p h e", e=OW)
                                a = dve.reciprocal(rec[:, 8 * q:8 * q + 8], o[:, :, D])
                            ch.link(a)
                        for q in range(2):
                            dst = on[:, b % 2, 8 * D * q:8 * D * (q + 1)].rearrange("p (h d) -> p h d", d=D)
                            o = ob[q][:, 0:8 * OW].rearrange("p (h e) -> p h e", e=OW)[:, :, 0:D]
                            if soft:
                                r8 = rec[:, 8 * q:8 * q + 8].unsqueeze(2).broadcast_to((P, 8, D))
                                a = dve.tensor_tensor(dst, o, r8, ALU.mult)
                            else:
                                a = dve.tensor_copy(dst, o)
                        a.then_inc(o_norm, 1)
                    for e, k in at_step(i, last):
                        if e[0] == "out" and e[1] > 0:
                            normalize(e[1] - 1, g)
                        lo_part(e, pp[k % 2], g * PER + (PRO + k), g * PER_HI + (PRO_HI + his_before(k, last)), g)
                normalize(GT - 1, g)

            per = GT * 2 + (U * (2 if kind == "causal" else 1) + GT if soft else 0)
            if kind == "gqa":
                dve.wait_ge(x_in, 16)
            over_groups(dve, [ch], [per], body)

        @block.tensor
        def _(pe):
            def pp_stage(e, bank, k, heads_free, g):
                what, i = e
                if what == "x":
                    pe.wait_ge(xs_in, (g + 1) * (32 if kind == "causal" else 16))
                    for c in range(C):
                        m = pe.transpose(bank[:, c * P:(c + 1) * P], xs[:, i, c * P:(c + 1) * P], S.ident[:, :])
                elif what == "c":
                    for t in range(GT):
                        m = pe.transpose(bank[:, t * P:(t + 1) * P], cs[:, t, :], S.ident[:, :])
                elif what in "qk":
                    if i == 0:
                        pe.wait_ge(pp_free, heads_free)
                        if isinstance(g, int) and g == 0:
                            pe.wait_ge(ws_lo, 1 if what == "q" else 2)
                    wh, wl = (wqh, wql) if what == "q" else (wkh, wkl)
                    src = [(cgh[:, :], cgl[:, :])] if what == "k" and kind == "causal" else \
                        [(xgh[:, c, :], xgl[:, c, :]) for c in range(C)]
                    cols = slice(i * P, (i + 1) * P)
                    for c, (xh, xl) in enumerate(src):
                        m = products(pe, bank[:, :], wh[:, c, cols], wl[:, c, cols], xh, xl,
                                     c == 0, c == len(src) - 1)
                elif what == "v":
                    if i == 0 and isinstance(g, int) and g == 0:
                        pe.wait_ge(ws_lo, 3)
                    cols = slice(i * P, (i + 1) * P)
                    src = [(cgh[:, cols], cgl[:, cols])] if kind == "causal" else \
                        [(xgh[:, c, cols], xgl[:, c, cols]) for c in range(C)]
                    for c, (xh, xl) in enumerate(src):
                        m = products(pe, bank[:, 0:vw], xh, xl, wvh[:, c, :], wvl[:, c, :],
                                     c == 0, c == len(src) - 1)
                elif what == "ot":
                    pe.wait_ge(o_norm, g * GT + (i + 1))
                    for c in range(C):
                        m = pe.transpose(bank[:, c * P:(c + 1) * P], on[:, i % 2, c * P:(c + 1) * P], S.ident[:, :])
                else:
                    pe.wait_ge(pp_free, heads_free)
                    for c in range(C):
                        m = products(pe, bank[:, :], oth[:, c, :], otl[:, c, :], woh[:, c, :], wol[:, c, :],
                                     c == 0, c == C - 1 and not bias)
                    if bias:
                        pe.matmul(bank[:, :], S.ones[:, :], boh[:, :], start=False, stop=False)
                        m = pe.matmul(bank[:, :], S.ones[:, :], bol[:, :], start=False, stop=True)
                m.then_inc(pp_full, 1)

            for k, e in enumerate(head + proj):
                if k >= 2:
                    pe.wait_ge(pp_free, k - 1)
                pp_stage(e, pp[k % 2], k, len(head), 0)
            pe.wait_ge(ws_lo, 4)
            if bias:
                pe.wait_ge(bias_lo, 1)

            def body(g, last):
                base = g * PER + PRO
                x_free = g * PER + (PRO + LAST_X + 1)
                uses = {e: k for _, e, k in stages(last)}
                for i in range(STEPS):
                    if i < U:
                        if i == 0:
                            pe.wait_ge(pp_free, base)
                        else:
                            pass
                        if i >= 2:
                            pe.wait_ge({"gqa": exp_done, "causal": max_done, "decay": pt_done}[kind], g * U + (i - 1))
                        tok = slice((i // 4) * P, (i // 4 + 1) * P)
                        for j, jq, jk, rows, h, hv in heads_of(i):
                            q, k = qt[rows, jq, tok], kt[rows, jk, tok]
                            a, b = (q, k) if soft else (k, q)
                            m = pe.matmul(sc[i % 2][:, j * P:(j + 1) * P], a, b, start=True, stop=True)
                        m.then_inc(sc_full, 1)
                    u = i - 2
                    if soft and 0 <= u < U:
                        pe.wait_ge(exp_done, g * U + (u + 1))
                        if u >= 2:
                            pe.wait_ge(pt_done, g * U + (u - 1))
                        for j in range(4):
                            m = pe.transpose(tp[u % 2][:, j * P:(j + 1) * P], pr[:, u % 2, j, :], S.ident[:, :])
                        m.then_inc(pt_full, 1)
                    u = i - LAG
                    if 0 <= u < U:
                        pe.wait_ge(pt_done, g * U + (u + 1))
                        if u % 4 == 0 and u:
                            pe.wait_ge(o_norm, g * GT + u // 4)
                        for j, _, _, _, h, hv in heads_of(u):
                            n = OW if soft else D
                            m = pe.matmul(ob[h // 8][:, (h % 8) * OW:(h % 8) * OW + n], pt[:, u % 2, j, :],
                                          v1[:, u // 4, hv, 0:n], start=True, stop=True)
                        m.then_inc(pv_done, 1)
                    for e, k in at_step(i, last):
                        pe.wait_ge(pp_free, base + max(k - 1, 0))
                        nx = e in head or e in proj
                        need = x_free if nx else base + (uses[("ot", e[1])] + 1)
                        pp_stage(e, pp[k % 2], base + k, need, g + 1 if nx else g)

            over_groups(pe, [], [], body)

        blocks.close()


def latent_phase(nc, S, w, half):
    HH = XH // 2
    T = HH // 2
    U = 2 * GT
    CB = DM + 3 * P + 3 * XR + P + DM
    name = f"latent{half}"
    with Phase(nc, name) as phase:
        sb, sem = phase.sb, phase.sem

        fold = sb("fold", [P, 2, CB])
        fm = sb("fm", [P, 2, XR])
        ch_, cl_ = sb("ch", [P, C, HH * XR], F32R), sb("cl", [P, C, HH * XR], F32R)
        vh, vl = sb("vh", [P, HH, DM], F32R), sb("vl", [P, HH, DM], F32R)
        kr = sb("kr", [P, HH * XR])
        krh, krl = sb("krh", [P, HH * XR], F32R), sb("krl", [P, HH * XR], F32R)
        kv = sb("kv", [P, B, P])
        kvr = sb("kvr", [P, 2, P])
        kvh, kvl = sb("kvh", [P, B * P], F32R), sb("kvl", [P, B * P], F32R)
        kvs = sb("kvs", [P, GT, P])
        xs = sb("xs", [P, GT, DM])
        xgh, xgl = sb("xgh", [P, C, N], F32R), sb("xgl", [P, C, N], F32R)
        qt, kt = sb("qt", [P, T, N]), sb("kt", [P, T, N])
        pr, pt = sb("pr", [P, 2, 4, P]), sb("pt", [P, 2, 4, P])
        nm, nb = sb("nm", [P, 2, 4]), sb("nb", [P, 2, 4])
        sums, rec = sb("sums", [P, 2, 4]), sb("rec", [P, 2, 4])
        cth, ctl = sb("cth", [P, 2, 2, N], F32R), sb("ctl", [P, 2, 2, N], F32R)
        st = [Stats(sb, i) for i in range(2)]
        t1 = fold[:, :, 0:8 * P].rearrange("p a (b n) -> p a b n", n=P)
        t2 = xs[:, :, :].rearrange("p (a q) (b n) -> p a (q b) n", a=2, n=P)
        kv4 = kv[:, :, :].rearrange("p (a b) n -> p a b n", a=2)
        pp, sc, tp, cb = S.bank[0:2], S.bank[2:4], S.bank[4:6], S.bank[6:8]

        x_src = S.X[:, :, :] if half == 0 else S.x_kept
        x_kept, kv_in, kr_in, kv_rot = sem("x_kept"), sem("kv_in"), sem("kr_in"), sem("kv_rot")
        kvt_full, kvt_hi, kvt_lo = sem("kvt_full"), sem("kvt_hi"), sem("kvt_lo")
        kr_hi, kr_lo = sem("kr_hi"), sem("kr_lo")
        fold_in = [sem(f"fold_in{i}") for i in range(2)]
        fm_full, fm_done = sem("fm_full"), sem("fm_done")
        c_full, c_hi, c_lo = sem("c_full"), sem("c_hi"), sem("c_lo")
        v_full, v_hi, v_lo = sem("v_full"), sem("v_hi"), sem("v_lo")
        xs_in, kvs_in = sem("xs_in"), sem("kvs_in")
        pp_full, pp_hi, pp_free = sem("pp_full"), sem("pp_hi"), sem("pp_free")
        sc_full, max_done, exp_done, p_norm = sem("sc_full"), sem("max_done"), sem("exp_done"), sem("p_norm")
        pt_full, pt_done = sem("pt_full"), sem("pt_done")
        ct_full, ct_hi, ct_lo = sem("ct_full"), sem("ct_hi"), sem("ct_lo")
        ve_done, rs_done, dve_chain = sem("ve_done"), sem("rs_done"), sem("dve_chain")

        def folded(s):
            r, at = fold[:, s, :], 0
            out = []
            for n in (DM, 3 * P, 3 * XR, P, DM):
                out.append(r[:, at:at + n])
                at += n
            return out

        head = [("x", i) for i in range(GT)]
        proj = [(q, j) for j in range(T) for q in "qk"]
        STEPS = U + 6
        own = {i: [] for i in range(STEPS)}
        nxt = {i: [] for i in range(STEPS)}
        for b in range(GT):
            own[2 * b + 6].append(("out", b))
        for n, e in enumerate(head):
            nxt[1 + n].append(e)
        for n, e in enumerate(proj):
            nxt[8 + n // 2].append(e)

        def stages(last):
            out, k = [], 0
            for i in range(STEPS):
                for e in ([] if last else nxt[i]) + own[i]:
                    out.append((i, e, k))
                    k += 1
            return out

        def at_step(i, last):
            return [(e, k) for j, e, k in stages(last) if j == i]

        PRO = len(head) + len(proj)
        PER = PRO + GT
        LAST_X = max(k for _, e, k in stages(False) if e in head)

        def his_before(k, last):
            return sum(e[0] == "x" for _, e, n in stages(last) if n < k)

        blocks = ExitStack()
        block = blocks.enter_context(nc.Block())

        @block.sync
        def _(sp):
            sp.dma_start(kv[:, :, :], S.ctx_dram).then_inc(kv_in, 16)
            sp.dma_start(kvr[:, :, :], S.kv_rope).then_inc(kv_in, 16)
            sp.dma_start(kr[:, :], w["kr"][:, half * HH * XR:(half + 1) * HH * XR]).then_inc(kr_in, 16)
            sp.wait_ge(kv_rot, 1)
            sp.dma_start(xs[:, :, :], x_src[:, 0:GT, :]).then_inc(xs_in, 16)
            sp.dma_start(kvs[:, :, :], kv[:, 0:GT, :]).then_inc(kvs_in, 16)
            for s in range(2):
                sp.dma_start(fold[:, s, :], w["fold"][half * HH + s]).then_inc(fold_in[s], 16)
            with sp.Fori(1, HH // 2) as n:
                for s in range(2):
                    sp.wait_ge(v_full, n * 2 + (s - 1))
                    src = w["fold"][bass.ds(n * 2 + (half * HH + s), 1)].rearrange("a p n -> (a p) n")
                    sp.dma_start(fold[:, s, :], src).then_inc(fold_in[s], 16)
            if half == 0:
                sp.dma_start(S.x_kept, S.X[:, :, :]).then_inc(x_kept, 16)
            sp.wait_ge(pp_full, len(head))
            sp.dma_start(xs[:, :, :], x_src[:, GT:2 * GT, :]).then_inc(xs_in, 16)

            def latents(g):
                sp.wait_ge(ct_full, g * U)
                sp.dma_start(kvs[:, :, :], kv[:, bass.ds(g * GT, GT), :]).then_inc(kvs_in, 16)

            with sp.Fori(0, G - 2) as g:
                sp.wait_ge(pp_full, g * PER + (PRO + LAST_X + 1))
                sp.dma_start(xs[:, :, :], x_src[:, bass.ds((g + 2) * GT, GT), :]).then_inc(xs_in, 16)
                latents(g + 1)
            latents(G - 1)

        @block.gpsimd
        def _(pool):
            if half == 1:
                with pool.Fori(0, B // 2) as n:
                    for i in range(2):
                        pool.wait_ge(ve_done, n * 2 + (i + 1))
                        pool.tensor_tensor(out=st[i].rs[:, :], in0=st[i].ve[:, :], in1=S.mhalf[:, :],
                                           op=ALU.pow).then_inc(rs_done, 1)

        @block.scalar
        def _(act):
            act.wait_ge(kr_in, 16)
            act.activation(krh[:, :], kr[:, :], ACT.Copy).then_inc(kr_hi, 1)
            for q in range(G):
                act.wait_ge(kvt_full, q + 1)
                act.activation(kvh[:, q * N:(q + 1) * N], pp[q % 2][:, :], ACT.Copy).then_inc(kvt_hi, 1)
            with act.Fori(0, HH // 2) as n:
                for s in range(2):
                    act.wait_ge(fm_full, n * 2 + (s + 1))
                    act.activation(fm[:, s, :], sc[s][:, 0:XR], ACT.Copy).then_inc(fm_done, 1)
                    act.wait_ge(v_full, n * 2 + (s + 1))
                    act.activation(vh[:, bass.ds(n * 2 + s, 1), :], cb[s][:, :].unsqueeze(1),
                                   ACT.Copy).then_inc(v_hi, 1)
                    act.wait_ge(c_full, n * 2 + (s + 1))
                    act.activation(ch_[:, :, bass.ds(n * (2 * XR) + s * XR, XR)],
                                   tp[s][:, 0:C * XR].rearrange("p (c r) -> p c r", r=XR), ACT.Copy).then_inc(c_hi, 1)

            def hi_part(e, bank, k):
                if e[0] == "x":
                    act.wait_ge(pp_full, k + 1)
                    act.activation(xgh[:, :, e[1] * P:(e[1] + 1) * P], four(bank), ACT.Copy).then_inc(pp_hi, 1)

            for k, e in enumerate(head + proj):
                hi_part(e, pp[k % 2], k)

            def body(g, last):
                for i in range(STEPS):
                    if i < U:
                        act.wait_ge(max_done, g * U + (i + 1))
                        if i >= 2:
                            act.wait_ge(pt_full, g * U + (i - 1))
                        for j in range(4):
                            a = act.activation(pr[:, i % 2, j, :], sc[i % 2][:, j * P:(j + 1) * P], ACT.Exp,
                                               bias=nb[:, i % 2, j:j + 1], accum_out=sums[:, i % 2, j:j + 1])
                        a.then_inc(exp_done, 1)
                    u = i - 3
                    if 0 <= u < U:
                        act.wait_ge(ct_full, g * U + (u + 1))
                        act.activation(cth[:, u // 2 % 2, u % 2, :], cb[u % 2][:, :], ACT.Copy).then_inc(ct_hi, 1)
                    for e, k in at_step(i, last):
                        hi_part(e, pp[k % 2], g * PER + (PRO + k))

            over_groups(act, [], [], body)

        @block.vector
        def _(dve):
            ch = Chain(dve, dve_chain)
            dve.wait_ge(kv_in, 32)
            half_of = lambda t, s: t[:, :, :, s * (P // 2):(s + 1) * (P // 2)]
            for s in range(2):
                sn = kvr[:, 1, s * (P // 2):(s + 1) * (P // 2)].unsqueeze(1).unsqueeze(1)
                a = dve.tensor_tensor(half_of(t1, s), half_of(kv4, 1 - s), sn.broadcast_to((P, 2, 8, P // 2)), ALU.mult)
            ch.link(a)
            cs = kvr[:, 0, :].unsqueeze(1).unsqueeze(1).broadcast_to((P, 2, 8, P))
            ch.link(dve.tensor_tensor(t2, kv4, cs, ALU.mult))
            dve.tensor_tensor(kv4, t1, t2, ALU.add).then_inc(kv_rot, 1)
            dve.wait_ge(kr_hi, 1)
            dve.tensor_tensor(krl[:, :], kr[:, :], f32(krh[:, :]), ALU.subtract).then_inc(kr_lo, 1)
            for q in range(G):
                dve.wait_ge(kvt_hi, q + 1)
                cols = slice(q * N, (q + 1) * N)
                dve.tensor_tensor(kvl[:, cols], pp[q % 2][:, :], f32(kvh[:, cols]), ALU.subtract).then_inc(kvt_lo, 1)
            with dve.Fori(0, HH // 2) as n:
                for s in range(2):
                    dve.wait_ge(v_hi, n * 2 + (s + 1))
                    dve.tensor_tensor(vl[:, bass.ds(n * 2 + s, 1), :], cb[s][:, :].unsqueeze(1),
                                      f32(vh[:, bass.ds(n * 2 + s, 1), :]), ALU.subtract).then_inc(v_lo, 1)
                    dve.wait_ge(c_hi, n * 2 + (s + 1))
                    cols = bass.ds(n * (2 * XR) + s * XR, XR)
                    dve.tensor_tensor(cl_[:, :, cols], tp[s][:, 0:C * XR].rearrange("p (c r) -> p c r", r=XR),
                                      f32(ch_[:, :, cols]), ALU.subtract).then_inc(c_lo, 1)

            def lo_part(e, bank, k, hi_k, g):
                what, i = e
                dve.wait_ge(pp_full, k + 1)
                if what == "x":
                    dve.wait_ge(pp_hi, hi_k + 1)
                    cols = slice(i * P, (i + 1) * P)
                    a = dve.tensor_tensor(xgl[:, :, cols], four(bank), f32(xgh[:, :, cols]), ALU.subtract)
                elif what in "qk":
                    a = dve.tensor_copy((qt if what == "q" else kt)[:, i, :], bank[:, :])
                else:
                    row = S.X[:, g * GT + i, :]
                    a = dve.tensor_tensor(row, row, bank[:, :], ALU.add)
                a.then_inc(pp_free, 1)
                if what == "out" and half == 1:
                    dve.wait_ge(pp_free, k + 1)
                    norm_stats(dve, ch, S.X[:, g * GT + i, :], st[i % 2], S).then_inc(ve_done, 1)

            n_hi = 0
            for k, e in enumerate(head + proj):
                lo_part(e, pp[k % 2], k, n_hi, 0)
                n_hi += e[0] == "x"

            def normalize(b, g):
                s = st[b % 2]
                row = S.X[:, g * GT + b, :]
                dve.wait_ge(rs_done, g * GT + (b + 1))
                dve.tensor_scalar(row, row, s.mv[:, 0:1], s.rs[:, 0:1], ALU.subtract, ALU.mult)

            def body(g, last):
                for i in range(STEPS):
                    if i < U:
                        dve.wait_ge(sc_full, g * U + (i + 1))
                        ch.link(dve.tensor_reduce(nm[:, i % 2, :], four(sc[i % 2]), AX, ALU.max))
                        dve.tensor_scalar(nb[:, i % 2, :], nm[:, i % 2, :], -1.0, None, ALU.mult).then_inc(max_done, 1)
                    u = i - 1
                    if 0 <= u < U:
                        dve.wait_ge(exp_done, g * U + (u + 1))
                        ch.link(dve.reciprocal(rec[:, u % 2, :], sums[:, u % 2, :]))
                        for j in range(4):
                            row = pr[:, u % 2, j, :]
                            a = dve.tensor_scalar(row, row, rec[:, u % 2, j:j + 1], None, ALU.mult)
                        a.then_inc(p_norm, 1)
                    u = i - 2
                    if 0 <= u < U:
                        dve.wait_ge(pt_full, g * U + (u + 1))
                        if u >= 2:
                            dve.wait_ge(ct_full, g * U + (u - 1))
                        dve.tensor_copy(pt[:, u % 2, :, :], four(tp[u % 2])).then_inc(pt_done, 1)
                    u = i - 3
                    if 0 <= u < U:
                        dve.wait_ge(ct_hi, g * U + (u + 1))
                        dve.tensor_tensor(ctl[:, u // 2 % 2, u % 2, :], cb[u % 2][:, :],
                                          f32(cth[:, u // 2 % 2, u % 2, :]), ALU.subtract).then_inc(ct_lo, 1)
                    for e, k in at_step(i, last):
                        if e[0] == "out" and e[1] > 0 and half == 1:
                            normalize(e[1] - 1, g)
                        lo_part(e, pp[k % 2], g * PER + (PRO + k), g * len(head) + (len(head) + his_before(k, last)), g)
                if half == 1:
                    normalize(GT - 1, g)

            if half == 0:
                dve.wait_ge(x_kept, 16)
            over_groups(dve, [ch], [2 * U + 2 * GT * half], body)

        @block.tensor
        def _(pe):
            pe.wait_ge(kv_rot, 1)
            for q in range(G):
                if q >= 2:
                    pe.wait_ge(kvt_lo, q - 1)
                for t in range(GT):
                    m = pe.transpose(pp[q % 2][:, t * P:(t + 1) * P], kv[:, GT * q + t, :], S.ident[:, :])
                m.then_inc(kvt_full, 1)

            def fold_head(n, s, first):
                wq, kcq, wqr, kckv, wo = folded(s)
                pe.wait_ge(fold_in[s], (n + 1) * 16)
                for c in range(3):
                    m = pe.matmul(sc[s][:, 0:XR], kcq[:, c * P:(c + 1) * P], wqr[:, c * XR:(c + 1) * XR],
                                  start=c == 0, stop=c == 2)
                m.then_inc(fm_full, 1)
                pe.wait_ge(fm_done, n * 2 + (s + 1))
                if not first:
                    pe.wait_ge(c_lo, n * 2 + (s - 1))
                for c in range(C):
                    m = pe.matmul(tp[s][:, c * XR:(c + 1) * XR], wq[:, c * P:(c + 1) * P], fm[:, s, :],
                                  start=True, stop=True)
                m.then_inc(c_full, 1)
                pe.matmul(cb[s][:, :], kckv, wo, start=True, stop=True).then_inc(v_full, 1)

            for s in range(2):
                fold_head(0, s, True)
            with pe.Fori(1, HH // 2) as n:
                for s in range(2):
                    fold_head(n, s, False)

            def pp_stage(e, bank, k, need, g):
                what, i = e
                if what == "x":
                    pe.wait_ge(xs_in, (g + 1) * 16)
                    for c in range(C):
                        m = pe.transpose(bank[:, c * P:(c + 1) * P], xs[:, i, c * P:(c + 1) * P], S.ident[:, :])
                elif what == "q":
                    if i == 0:
                        pe.wait_ge(pp_free, need)
                    cols = slice(i * P, (i + 1) * P)
                    for c in range(C):
                        m = products(pe, bank[:, :], ch_[:, c, cols], cl_[:, c, cols], xgh[:, c, :], xgl[:, c, :],
                                     c == 0, c == C - 1)
                elif what == "k":
                    cols = slice(i * P, (i + 1) * P)
                    toks = bass.ds(g * N, N)
                    m = products(pe, bank[:, :], krh[:, cols], krl[:, cols], kvh[:, toks], kvl[:, toks], True, True)
                else:
                    pe.wait_ge(ct_lo, need)
                    for u in range(2):
                        for j in range(4):
                            cols = slice(j * P, (j + 1) * P)
                            h = 2 * j + u
                            m = products(pe, bank[:, :], cth[:, i % 2, u, cols], ctl[:, i % 2, u, cols],
                                         vh[:, h, :], vl[:, h, :], u == 0 and j == 0, u == 1 and j == 3)
                m.then_inc(pp_full, 1)

            pe.wait_ge(kvt_lo, G)
            for k, e in enumerate(head + proj):
                if k >= 2:
                    pe.wait_ge(pp_free, k - 1)
                if k == len(head):
                    pe.wait_ge(c_lo, HH)
                    pe.wait_ge(kr_lo, 1)
                pp_stage(e, pp[k % 2], k, len(head), 0)
            pe.wait_ge(v_lo, HH)

            def body(g, last):
                base = g * PER + PRO
                for i in range(STEPS):
                    if i < U:
                        if i == 0:
                            pe.wait_ge(pp_free, base)
                        if i >= 2:
                            pe.wait_ge(exp_done, g * U + (i - 1))
                        tok = slice((i // 2) * P, (i // 2 + 1) * P)
                        rows = slice(XR * (i % 2), XR * (i % 2 + 1))
                        for j in range(4):
                            m = pe.matmul(sc[i % 2][:, j * P:(j + 1) * P], qt[rows, j, tok], kt[rows, j, tok],
                                          start=True, stop=True)
                        m.then_inc(sc_full, 1)
                    u = i - 2
                    if 0 <= u < U:
                        pe.wait_ge(p_norm, g * U + (u + 1))
                        if u >= 2:
                            pe.wait_ge(pt_done, g * U + (u - 1))
                        for j in range(4):
                            m = pe.transpose(tp[u % 2][:, j * P:(j + 1) * P], pr[:, u % 2, j, :], S.ident[:, :])
                        m.then_inc(pt_full, 1)
                    u = i - 3
                    if 0 <= u < U:
                        if u == 0:
                            pe.wait_ge(kvs_in, (g + 1) * 16)
                        pe.wait_ge(pt_done, g * U + (u + 1))
                        if u >= 2:
                            pe.wait_ge(ct_lo, g * U + (u - 1))
                        pe.matmul(cb[u % 2][:, :], kvs[:, u // 2, :],
                                  pt[:, u % 2, :, :].rearrange("p j t -> p (j t)"),
                                  start=True, stop=True).then_inc(ct_full, 1)
                    for e, k in at_step(i, last):
                        pe.wait_ge(pp_free, base + max(k - 1, 0))
                        if e[0] == "out":
                            pp_stage(e, pp[k % 2], base + k, g * U + (2 * e[1] + 2), g)
                        else:
                            pp_stage(e, pp[k % 2], base + k, base + (LAST_X + 1), g + 1)

            over_groups(pe, [], [], body)

        blocks.close()


def ternary_ffn_phase(nc, S, w):
    J = NF0
    with Phase(nc, "ternary") as phase:
        sb, sem = phase.sb, phase.sem

        xth, xtl = sb("xth", [P, C, B * P], F32R), sb("xtl", [P, C, B * P], F32R)
        RB = 3
        raw = sb("raw", [P, RB, 3, DM])
        wq = sb("wq", [P, J, 3, DM], F32R)
        below = sb("below", [P, 3, DM])
        tot, thr = sb("tot", [P, 3]), sb("thr", [P, 3, 2])
        sg, hf = sb("sg", [P, 2, N]), sb("hf", [P, 2, N])
        hh, hl = sb("hh", [P, 2, N], F32R), sb("hl", [P, 2, N], F32R)
        st = [Stats(sb, i) for i in range(GT)]
        gate, up, yb = S.bank[0:2], S.bank[2:4], S.bank[4:8]

        raw_in = [sem(f"raw_in{b}") for b in range(RB)]
        summed, total, thr_done = sem("summed"), sem("total"), sem("thr_done")
        below_done, quant = sem("below_done"), sem("quant")
        gate_full, up_full, sig_done = sem("gate_full"), sem("up_full"), sem("sig_done")
        hf_done, hh_done, hl_done = sem("hf_done"), sem("hh_done"), sem("hl_done")
        down_done, y_free = sem("down_done"), sem("y_free")
        ve_done, rs_done, dve_chain = sem("ve_done"), sem("rs_done"), sem("dve_chain")

        blocks = ExitStack()
        block = blocks.enter_context(nc.Block())
        xt = Transposer(S, xth, xtl, sem)

        def over_tokens(eng, body):
            body(0, True)
            with eng.Fori(1, G) as g:
                body(g, False)

        @block.sync
        def _(sp):
            for j in range(J):
                if j >= RB:
                    sp.wait_ge(quant, 3 * (j - RB + 1))
                sp.dma_start(raw[:, j % RB, :, :], S.ternary[:, j, :, :]).then_inc(raw_in[j % RB], 16)

        @block.gpsimd
        def _(pool):
            pool.wait_ge(thr_done, 6)
            for j in range(J):
                pool.wait_ge(raw_in[j % RB], 16 * (j // RB + 1))
                for m in range(3):
                    if j:
                        pool.wait_ge(quant, 3 * (j - 1) + m + 1)
                    pool.tensor_scalar(below[:, m, :], raw[:, j % RB, m, :], thr[:, m, 1:2], None,
                                       ALU.is_lt).then_inc(below_done, 1)
            with pool.Fori(0, G) as g:
                for i in range(GT):
                    pool.wait_ge(ve_done, g * GT + (i + 1))
                    pool.tensor_tensor(out=st[i].rs[:, :], in0=st[i].ve[:, :], in1=S.mhalf[:, :],
                                       op=ALU.pow).then_inc(rs_done, 1)

        @block.scalar
        def _(act):
            for t in range(B):
                xt.on_act(act, t)

            def body(g, first):
                for j in range(J + 1):
                    if j < J:
                        act.wait_ge(gate_full, g * J + (j + 1))
                        if j >= 2:
                            act.wait_ge(hf_done, g * J + (j - 1))
                        act.activation(sg[:, j % 2, :], gate[j % 2][:, :], ACT.Sigmoid).then_inc(sig_done, 1)
                    if j >= 1:
                        act.wait_ge(hf_done, g * J + j)
                        if j >= 3:
                            act.wait_ge(down_done, g * (J * GT) + (j - 2) * GT)
                        act.activation(hh[:, (j - 1) % 2, :], hf[:, (j - 1) % 2, :], ACT.Copy).then_inc(hh_done, 1)

            over_tokens(act, body)

        @block.vector
        def _(dve):
            ch = Chain(dve, dve_chain)
            dve.tensor_reduce(tot[:, :], S.tern_part[:, :].rearrange("p (g m) -> p m g", m=3), AX,
                              ALU.add).then_inc(summed, 1)
            dve.wait_ge(total, 1)
            for m in range(3):
                for s in range(2):
                    sign = 0.5 if s == 0 else -0.5
                    dve.tensor_scalar(thr[:, m, s:s + 1], yb[0][:, m:m + 1], sign / (F0 * DM), sign * 1e-8,
                                      ALU.mult, ALU.add).then_inc(thr_done, 1)
            dve.wait_ge(thr_done, 6)

            def compare(j):
                for m in range(3):
                    dve.wait_ge(below_done, 3 * j + m + 1)
                    dve.scalar_tensor_tensor(out=wq[:, j, m, :], in0=raw[:, j % RB, m, :], scalar=thr[:, m, 0:1],
                                             in1=below[:, m, :], op0=ALU.is_gt, op1=ALU.subtract).then_inc(quant, 1)

            for t in range(B):
                xt.on_dve(dve, t)
                if t in (B // 2, B - 1):
                    compare(0 if t < B - 1 else 1)

            def stats(g, i):
                norm_stats(dve, ch, S.X[:, g * GT + i, :], st[i], S).then_inc(ve_done, 1)

            def normalize(g, i):
                row = S.X[:, g * GT + i, :]
                dve.wait_ge(rs_done, g * GT + (i + 1))
                dve.tensor_scalar(row, row, st[i].mv[:, 0:1], st[i].rs[:, 0:1], ALU.subtract, ALU.mult)

            def body(g, first):
                if not first:
                    ch.turn(0, g - 1, 2 * GT)
                for j in range(J + 1):
                    if j < J:
                        dve.wait_ge(sig_done, g * J + (j + 1))
                        dve.wait_ge(up_full, g * J + (j + 1))
                        if j >= 2:
                            dve.wait_ge(hh_done, g * J + (j - 1))
                        dve.tensor_tensor(hf[:, j % 2, :], sg[:, j % 2, :], up[j % 2][:, :], ALU.mult).then_inc(hf_done, 1)
                    if j >= 1:
                        q = (j - 1) % 2
                        dve.wait_ge(hh_done, g * J + j)
                        dve.tensor_tensor(hl[:, q, :], hf[:, q, :], f32(hh[:, q, :]), ALU.subtract).then_inc(hl_done, 1)
                    if first and j + 2 < J:
                        compare(j + 2)
                    if not first and 1 <= j <= GT:
                        stats(g - 1, j - 1)
                    if not first and GT < j <= 2 * GT:
                        normalize(g - 1, j - GT - 1)
                for i in range(GT):
                    row = S.X[:, g * GT + i, :]
                    dve.wait_ge(down_done, g * (J * GT) + ((J - 1) * GT + i + 1))
                    dve.tensor_tensor(row, row, yb[i][:, :], ALU.add).then_inc(y_free, 1)
                dve.wait_ge(y_free, g * GT + GT)

            over_tokens(dve, body)
            ch.turn(0, G - 1, 2 * GT)
            for i in range(GT):
                stats(G - 1, i)
            for i in range(GT):
                normalize(G - 1, i)

        @block.tensor
        def _(pe):
            pe.wait_ge(summed, 1)
            pe.matmul(yb[0][:, 0:3], S.ones_f[:, :], tot[:, :], start=True, stop=True).then_inc(total, 1)
            xt.on_pe(pe)
            pe.wait_ge(xt.lo, B)
            pe.wait_ge(thr_done, 6)

            def body(g, first):
                toks = bass.ds(g * N, N)

                def ups(dst, m, j):
                    if first:
                        pe.wait_ge(quant, 3 * j + m + 1)
                    for c in range(C):
                        for n, x in enumerate((xth, xtl)):
                            a = pe.matmul(dst[:, :], wq[:, j, m, c * P:(c + 1) * P], x[:, c, toks],
                                          start=c == 0 and n == 0, stop=c == C - 1 and n == 1)
                    return a

                def down(j):
                    pe.wait_ge(hl_done, g * J + (j + 1))
                    if first:
                        pe.wait_ge(quant, 3 * j + 3)
                    for i in range(GT):
                        for n, h in enumerate((hh, hl)):
                            a = pe.matmul(yb[i][:, :], h[:, j % 2, i * P:(i + 1) * P], wq[:, j, 2, :],
                                          start=j == 0 and n == 0, stop=j == J - 1 and n == 1)
                        a.then_inc(down_done, 1)

                for j in range(J):
                    if j >= 2:
                        pe.wait_ge(sig_done, g * J + (j - 1))
                    ups(gate[j % 2], 0, j).then_inc(gate_full, 1)
                    if j >= 2:
                        pe.wait_ge(hf_done, g * J + (j - 1))
                    if j >= 2:
                        down(j - 2)
                    ups(up[j % 2], 1, j).then_inc(up_full, 1)
                down(J - 2)
                down(J - 1)

            over_tokens(pe, body)

        blocks.close()


def expert_ffn_phase(nc, S, w):
    WU, WD = 2 * F1 * C, len(FT) * DM
    WE = WU + WD
    J = len(FT)
    Q = 2 * J
    with Phase(nc, "expert") as phase:
        sb, sem = phase.sb, phase.sem

        xth, xtl = sb("xth", [P, C, B * P], F32R), sb("xtl", [P, C, B * P], F32R)
        raw = sb("raw", [P, WE])
        weh, wel = sb("weh", [P, 2, WE], F32R), sb("wel", [P, 2, WE], F32R)
        sg, hf = sb("sg", [P, 2, N]), sb("hf", [P, 2, N])
        hh, hl = sb("hh", [P, 2, N], F32R), sb("hl", [P, 2, N], F32R)
        gw = sb("gw", [P, C, E])
        gwh, gwl = (t[:, 0, 0:C * P].rearrange("p (c n) -> p c n", c=C) for t in (hh, hl))
        lg, ex, m8, eq = (sb(n, [P, B, E]) for n in ("lg", "ex", "m8", "eq"))
        ix, ixf = sb("ix", [P, B, E], U32), sb("ixf", [P, B, E])
        mx, rec = sb("mx", [P, B]), sb("rec", [P, B])
        comb = sb("comb", [P, NE * B])
        st = [Stats(sb, i) for i in range(GT)]
        gate, up, yb = S.bank[0:2], S.bank[2:4], S.bank[4:8]

        raw_in, w_hi, w_lo = sem("raw_in"), sem("w_hi"), sem("w_lo")
        gw_in, gw_zero, gw_hi, gw_lo = sem("gw_in"), sem("gw_zero"), sem("gw_hi"), sem("gw_lo")
        rt_full, rt_copied, lg_full = sem("rt_full"), sem("rt_copied"), sem("lg_full")
        diff_done, ex_done, router_chain = sem("diff_done"), sem("ex_done"), sem("router_chain")
        gate_full, up_full, sig_done = sem("gate_full"), sem("up_full"), sem("sig_done")
        hf_done, hh_done, hl_done = sem("hf_done"), sem("hh_done"), sem("hl_done")
        down_done, y_free = sem("down_done"), sem("y_free")
        ve_done, rs_done, dve_chain = sem("ve_done"), sem("rs_done"), sem("dve_chain")
        x_done, stored = sem("x_done"), sem("stored")

        blocks = ExitStack()
        block = blocks.enter_context(nc.Block())
        xt = Transposer(S, xth, xtl, sem)

        def up_w(t, s, c, col, width):
            return t[:, s, c * 2 * F1 + col:c * 2 * F1 + col + width]

        def down_w(t, s, j):
            return t[0:FT[j], s, WU + j * DM:WU + (j + 1) * DM]

        def over_experts(eng, body):
            with eng.Fori(0, NE // 2 - 1) as n:
                for s in range(2):
                    body(n, s, False)
            for s in range(2):
                body(NE // 2 - 1, s, s == 1)

        @block.sync
        def _(sp):
            sp.dma_start(gw[:, :, :], w["router"]).then_inc(gw_in, 16)
            sp.dma_start(raw[:, :], w["experts"][0]).then_inc(raw_in, 16)
            with sp.Fori(1, NE) as e:
                sp.wait_ge(w_lo, e * 1)
                sp.dma_start(raw[:, :], w["experts"][bass.ds(e, 1)].rearrange("a p n -> (a p) n")).then_inc(raw_in, 16)
            with sp.Fori(0, G) as g:
                sp.wait_ge(x_done, g * 1 + 1)
                sp.dma_start(S.out_dram[:, bass.ds(g * GT, GT), :], S.X[:, bass.ds(g * GT, GT), :]).then_inc(stored, 16)
            sp.wait_ge(stored, 16 * G)

        @block.gpsimd
        def _(pool):
            pool.memset(comb[:, E * B:NE * B], 1.0).then_inc(gw_zero, 1)
            with pool.Fori(0, G) as g:
                for i in range(GT):
                    pool.wait_ge(ve_done, g * GT + (i + 1))
                    pool.tensor_tensor(out=st[i].rs[:, :], in0=st[i].ve[:, :], in1=S.mhalf[:, :],
                                       op=ALU.pow).then_inc(rs_done, 1)

        @block.scalar
        def _(act):
            act.wait_ge(gw_in, 16)
            act.wait_ge(gw_zero, 3)
            act.activation(gwh[:, :, 0:E], gw[:, :, :], ACT.Copy).then_inc(gw_hi, 1)
            for t in range(B):
                xt.on_act(act, t)
            act.wait_ge(raw_in, 16)
            act.activation(weh[:, 0, :], raw[:, :], ACT.Copy).then_inc(w_hi, 1)
            act.wait_ge(diff_done, 1)
            act.activation(ex[:, :, :], lg[:, :, :], ACT.Exp).then_inc(ex_done, 1)

            def body(n, s, last):
                if not last:
                    act.wait_ge(raw_in, n * 32 + (16 * s + 32))
                    act.wait_ge(gate_full, n * (4 * Q) + (2 * Q * s + 1))
                    act.activation(weh[:, 1 - s, :], raw[:, :], ACT.Copy).then_inc(w_hi, 1)
                with act.Fori(0, G // 2) as m:
                    t = n * (4 * Q) + m * Q
                    for q in range(Q + 1):
                        if q < Q:
                            act.wait_ge(gate_full, t + (2 * Q * s + q + 1))
                            if q >= 2:
                                act.wait_ge(hf_done, t + (2 * Q * s + q - 1))
                            r = FT[q % J]
                            act.activation(sg[0:r, q % 2, :], gate[q % 2][0:r, :], ACT.Silu).then_inc(sig_done, 1)
                        if q >= 1:
                            act.wait_ge(hf_done, t + (2 * Q * s + q))
                            if q >= 3:
                                act.wait_ge(down_done, t * GT + GT * (2 * Q * s + q - 2))
                            b, r = (q - 1) % 2, FT[(q - 1) % J]
                            act.activation(hh[0:r, b, :], hf[0:r, b, :], ACT.Copy).then_inc(hh_done, 1)

            over_experts(act, body)

        @block.vector
        def _(dve):
            ch = Chain(dve, dve_chain)
            rc = Chain(dve, router_chain)
            for t in (gwh, gwl):
                dve.memset(f32(t), 0.0).then_inc(gw_zero, 1)
            dve.wait_ge(gw_hi, 1)
            dve.tensor_tensor(gwl[:, :, 0:E], gw[:, :, :], f32(gwh[:, :, 0:E]), ALU.subtract).then_inc(gw_lo, 1)
            for t in range(B):
                xt.on_dve(dve, t)
            dve.wait_ge(w_hi, 1)
            dve.tensor_tensor(wel[:, 0, :], raw[:, :], f32(weh[:, 0, :]), ALU.subtract).then_inc(w_lo, 1)
            for g in range(G):
                dve.wait_ge(rt_full, g + 1)
                dve.tensor_copy(sg[0:E, g % 2, :], gate[g % 2][0:E, :]).then_inc(rt_copied, 1)
            dve.wait_ge(lg_full, 1)
            b8 = lambda t: t.unsqueeze(2).broadcast_to((P, B, E))
            rc.link(dve.tensor_copy(lg[:, :, :], yb[-1][:, 0:B * E].rearrange("p (t e) -> p t e", e=E)))
            rc.link(dve.tensor_reduce(mx[:, :], lg[:, :, :], AX, ALU.max))
            dve.tensor_tensor(lg[:, :, :], lg[:, :, :], b8(mx[:, :]), ALU.subtract).then_inc(diff_done, 1)
            dve.wait_ge(ex_done, 1)
            rc.link(dve.tensor_reduce(mx[:, :], ex[:, :, :], AX, ALU.add))
            rc.link(dve.reciprocal(rec[:, :], mx[:, :]))
            rc.link(dve.tensor_tensor(ex[:, :, :], ex[:, :, :], b8(rec[:, :]), ALU.mult))
            for t in range(B):
                a = dve.max(out=m8[:, t, :], in_=ex[:, t, :])
            rc.link(a)
            for t in range(B):
                a = dve.max_index(ix[:, t, :], m8[:, t, :], ex[:, t, :])
            rc.link(a)
            rc.link(dve.tensor_copy(ixf[:, :, :], ix[:, :, :]))
            for q in range(2):
                dst = (eq, lg)[q]
                io = S.iota[:, :].unsqueeze(1).broadcast_to((P, B, E))
                rc.link(dve.tensor_tensor(dst[:, :, :], io, b8(ixf[:, :, q]), ALU.is_equal))
                rc.link(dve.tensor_tensor(dst[:, :, :], dst[:, :, :], b8(m8[:, :, q]), ALU.mult))
            rc.link(dve.tensor_tensor(comb[:, 0:E * B].rearrange("p (e t) -> p t e", e=E), eq[:, :, :], lg[:, :, :], ALU.add))
            dve.wait_ge(gw_zero, 3)

            def body(n, s, last):
                if not last:
                    dve.wait_ge(w_hi, n * 2 + (s + 2))
                    dve.tensor_tensor(wel[:, 1 - s, :], raw[:, :], f32(weh[:, 1 - s, :]), ALU.subtract).then_inc(w_lo, 1)
                with dve.Fori(0, G // 2) as m:
                    t = n * (4 * Q) + m * Q
                    y = n * (2 * B) + m * (2 * GT)
                    if last:
                        ch.turn(0, m, 4 * GT)

                    def sums(gg):
                        for i in range(GT):
                            k = B * s + gg * GT + i
                            dve.wait_ge(down_done, t * GT + GT * (2 * Q * s) + (gg * J * GT + (J - 1) * GT + i + 1))
                            weight = comb[:, bass.ds(n * (2 * B) + m * (2 * GT) + k, 1)]
                            dve.scalar_tensor_tensor(out=row(gg, i), in0=yb[i][:, :], scalar=weight, in1=row(gg, i),
                                                     op0=ALU.mult, op1=ALU.add).then_inc(y_free, 1)

                    def row(gg, i):
                        return S.X[:, bass.ds(m * (2 * GT) + (gg * GT + i), 1), :].rearrange("p a n -> p (a n)")

                    for q in range(Q + 1):
                        if q in (J + 1, Q):
                            gg = 0 if q == J + 1 else 1
                        if q == J + 1:
                            sums(gg)
                        if q < Q:
                            r = FT[q % J]
                            dve.wait_ge(sig_done, t + (2 * Q * s + q + 1))
                            dve.wait_ge(up_full, t + (2 * Q * s + q + 1))
                            if q >= 2:
                                dve.wait_ge(hh_done, t + (2 * Q * s + q - 1))
                            dve.tensor_tensor(hf[0:r, q % 2, :], sg[0:r, q % 2, :], up[q % 2][0:r, :],
                                              ALU.mult).then_inc(hf_done, 1)
                        if q >= 1:
                            b, r = (q - 1) % 2, FT[(q - 1) % J]
                            dve.wait_ge(hh_done, t + (2 * Q * s + q))
                            dve.tensor_tensor(hl[0:r, b, :], hf[0:r, b, :], f32(hh[0:r, b, :]),
                                              ALU.subtract).then_inc(hl_done, 1)
                        if q == Q:
                            sums(gg)
                        if last and q in (J + 1, Q):
                            for i in range(GT):
                                dve.wait_ge(y_free, y + (B * s + gg * GT + i + 1))
                                norm_stats(dve, ch, row(gg, i), st[i], S).then_inc(ve_done, 1)
                            for i in range(GT):
                                dve.wait_ge(rs_done, m * (2 * GT) + (gg * GT + i + 1))
                                a = dve.tensor_scalar(row(gg, i), row(gg, i), st[i].mv[:, 0:1], st[i].rs[:, 0:1],
                                                      ALU.subtract, ALU.mult)
                                if i == GT - 1:
                                    a.then_inc(x_done, 1)

            over_experts(dve, body)

        @block.tensor
        def _(pe):
            def router_rows(g):
                pe.wait_ge(rt_copied, g + 1)
                for i in range(GT):
                    t = g * GT + i
                    m = pe.transpose(yb[-1][:, t * E:(t + 1) * E], sg[0:E, g % 2, i * P:(i + 1) * P], S.ident[0:E, 0:E])
                return m

            xt.on_pe(pe)
            pe.wait_ge(xt.lo, B)
            pe.wait_ge(gw_lo, 1)
            for g in range(G):
                if g >= 2:
                    pe.wait_ge(rt_copied, g - 1)
                cols = slice(g * N, (g + 1) * N)
                for c in range(C):
                    m = products(pe, gate[g % 2][:, :], gwh[:, c, :], gwl[:, c, :], xth[:, c, cols], xtl[:, c, cols],
                                 c == 0, c == C - 1)
                m.then_inc(rt_full, 1)
                if g >= 1:
                    router_rows(g - 1)
            router_rows(G - 1).then_inc(lg_full, 1)

            def ups(dst, s, col, r, toks):
                for c in range(C):
                    m = products(pe, dst[0:r, :], up_w(weh, s, c, col, r), up_w(wel, s, c, col, r),
                                 xth[:, c, toks], xtl[:, c, toks], c == 0, c == C - 1)
                return m

            def body(n, s, last):
                with pe.Fori(0, G // 2) as m:
                    pe.wait_ge(w_lo, n * 2 + (s + 1))
                    t = n * (4 * Q) + m * Q

                    def down(q):
                        j, r = q % J, FT[q % J]
                        pe.wait_ge(hl_done, t + (2 * Q * s + q + 1))
                        if j == 0 and q:
                            pe.wait_ge(y_free, n * (2 * B) + m * (2 * GT) + (B * s + (q // J) * GT))
                        for i in range(GT):
                            cols = slice(i * P, (i + 1) * P)
                            ins = products(pe, yb[i][:, :], hh[0:r, q % 2, cols], hl[0:r, q % 2, cols],
                                           down_w(weh, s, j), down_w(wel, s, j), j == 0, j == J - 1)
                            ins.then_inc(down_done, 1)

                    for q in range(Q):
                        j = q % J
                        toks = bass.ds(m * (2 * N) + (q // J) * N, N)
                        if q >= 2:
                            pe.wait_ge(sig_done, t + (2 * Q * s + q - 1))
                        ups(gate[q % 2], s, j * P, FT[j], toks).then_inc(gate_full, 1)
                        if q >= 2:
                            pe.wait_ge(hf_done, t + (2 * Q * s + q - 1))
                        ups(up[q % 2], s, F1 + j * P, FT[j], toks).then_inc(up_full, 1)
                        if q >= 1:
                            down(q - 1)
                    down(Q - 1)

            over_experts(pe, body)

        blocks.close()


def build(nc, a, out, phases=6):
    with ExitStack() as ctx:
        S = Shared()

        def sb(n, shape, dt=F32):
            return ctx.enter_context(nc.sbuf_tensor(n, shape, dt))

        S.bank = [ctx.enter_context(nc.psum_tensor(f"bank{i}", [P, N], F32)) for i in range(8)]
        S.X = sb("X", [P, B, DM])
        S.ident, S.ones_f = sb("ident", [P, P]), sb("ones_f", [P, P])
        S.ones = sb("ones", [1, P], F32R)
        S.mhalf, S.iota = sb("mhalf", [P, 1]), sb("iota", [P, E])
        S.tern_part = sb("tern_part", [P, 3 * G])
        lower, upper, causal = sb("lower", [P, P]), sb("upper", [P, P]), sb("causal", [P, P])
        S.dist = sb("dist", [P, P])
        S.lower4, S.upper4, S.causal4 = (t[:, :].unsqueeze(1).broadcast_to((P, 4, P)) for t in (lower, upper, causal))
        S.x_dram = a[""]["x"].rearrange("b p n -> p b n")
        S.ctx_dram = a[""]["ctx"].rearrange("b p n -> p b n")
        S.out_dram = out.rearrange("b p n -> p b n")
        S.x_kept = nc.dram_tensor("x_kept", (P, B, DM), F32).ap()
        S.ternary = a["ternary"]["w"]
        S.rope_rows, S.rope_cols, S.kv_rope = a[""]["rope_rows"], a[""]["rope_cols"], a[""]["kv_rope"]
        loaded, S.ones_set = ctx.enter_context(nc.semaphore("tables_in")), ctx.enter_context(nc.semaphore("ones_set"))
        tables = [(S.ident, a[""]["ident"]), (lower, a[""]["lower"]), (upper, a[""]["upper"]), (causal, a[""]["causal"]), (S.dist, a[""]["dist"]), (S.iota, a[""]["iota"])]
        with nc.Block() as block:
            @block.sync
            def _(sp):
                for dst, src in tables:
                    sp.dma_start(dst[:, :], src).then_inc(loaded, 16)
                sp.wait_ge(loaded, 16 * len(tables))

            @block.vector
            def _(dve):
                for t, v in ((S.ones_f[:, :], 1.0), (f32(S.ones[:, :]), 1.0), (S.mhalf[:, :], -0.5)):
                    dve.memset(t, v).then_inc(S.ones_set, 1)
                dve.wait_ge(S.ones_set, 3)

        if phases >= 1:
            attention_phase(nc, S, "gqa", a["attn0"])
        if phases >= 2:
            latent_phase(nc, S, a["latent"], 0)
            latent_phase(nc, S, a["latent"], 1)
        if phases >= 3:
            ternary_ffn_phase(nc, S, a["ternary"])
        if phases >= 4:
            attention_phase(nc, S, "decay", a["attn1"])
        if phases >= 5:
            attention_phase(nc, S, "causal", a["cross1"])
        if phases >= 6:
            expert_ffn_phase(nc, S, a["expert"])
        else:
            with nc.Block() as block:
                dbg = ctx.enter_context(nc.semaphore("dbg"))

                @block.sync
                def _(sp):
                    sp.dma_start(S.out_dram, S.X[:, :, :]).then_inc(dbg, 16)
                    sp.wait_ge(dbg, 16)


def layouts(i):
    import numpy as np

    def lay(t):
        return np.ascontiguousarray(t.reshape(-1, P, t.shape[1]).transpose(1, 0, 2))

    def rows(t):
        return np.ascontiguousarray(np.broadcast_to(t.reshape(1, -1), (P, t.size)))

    def cols(*ts):
        t = np.concatenate([t.reshape(-1, P) for t in ts]).T
        return np.ascontiguousarray(np.concatenate([t, np.zeros((P, 8 - t.shape[1]), t.dtype)], 1))

    o = {"x": i["x"], "ctx": i["ctx_512"]}
    turn = lambda t: t.reshape(KV, H // KV, D, -1).transpose(1, 0, 2, 3).reshape(DM, -1)
    swap = lambda t: t.reshape(-1, 2, D // 2)[:, ::-1].reshape(-1)
    bq, bk = turn(i["L0_attn_bq"]).reshape(-1), i["L0_attn_bk"]
    o |= {"attn0.q": lay(turn(i["L0_attn_wq"]).T), "attn0.k": lay(i["L0_attn_wk"].T), "attn0.v": lay(i["L0_attn_wv"].T),
          "attn0.o": lay(i["L0_attn_wo"].T), "attn0.bqk": cols(bq, bk), "attn0.bqk_swapped": cols(swap(bq), swap(bk)),
          "attn0.bv": rows(i["L0_attn_bv"]), "attn0.bo": i["L0_attn_bo"].reshape(1, -1)}
    w = i["L1_attn_Wqkv"]
    b = i["L1_attn_bqkv"]
    o |= {"attn1.q": lay(w[:, :DM]), "attn1.k": lay(w[:, DM:2 * DM]), "attn1.v": lay(w[:, 2 * DM:]),
          "attn1.o": lay(i["L1_attn_Wout"]), "attn1.bqk": cols(b[:2 * DM]), "attn1.bv": rows(b[2 * DM:]),
          "attn1.bo": i["L1_attn_bout"].reshape(1, -1), "attn1.slopes": rows(i["L1_attn_slopes"])}
    w = i["L1_xattn_Wkv_expand"].T
    o |= {"cross1.q": lay(i["L1_xattn_Wq"].T), "cross1.k": lay(w[:, :DM]), "cross1.v": lay(w[:, DM:]),
          "cross1.o": lay(i["L1_xattn_Wout"].T)}
    o["latent.fold"] = np.concatenate([
        i["L0_xattn_Wq"].reshape(XH, P, DM),
        i["L0_xattn_w_kc_q"].reshape(XH, P, 3, P).transpose(0, 3, 2, 1).reshape(XH, P, 3 * P),
        i["L0_xattn_W_qr"].reshape(XH, 3, P, XR).transpose(0, 2, 1, 3).reshape(XH, P, 3 * XR),
        i["L0_xattn_w_kc_kv"],
        i["L0_xattn_Wo"].T.reshape(XH, P, DM)], 2)
    o["latent.kr"] = np.ascontiguousarray(i["L0_xattn_W_kr"].transpose(1, 0, 2)).reshape(P, -1)
    up = [lay(i[f"L0_ffn_{k}"].T).reshape(P, C, NF0, P).transpose(0, 2, 1, 3).reshape(P, NF0, DM) for k in ("w1", "w2")]
    o["ternary.w"] = np.stack(up + [lay(i["L0_ffn_w3"].T)], 2)
    gu, dn = i["L1_ffn_gate_up_weights"], i["L1_ffn_down_weights"]
    sg, sd = i["L1_ffn_shared_gate_up"].reshape(2, 2, F1, DM), i["L1_ffn_shared_down"].reshape(DM, 2, F1)
    ex = []
    for e in range(NE):
        u = gu[e] if e < E else sg[:, e - E].reshape(2 * F1, DM)
        d = (dn[e] if e < E else sd[:, e - E]).T
        d = np.concatenate([d, np.zeros((len(FT) * P - F1, DM), d.dtype)])
        ex.append(np.concatenate([lay(u.T).reshape(P, -1), lay(d).reshape(P, -1)], 1))
    o["expert.experts"] = np.stack(ex)
    o["expert.router"] = lay(i["L1_ffn_gate_weight"].T)
    return {k: np.ascontiguousarray(v) for k, v in o.items()}


def tables():
    import numpy as np
    f = np.float32
    t = np.arange(P)
    inv = (1.0 / f(10000.0) ** (np.arange(0, D, 2, dtype=f) / f(D))).astype(f)

    def rope(pos, inv, repeat):
        fr = pos[:, None].astype(f) * inv[None, :]
        e = np.repeat(fr, 2, -1) if repeat else np.concatenate([fr, fr], -1)
        sn = np.sin(e)
        sn[:, :e.shape[1] // 2] *= -1
        return np.stack([np.cos(e), sn])

    r = rope(np.arange(H), inv, False)
    q = r.reshape(2, KV, H // KV, D).transpose(0, 2, 1, 3).reshape(2, DM)
    qk = np.concatenate([q, r[:, :KV].reshape(2, P)], 1)
    cols = np.concatenate([qk.reshape(2, 5, P), np.zeros((2, 3, P), f)], 1).transpose(2, 0, 1)
    invk = (1.0 / f(10000.0) ** (np.arange(0, P, 2, dtype=f) / f(P))).astype(f)
    d = t[:, None] - t[None, :]
    o = {"ident": np.eye(P), "lower": np.where(d <= 0, np.exp(1.0), 1.0), "upper": np.where(d <= 0, 1.0, 0.0),
         "causal": np.where(d >= 0, 0.0, -1e38), "dist": np.maximum(-d, 0), "iota": np.tile(np.arange(E), (P, 1)),
         "rope_rows": np.broadcast_to(qk, (P, 2, DM + P)), "rope_cols": cols,
         "kv_rope": rope(t, invk, True).transpose(1, 0, 2)}
    return {k: np.ascontiguousarray(v.astype(f)) for k, v in o.items()}


def kernel(**inputs):
    import concourse.bacc as bacc
    import numpy as np
    from concourse.bass_utils import run_bass_kernel_spmd

    arrays = layouts({k: np.asarray(v) for k, v in inputs.items()}) | tables()
    nc = bacc.Bacc("TRN2", target_bir_lowering=False, num_devices=1)
    a = {g: {} for g in ("", "attn0", "latent", "ternary", "attn1", "cross1", "expert")}
    for name, v in arrays.items():
        group, _, key = name.rpartition(".")
        a[group][key] = nc.dram_tensor("in_" + name.replace(".", "_"), v.shape, F32, kind="ExternalInput").ap()
    out = nc.dram_tensor("out", (B, P, DM), F32, kind="ExternalOutput").ap()
    build(nc, a, out)
    r = run_bass_kernel_spmd(nc, [{"in_" + k.replace(".", "_"): v for k, v in arrays.items()}], core_ids=[0])
    return r.results[0]["out"]
```

```python
import concourse.bass as bass
from concourse import mybir
from contextlib import ExitStack

F32 = mybir.dt.float32
F32R = mybir.dt.float32r
U32 = mybir.dt.uint32
ALU = mybir.AluOpType
ACT = mybir.ActivationFunctionType
AX = mybir.AxisListType.X

P = 128
B = 16
DM = 512
C = DM // P
GT = 4
G = B // GT
N = GT * P
H = 16
D = DM // H
KV = 4
XH = 16
XR = 64
XQ = 384
F0 = 1408
NF0 = F0 // P
E = 8
ST = 2
SN = ST * P
TILES = (2 * B * P - E) // SN + E
SLOTS = TILES * SN
F1 = 352
NE = E + 2
FT = [128, 128, 96]
EPS = 1e-5


class Shared:
    pass


class Stats:

    def __init__(self, sb, i):
        self.six, self.mv = sb(f"six{i}", [P, 6]), sb(f"mv{i}", [P, 2])
        self.ve, self.rs, self.spare = sb(f"ve{i}", [P, 1]), sb(f"rs{i}", [P, 1]), sb(f"spare{i}", [P, 2])


class Transposer:

    def __init__(self, S, xth, xtl, sem):
        self.S, self.xth, self.xtl = S, xth, xtl
        self.full, self.hi, self.lo = sem("xt_full"), sem("xt_hi"), sem("xt_lo")

    def on_pe(self, pe):
        S = self.S
        for t in range(B):
            if t >= 2:
                pe.wait_ge(self.lo, t - 1)
            for c in range(C):
                m = pe.transpose(S.bank[t % 2][:, c * P:(c + 1) * P], S.X[:, t, c * P:(c + 1) * P], S.ident[:, :])
            m.then_inc(self.full, 1)

    def on_act(self, act, t):
        act.wait_ge(self.full, t + 1)
        act.activation(self.xth[:, :, t * P:(t + 1) * P], four(self.S.bank[t % 2]), ACT.Copy).then_inc(self.hi, 1)

    def on_dve(self, dve, t):
        dve.wait_ge(self.hi, t + 1)
        cols = slice(t * P, (t + 1) * P)
        dve.tensor_tensor(self.xtl[:, :, cols], four(self.S.bank[t % 2]), f32(self.xth[:, :, cols]),
                          ALU.subtract).then_inc(self.lo, 1)


class Chain:

    def __init__(self, eng, sem):
        self.eng, self.sem, self.base, self.k = eng, sem, 0, 0

    def mark(self, ins):
        ins.then_inc(self.sem, 1)
        self.k += 1
        return self.base + self.k

    def link(self, ins):
        self.eng.wait_ge(self.sem, self.mark(ins))

    def wait(self, value):
        self.eng.wait_ge(self.sem, value)

    def turn(self, start, g, per):
        self.base, self.k = start + g * per, 0


def over_groups(eng, chains, per, body):
    starts = [c.base + c.k for c in chains]
    with eng.Fori(0, G - 1) as g:
        for c, s, p in zip(chains, starts, per):
            c.turn(s, g, p)
        body(g, False)
        for c, p in zip(chains, per):
            assert c.k == p, (c.k, p)
    for c, s, p in zip(chains, starts, per):
        c.turn(s, G - 1, p)
    body(G - 1, True)


def products(pe, out, wh, wl, xh, xl, first, last, **kw):
    pe.matmul(out, wh, xh, start=first, stop=False, **kw)
    pe.matmul(out, wh, xl, start=False, stop=False, **kw)
    return pe.matmul(out, wl, xh, start=False, stop=last, **kw)


class Phase:

    def __init__(self, nc, name):
        self.nc, self.name, self.ctx, self.sems = nc, name, ExitStack(), []

    def __enter__(self):
        return self

    def sb(self, name, shape, dt=F32):
        return self.ctx.enter_context(self.nc.sbuf_tensor(f"{self.name}_{name}", shape, dt))

    def sem(self, name):
        self.sems.append(self.ctx.enter_context(self.nc.semaphore(f"{self.name}_{name}")))
        return self.sems[-1]

    def __exit__(self, *exc):
        if exc[0] is None:
            with self.nc.Block() as block:
                @block.sync
                def _(sp):
                    for s in self.sems:
                        sp.sem_clear(s)
        self.ctx.__exit__(*exc)


def four(bank):
    return bank[:, :].rearrange("p (c n) -> p c n", n=P)


def f32(ap):
    return ap.bitcast(F32)


def norm_stats(dve, ch, row, st, S):
    dve.tensor_copy(st.spare[:, 0:1], S.mhalf[:, :])
    ch.link(dve.bn_stats(out=st.six[:, :], in_=row))
    dve.tensor_copy(st.spare[:, 1:2], S.mhalf[:, :])
    ch.link(dve.bn_aggr(out=st.mv[:, :], in_=st.six[:, :]))
    return dve.tensor_scalar(st.ve[:, :], st.mv[:, 1:2], EPS, None, ALU.add)


def attention_phase(nc, S, kind, w):
    nk = 1 if kind == "gqa" else C
    kc = 1 if kind == "causal" else C
    nv = KV if kind == "gqa" else H
    vw = nv * D
    soft = kind != "decay"
    bias = kind != "causal"
    scale = D ** -0.5
    U = 4 * GT
    OW = D + 1
    with Phase(nc, kind) as phase:
        sb, sem = phase.sb, phase.sem

        ws = sb("ws", [P, 2, C * DM])
        xs = sb("xs", [P, GT, DM])
        xgh, xgl = sb("xgh", [P, C, N], F32R), sb("xgl", [P, C, N], F32R)
        wqh, wql = sb("wqh", [P, C, DM], F32R), sb("wql", [P, C, DM], F32R)
        wkh, wkl = sb("wkh", [P, kc, nk * P], F32R), sb("wkl", [P, kc, nk * P], F32R)
        wvh, wvl = sb("wvh", [P, kc, vw], F32R), sb("wvl", [P, kc, vw], F32R)
        woh, wol = sb("woh", [P, C, DM], F32R), sb("wol", [P, C, DM], F32R)
        qt, kt = sb("qt", [P, C, N]), sb("kt", [P, nk, N])
        v1 = sb("v1", [P, GT, nv, OW])
        pt = sb("pt", [P, 2, 4, P])
        on = sb("on", [P, 2, DM])
        oth, otl = sb("oth", [P, C, P], F32R), sb("otl", [P, C, P], F32R)
        rec = sb("rec", [P, H])
        st = [Stats(sb, i) for i in range(2)]
        if soft:
            pr = sb("pr", [P, 2, 4, P])
            nm, nb = sb("nm", [P, 2, 4]), sb("nb", [P, 2, 4])
        if kind == "causal":
            sm = sb("sm", [P, 2, 4, P])
            cs = sb("cs", [P, GT, P])
            cgh, cgl = sb("cgh", [P, N], F32R), sb("cgl", [P, N], F32R)
        if bias:
            bqk = sb("bqk", [P, 8])
            bvr = sb("bvr", [P, vw])
            bor = sb("bor", [1, DM])
            boh, bol = sb("boh", [1, DM], F32R), sb("bol", [1, DM], F32R)
        if kind == "gqa":
            rope = sb("rope", [P, 2, C * P + P])
            rt = sb("rt", [P, 2, DM])
            bsw, brp = sb("bsw", [P, 8]), sb("brp", [P, 2, 8])
            bt = sb("bt", [P, 8])
            tw, junk = sb("tw", [P, NF0, 3, P]), sb("junk", [P, NF0, P])
        if kind == "decay":
            dec = sb("dec", [P, 4, 4, P])
            slp, nslp = sb("slp", [P, H]), sb("nslp", [P, H])
            zeros = sb("zeros", [P, 2 * DM])
        pp, sc, tp, ob = S.bank[0:2], S.bank[2:4], S.bank[4:6], S.bank[6:8]

        ws_in = [sem(f"ws_in{i}") for i in range(2)]
        ws_hi, ws_lo, ws_rope = sem("ws_hi"), sem("ws_lo"), sem("ws_rope")
        const_in, ones_set, bias_hi, const_ok = sem("const_in"), sem("ones_set"), sem("bias_hi"), sem("const_ok")
        x_in, xs_in = sem("x_in"), sem("xs_in")
        pp_full, pp_hi, pp_free = sem("pp_full"), sem("pp_hi"), sem("pp_free")
        sc_full, max_done, exp_done = sem("sc_full"), sem("max_done"), sem("exp_done")
        pt_full, pt_done, pv_done = sem("pt_full"), sem("pt_done"), sem("pv_done")
        o_norm = sem("o_norm")
        ve_done, rs_done = sem("ve_done"), sem("rs_done")
        dve_chain, act_chain = sem("dve_chain"), sem("act_chain")
        bias_lo = sem("bias_lo")
        tw_in, tw_summed = sem("tw_in"), sem("tw_summed")
        zero_set, slots_zero = sem("zero_set"), sem("slots_zero")

        pieces = [(w["q"], wqh, wql), (w["k"], wkh, wkl), (w["v"], wvh, wvl), (w["o"], woh, wol)]
        flat = lambda t: t[:, :, :].rearrange("p c n -> p (c n)")

        head = [("x", i) for i in range(GT)] + ([("c", 0)] if kind == "causal" else [])
        proj = [("q", j) for j in range(C)] + [("k", j) for j in range(nk)] + [("v", i) for i in range(GT)]
        STEPS = U + 8
        own = {i: [] for i in range(STEPS)}
        nxt = {i: [] for i in range(STEPS)}
        for b in range(GT):
            own[4 * b + 8].append(("ot", b))
            own[4 * b + 10].append(("out", b))
        for n, e in enumerate(head):
            nxt[1 + 2 * n].append(e)
        for n, e in enumerate(proj):
            nxt[19 + e[1] // 2 if e[0] == "v" else 16 + n // 3].append(e)
        LAG = 3 if soft else 1

        def stages(last):
            out, k = [], 0
            for i in range(STEPS):
                for e in ([] if last else nxt[i]) + own[i]:
                    out.append((i, e, k))
                    k += 1
            return out

        def at_step(i, last):
            return [(e, k) for j, e, k in stages(last) if j == i]

        PRO = len(head) + len(proj)
        PER = PRO + 2 * GT
        HI = ("x", "c", "ot")
        PRO_HI, PER_HI = len(head), len(head) + GT
        LAST_X = max(k for _, e, k in stages(False) if e in head)

        def his_before(k, last):
            return sum(e[0] in HI for _, e, n in stages(last) if n < k)

        def heads_of(u):
            r = u % 4
            for j in range(4):
                yield j, j, (0 if kind == "gqa" else j), slice(D * r, D * r + D), \
                    (4 * r + j if kind == "gqa" else 4 * j + r), (r if kind == "gqa" else 4 * j + r)

        FIRST_STAGED = kind == "gqa"
        loads_n = 3 * bias + 3 * (kind == "gqa") + (kind == "decay")
        if kind == "causal":
            cgh_v = cgh[:, :].rearrange("p (c n) -> p c n", n=P)
            cgl_v = cgl[:, :].rearrange("p (c n) -> p c n", n=P)
        else:
            cgh_v = cgl_v = None

        blocks = ExitStack()
        block = blocks.enter_context(nc.Block())

        @block.sync
        def _(sp):
            x_src = S.x_dram if kind == "gqa" else S.X

            def stage(g):
                if FIRST_STAGED or not isinstance(g, int) or g:
                    sp.dma_start(xs[:, :, :], x_src[:, bass.ds(g * GT, GT), :]).then_inc(xs_in, 16)
                if kind == "causal":
                    sp.dma_start(cs[:, :, :], S.ctx_dram[:, bass.ds(g * GT, GT), :]).then_inc(xs_in, 16)

            stage(0)
            for p, (src, hi, lo) in enumerate(pieces):
                if p >= 2:
                    sp.wait_ge(ws_lo, p - 1)
                n = src.shape[1] * src.shape[2]
                sp.dma_start(ws[:, p % 2, 0:n], src.rearrange("p c n -> p (c n)")).then_inc(ws_in[p % 2], 16)
            sp.wait_ge(pp_full, len(head))
            stage(1)
            if kind == "gqa":
                sp.dma_start(S.X[:, :, :], S.x_dram).then_inc(x_in, 16)
            with sp.Fori(2, G) as g:
                sp.wait_ge(pp_full, g * PER + (PRO - 2 * PER + LAST_X + 1))
                stage(g)
            if kind == "decay":
                sp.wait_ge(zero_set, 1)
                with sp.Fori(0, SLOTS // (2 * P)) as i:
                    rows = S.x_slots.rearrange("(i p a) n -> i p (a n)", p=P, a=2)[bass.ds(i, 1)].rearrange("o p n -> (o p) n")
                    sp.dma_start(rows, zeros[:, :]).then_inc(slots_zero, 16)
                sp.wait_ge(slots_zero, 16 * (SLOTS // (2 * P)))

        @block.gpsimd
        def _(pool):
            pool.memset(v1[:, :, :, :], 1.0).then_inc(const_ok, 1)
            if kind == "decay":
                pool.memset(zeros[:, :], 0.0).then_inc(zero_set, 1)
            with pool.Fori(0, B // 2) as n:
                for i in range(2):
                    pool.wait_ge(ve_done, n * 2 + (i + 1))
                    pool.tensor_tensor(out=st[i].rs[:, :], in0=st[i].ve[:, :], in1=S.mhalf[:, :],
                                       op=ALU.pow).then_inc(rs_done, 1)

        @block.scalar
        def _(act):
            ac = Chain(act, act_chain)
            loads = []
            if bias:
                loads += [(bqk[:, :], w["bqk"]), (bvr[:, :], w["bv"]), (bor[:, :], w["bo"])]
            if kind == "gqa":
                loads = [(rope[:, :, :], S.rope_rows)] + loads + [(bsw[:, :], w["bqk_swapped"]), (brp[:, :, :], S.rope_cols)]
            if kind == "decay":
                loads += [(slp[:, :], w["slopes"])]
            for dst, src in loads:
                act.dma_start(dst, src).then_inc(const_in, 16)

            def split(p):
                src, hi, lo = pieces[p]
                n = src.shape[1] * src.shape[2]
                if kind == "gqa" and p < 2:
                    act.wait_ge(ws_rope, p + 1)
                else:
                    act.wait_ge(ws_in[p % 2], 16 * (p // 2 + 1))
                act.activation(flat(hi), ws[:, p % 2, 0:n], ACT.Copy).then_inc(ws_hi, 1)

            def hi_part(e, bank, k):
                what, i = e
                if what not in HI:
                    return
                act.wait_ge(pp_full, k + 1)
                dst = {"x": xgh[:, :, i * P:(i + 1) * P], "c": cgh_v, "ot": oth[:, :, :]}[what]
                act.activation(dst, four(bank), ACT.Copy).then_inc(pp_hi, 1)

            def ternary_quarter(g):
                act.dma_start(tw[:, :, :, :], S.ternary[:, :, :, bass.ds(g * P, P)]).then_inc(tw_in, 16)

            def magnitudes(g, m):
                if m == 0:
                    act.wait_ge(tw_in, g * 16 + 16)
                else:
                    act.wait_ge(tw_summed, g * 3 + m)
                act.activation(junk[:, :, :], tw[:, :, m, :], ACT.Abs,
                               accum_out=S.tern_part[:, bass.ds(g * 3 + m, 1)]).then_inc(tw_summed, 1)

            split(0)
            for k, e in enumerate(head):
                hi_part(e, pp[k % 2], k)
            split(1)
            split(2)
            if loads:
                act.wait_ge(const_in, 16 * len(loads))
            if bias:
                act.activation(boh[:, :], bor[:, :], ACT.Copy).then_inc(bias_hi, 1)
            if kind == "decay":
                ac.link(act.activation(nslp[:, :], slp[:, :], ACT.Copy, scale=-1.0))
                for r in range(4):
                    for j in range(4):
                        a = act.activation(dec[:, r, j, :], S.dist[:, :], ACT.Exp,
                                           scale=nslp[:, 4 * j + r:4 * j + r + 1])
                a.then_inc(bias_hi, 1)
            split(3)
            if kind == "gqa":
                ternary_quarter(0)

            def body(g, last):
                for i in range(STEPS):
                    if kind == "gqa" and i in (6, 10, 14):
                        magnitudes(g, (i - 6) // 4)
                    if kind == "gqa" and i == 18 and not last:
                        act.wait_ge(tw_summed, g * 3 + 3)
                        ternary_quarter(g + 1)
                    if kind == "causal" and 0 <= i - 2 < U:
                        u = i - 2
                        act.wait_ge(pt_full, g * U + (u + 1))
                        if u >= 2:
                            act.wait_ge(pv_done, g * U + (u - 1))
                        act.activation(pt[:, u % 2, :, :], four(tp[u % 2]), ACT.Copy).then_inc(pt_done, 1)
                    if soft and i < U:
                        act.wait_ge(max_done, g * U + (i + 1))
                        if i >= 2:
                            act.wait_ge(pt_full, g * U + (i - 1))
                        for j in range(4):
                            src = sm[:, i % 2, j, :] if kind == "causal" else sc[i % 2][:, j * P:(j + 1) * P]
                            a = act.activation(pr[:, i % 2, j, :], src, ACT.Exp,
                                               bias=nb[:, i % 2, j:j + 1], scale=scale)
                        a.then_inc(exp_done, 1)
                    for e, k in at_step(i, last):
                        hi_part(e, pp[k % 2], g * PER + (PRO + k))

            over_groups(act, [], [], body)

        @block.vector
        def _(dve):
            ch = Chain(dve, dve_chain)

            def rotate(p):
                dve.wait_ge(ws_in[p], 16)
                n = DM if p == 0 else P
                t0 = 0 if p == 0 else DM
                for c in range(C):
                    row = ws[:, p, c * n:(c + 1) * n]
                    dst = rt[:, 1, 0:n]
                    w2 = row.rearrange("p (h s e) -> p h s e", s=2, e=D // 2)
                    sn = rope[:, 1, t0:t0 + n].rearrange("p (h s e) -> p h s e", s=2, e=D // 2)
                    d2 = dst.rearrange("p (h s e) -> p h s e", s=2, e=D // 2)
                    for s in range(2):
                        a = dve.tensor_tensor(d2[:, :, s, :], w2[:, :, 1 - s, :], sn[:, :, s, :], ALU.mult)
                    ch.link(a)
                    ch.link(dve.tensor_tensor(rt[:, 0, 0:n], row, rope[:, 0, t0:t0 + n], ALU.mult))
                    a = dve.tensor_tensor(row, rt[:, 0, 0:n], rt[:, 1, 0:n], ALU.add)
                    if c < C - 1:
                        ch.link(a)
                a.then_inc(ws_rope, 1)
                dve.wait_ge(ws_rope, p + 1)

            def split(p):
                src, hi, lo = pieces[p]
                n = src.shape[1] * src.shape[2]
                if kind == "gqa" and p < 2:
                    rotate(p)
                dve.wait_ge(ws_hi, p + 1)
                dve.wait_ge(ws_in[p % 2], 16 * (p // 2 + 1))
                dve.tensor_tensor(flat(lo), ws[:, p % 2, 0:n], f32(flat(hi)), ALU.subtract).then_inc(ws_lo, 1)

            if loads_n:
                dve.wait_ge(const_in, 16 * loads_n)
            if kind == "gqa":
                ch.link(dve.tensor_tensor(bt[:, :], bqk[:, :], brp[:, 0, :], ALU.mult))
                ch.link(dve.tensor_tensor(bsw[:, :], bsw[:, :], brp[:, 1, :], ALU.mult))
                ch.link(dve.tensor_tensor(bqk[:, :], bsw[:, :], bt[:, :], ALU.add))

            def lo_part(e, bank, k, hi_k, g):
                what, i = e
                dve.wait_ge(pp_full, k + 1)
                if what in HI:
                    dve.wait_ge(pp_hi, hi_k + 1)
                    hi = {"x": xgh[:, :, i * P:(i + 1) * P], "c": cgh_v, "ot": oth[:, :, :]}[what]
                    lo = {"x": xgl[:, :, i * P:(i + 1) * P], "c": cgl_v, "ot": otl[:, :, :]}[what]
                    a = dve.tensor_tensor(lo, four(bank), f32(hi), ALU.subtract)
                elif what in "qk":
                    dst = (qt if what == "q" else kt)[:, i, :]
                    if bias:
                        col = i if what == "q" else 4 + i
                        a = dve.tensor_scalar(dst, bank[:, :], bqk[:, col:col + 1], None, ALU.add)
                    else:
                        a = dve.tensor_copy(dst, bank[:, :])
                elif what == "v":
                    dst = v1[:, i, :, 0:D]
                    src = bank[:, 0:vw].rearrange("p (h d) -> p h d", d=D)
                    if bias:
                        a = dve.tensor_tensor(dst, src, bvr[:, :].rearrange("p (h d) -> p h d", d=D), ALU.add)
                    else:
                        a = dve.tensor_copy(dst, src)
                else:
                    if kind == "gqa" and i == 0 and not dve_state["x"]:
                        dve.wait_ge(x_in, 16)
                    row = S.X[:, g * GT + i, :]
                    a = dve.tensor_tensor(row, row, bank[:, :], ALU.add)
                a.then_inc(pp_free, 1)
                if what == "out":
                    s = st[i % 2]
                    dve.wait_ge(pp_free, k + 1)
                    norm_stats(dve, ch, S.X[:, g * GT + i, :], s, S).then_inc(ve_done, 1)

            dve_state = {"x": False}
            n_hi = 0
            split(0)
            for k, e in enumerate(head + proj):
                if e[0] in "qkv" and e[1] == 0:
                    split("qkv".index(e[0]) + 1)
                if e == ("v", 0):
                    dve.wait_ge(const_ok, 1)
                lo_part(e, pp[k % 2], k, n_hi, 0)
                n_hi += e[0] in HI
            if bias:
                dve.wait_ge(bias_hi, 1)
                dve.tensor_tensor(bol[:, :], bor[:, :], f32(boh[:, :]), ALU.subtract).then_inc(bias_lo, 1)
            if kind == "decay":
                dve.wait_ge(bias_hi, 2)
                for r in range(4):
                    a = dve.tensor_tensor(dec[:, r, :, :], dec[:, r, :, :], S.upper4, ALU.mult)
                ch.link(a)

            def normalize(b, g):
                s = st[b % 2]
                row = S.X[:, g * GT + b, :]
                dve.wait_ge(rs_done, g * GT + (b + 1))
                dve.tensor_scalar(row, row, s.mv[:, 0:1], s.rs[:, 0:1], ALU.subtract, ALU.mult)

            def body(g, last):
                for i in range(STEPS):
                    if i < U:
                        dve.wait_ge(sc_full, g * U + (i + 1))
                        if soft:
                            if i >= 2:
                                dve.wait_ge(exp_done, g * U + (i - 1))
                            src = four(sc[i % 2])
                            if kind == "causal":
                                ch.link(dve.tensor_tensor(sm[:, i % 2, :, :], src, S.causal4, ALU.add))
                                src = sm[:, i % 2, :, :]
                            ch.link(dve.tensor_reduce(nm[:, i % 2, :], src, AX, ALU.max))
                            dve.tensor_scalar(nb[:, i % 2, :], nm[:, i % 2, :], -scale, None,
                                              ALU.mult).then_inc(max_done, 1)
                        else:
                            if i >= 2:
                                dve.wait_ge(pv_done, g * U + (i - 1))
                            dve.tensor_tensor(pt[:, i % 2, :, :], four(sc[i % 2]), dec[:, i % 4, :, :],
                                              ALU.mult).then_inc(pt_done, 1)
                    if kind == "gqa" and 0 <= i - 2 < U:
                        u = i - 2
                        dve.wait_ge(pt_full, g * U + (u + 1))
                        if u >= 2:
                            dve.wait_ge(pv_done, g * U + (u - 1))
                        dve.tensor_tensor(pt[:, u % 2, :, :], four(tp[u % 2]), S.lower4, ALU.mult).then_inc(pt_done, 1)
                    u = i - LAG
                    if 0 <= u < U and u % 4 == 3:
                        b = u // 4
                        dve.wait_ge(pv_done, g * U + (u + 1))
                        if soft:
                            for q in range(2):
                                o = ob[q][:, 0:8 * OW].rearrange("p (h e) -> p h e", e=OW)
                                a = dve.reciprocal(rec[:, 8 * q:8 * q + 8], o[:, :, D])
                            ch.link(a)
                        for q in range(2):
                            dst = on[:, b % 2, 8 * D * q:8 * D * (q + 1)].rearrange("p (h d) -> p h d", d=D)
                            o = ob[q][:, 0:8 * OW].rearrange("p (h e) -> p h e", e=OW)[:, :, 0:D]
                            if soft:
                                r8 = rec[:, 8 * q:8 * q + 8].unsqueeze(2).broadcast_to((P, 8, D))
                                a = dve.tensor_tensor(dst, o, r8, ALU.mult)
                            else:
                                a = dve.tensor_copy(dst, o)
                        a.then_inc(o_norm, 1)
                    for e, k in at_step(i, last):
                        if e[0] == "out" and e[1] > 0:
                            normalize(e[1] - 1, g)
                        lo_part(e, pp[k % 2], g * PER + (PRO + k), g * PER_HI + (PRO_HI + his_before(k, last)), g)
                normalize(GT - 1, g)

            per = GT * 2 + (U * (2 if kind == "causal" else 1) + GT if soft else 0)
            if kind == "gqa":
                dve.wait_ge(x_in, 16)
            over_groups(dve, [ch], [per], body)

        @block.tensor
        def _(pe):
            def pp_stage(e, bank, k, heads_free, g):
                what, i = e
                first = isinstance(g, int) and g == 0
                if what == "x":
                    staged = FIRST_STAGED or not first
                    if staged:
                        pe.wait_ge(xs_in, g * (32 if kind == "causal" else 16) + (0 if kind == "decay" else 16))
                    src = xs if staged else S.X
                    for c in range(C):
                        m = pe.transpose(bank[:, c * P:(c + 1) * P], src[:, i, c * P:(c + 1) * P], S.ident[:, :])
                elif what == "c":
                    if first:
                        pe.wait_ge(xs_in, 16)
                    for t in range(GT):
                        m = pe.transpose(bank[:, t * P:(t + 1) * P], cs[:, t, :], S.ident[:, :])
                elif what in "qk":
                    if i == 0:
                        pe.wait_ge(pp_free, heads_free)
                        if isinstance(g, int) and g == 0:
                            pe.wait_ge(ws_lo, 1 if what == "q" else 2)
                    wh, wl = (wqh, wql) if what == "q" else (wkh, wkl)
                    src = [(cgh[:, :], cgl[:, :])] if what == "k" and kind == "causal" else \
                        [(xgh[:, c, :], xgl[:, c, :]) for c in range(C)]
                    cols = slice(i * P, (i + 1) * P)
                    for c, (xh, xl) in enumerate(src):
                        m = products(pe, bank[:, :], wh[:, c, cols], wl[:, c, cols], xh, xl,
                                     c == 0, c == len(src) - 1)
                elif what == "v":
                    if i == 0 and isinstance(g, int) and g == 0:
                        pe.wait_ge(ws_lo, 3)
                    cols = slice(i * P, (i + 1) * P)
                    src = [(cgh[:, cols], cgl[:, cols])] if kind == "causal" else \
                        [(xgh[:, c, cols], xgl[:, c, cols]) for c in range(C)]
                    for c, (xh, xl) in enumerate(src):
                        m = products(pe, bank[:, 0:vw], xh, xl, wvh[:, c, :], wvl[:, c, :],
                                     c == 0, c == len(src) - 1)
                elif what == "ot":
                    pe.wait_ge(o_norm, g * GT + (i + 1))
                    for c in range(C):
                        m = pe.transpose(bank[:, c * P:(c + 1) * P], on[:, i % 2, c * P:(c + 1) * P], S.ident[:, :])
                else:
                    pe.wait_ge(pp_free, heads_free)
                    for c in range(C):
                        m = products(pe, bank[:, :], oth[:, c, :], otl[:, c, :], woh[:, c, :], wol[:, c, :],
                                     c == 0, c == C - 1 and not bias)
                    if bias:
                        pe.matmul(bank[:, :], S.ones[:, :], boh[:, :], start=False, stop=False)
                        m = pe.matmul(bank[:, :], S.ones[:, :], bol[:, :], start=False, stop=True)
                m.then_inc(pp_full, 1)

            for k, e in enumerate(head + proj):
                if k >= 2:
                    pe.wait_ge(pp_free, k - 1)
                pp_stage(e, pp[k % 2], k, len(head), 0)
            pe.wait_ge(ws_lo, 4)
            if bias:
                pe.wait_ge(bias_lo, 1)

            def body(g, last):
                base = g * PER + PRO
                x_free = g * PER + (PRO + LAST_X + 1)
                uses = {e: k for _, e, k in stages(last)}
                for i in range(STEPS):
                    if i < U:
                        if i == 0:
                            pe.wait_ge(pp_free, base)
                        else:
                            pass
                        if i >= 2:
                            pe.wait_ge({"gqa": exp_done, "causal": max_done, "decay": pt_done}[kind], g * U + (i - 1))
                        tok = slice((i // 4) * P, (i // 4 + 1) * P)
                        for j, jq, jk, rows, h, hv in heads_of(i):
                            q, k = qt[rows, jq, tok], kt[rows, jk, tok]
                            a, b = (q, k) if soft else (k, q)
                            m = pe.matmul(sc[i % 2][:, j * P:(j + 1) * P], a, b, start=True, stop=True)
                        m.then_inc(sc_full, 1)
                    u = i - 2
                    if soft and 0 <= u < U:
                        pe.wait_ge(exp_done, g * U + (u + 1))
                        if u >= 2:
                            pe.wait_ge(pt_done, g * U + (u - 1))
                        for j in range(4):
                            m = pe.transpose(tp[u % 2][:, j * P:(j + 1) * P], pr[:, u % 2, j, :], S.ident[:, :])
                        m.then_inc(pt_full, 1)
                    u = i - LAG
                    if 0 <= u < U:
                        pe.wait_ge(pt_done, g * U + (u + 1))
                        if u % 4 == 0 and u:
                            pe.wait_ge(o_norm, g * GT + u // 4)
                        for j, _, _, _, h, hv in heads_of(u):
                            n = OW if soft else D
                            m = pe.matmul(ob[h // 8][:, (h % 8) * OW:(h % 8) * OW + n], pt[:, u % 2, j, :],
                                          v1[:, u // 4, hv, 0:n], start=True, stop=True)
                        m.then_inc(pv_done, 1)
                    for e, k in at_step(i, last):
                        pe.wait_ge(pp_free, base + max(k - 1, 0))
                        nx = e in head or e in proj
                        need = x_free if nx else base + (uses[("ot", e[1])] + 1)
                        pp_stage(e, pp[k % 2], base + k, need, g + 1 if nx else g)

            over_groups(pe, [], [], body)

        blocks.close()


def latent_phase(nc, S, w, half):
    HH = XH // 2
    T = HH // 2
    U = 2 * GT
    CB = DM + 3 * P + 3 * XR + P + DM
    name = f"latent{half}"
    with Phase(nc, name) as phase:
        sb, sem = phase.sb, phase.sem

        fold = sb("fold", [P, 2, CB])
        fm = sb("fm", [P, 2, XR])
        ch_, cl_ = sb("ch", [P, C, HH * XR], F32R), sb("cl", [P, C, HH * XR], F32R)
        vh, vl = sb("vh", [P, HH, DM], F32R), sb("vl", [P, HH, DM], F32R)
        kr = sb("kr", [P, HH * XR])
        krh, krl = sb("krh", [P, HH * XR], F32R), sb("krl", [P, HH * XR], F32R)
        kv = sb("kv", [P, B, P])
        kvr = sb("kvr", [P, 2, P])
        kvh, kvl = sb("kvh", [P, B * P], F32R), sb("kvl", [P, B * P], F32R)
        kvs = sb("kvs", [P, GT, P])
        xs = sb("xs", [P, GT, DM])
        xgh, xgl = sb("xgh", [P, C, N], F32R), sb("xgl", [P, C, N], F32R)
        qt, kt = sb("qt", [P, T, N]), sb("kt", [P, T, N])
        pr, pt = sb("pr", [P, 2, 4, P]), sb("pt", [P, 2, 4, P])
        nm, nb = sb("nm", [P, 2, 4]), sb("nb", [P, 2, 4])
        sums, rec = sb("sums", [P, 2, 4]), sb("rec", [P, 2, 4])
        cth, ctl = sb("cth", [P, 2, 2, N], F32R), sb("ctl", [P, 2, 2, N], F32R)
        st = [Stats(sb, i) for i in range(2)]
        t1 = fold[:, :, 0:8 * P].rearrange("p a (b n) -> p a b n", n=P)
        t2 = xs[:, :, :].rearrange("p (a q) (b n) -> p a (q b) n", a=2, n=P)
        kv4 = kv[:, :, :].rearrange("p (a b) n -> p a b n", a=2)
        pp, sc, tp, cb = S.bank[0:2], S.bank[2:4], S.bank[4:6], S.bank[6:8]

        x_src = S.X[:, :, :] if half == 0 else S.x_kept
        x_kept, kv_in, kr_in, kv_rot = sem("x_kept"), sem("kv_in"), sem("kr_in"), sem("kv_rot")
        kvt_full, kvt_hi, kvt_lo = sem("kvt_full"), sem("kvt_hi"), sem("kvt_lo")
        kr_hi, kr_lo = sem("kr_hi"), sem("kr_lo")
        fold_in = [sem(f"fold_in{i}") for i in range(2)]
        fm_full, fm_done = sem("fm_full"), sem("fm_done")
        c_full, c_hi, c_lo = sem("c_full"), sem("c_hi"), sem("c_lo")
        v_full, v_hi, v_lo = sem("v_full"), sem("v_hi"), sem("v_lo")
        xs_in, kvs_in = sem("xs_in"), sem("kvs_in")
        pp_full, pp_hi, pp_free = sem("pp_full"), sem("pp_hi"), sem("pp_free")
        sc_full, max_done, exp_done, p_norm = sem("sc_full"), sem("max_done"), sem("exp_done"), sem("p_norm")
        pt_full, pt_done = sem("pt_full"), sem("pt_done")
        ct_full, ct_hi, ct_lo = sem("ct_full"), sem("ct_hi"), sem("ct_lo")
        ve_done, rs_done, dve_chain = sem("ve_done"), sem("rs_done"), sem("dve_chain")

        def folded(s):
            r, at = fold[:, s, :], 0
            out = []
            for n in (DM, 3 * P, 3 * XR, P, DM):
                out.append(r[:, at:at + n])
                at += n
            return out

        head = [("x", i) for i in range(GT)]
        proj = [(q, j) for j in range(T) for q in "qk"]
        STEPS = U + 6
        own = {i: [] for i in range(STEPS)}
        nxt = {i: [] for i in range(STEPS)}
        for b in range(GT):
            own[2 * b + 6].append(("out", b))
        for n, e in enumerate(head):
            nxt[1 + n].append(e)
        for n, e in enumerate(proj):
            nxt[8 + n // 2].append(e)

        def stages(last):
            out, k = [], 0
            for i in range(STEPS):
                for e in ([] if last else nxt[i]) + own[i]:
                    out.append((i, e, k))
                    k += 1
            return out

        def at_step(i, last):
            return [(e, k) for j, e, k in stages(last) if j == i]

        PRO = len(head) + len(proj)
        PER = PRO + GT
        LAST_X = max(k for _, e, k in stages(False) if e in head)

        def his_before(k, last):
            return sum(e[0] == "x" for _, e, n in stages(last) if n < k)

        blocks = ExitStack()
        block = blocks.enter_context(nc.Block())

        @block.sync
        def _(sp):
            sp.dma_start(kv[:, :, :], S.ctx_dram).then_inc(kv_in, 16)
            sp.dma_start(kvr[:, :, :], S.kv_rope).then_inc(kv_in, 16)
            sp.dma_start(kr[:, :], w["kr"][:, half * HH * XR:(half + 1) * HH * XR]).then_inc(kr_in, 16)
            sp.wait_ge(kv_rot, 1)
            sp.dma_start(xs[:, :, :], x_src[:, 0:GT, :]).then_inc(xs_in, 16)
            sp.dma_start(kvs[:, :, :], kv[:, 0:GT, :]).then_inc(kvs_in, 16)
            for s in range(2):
                sp.dma_start(fold[:, s, :], w["fold"][half * HH + s]).then_inc(fold_in[s], 16)
            with sp.Fori(1, HH // 2) as n:
                for s in range(2):
                    sp.wait_ge(v_full, n * 2 + (s - 1))
                    src = w["fold"][bass.ds(n * 2 + (half * HH + s), 1)].rearrange("a p n -> (a p) n")
                    sp.dma_start(fold[:, s, :], src).then_inc(fold_in[s], 16)
            if half == 0:
                sp.dma_start(S.x_kept, S.X[:, :, :]).then_inc(x_kept, 16)
            sp.wait_ge(pp_full, len(head))
            sp.dma_start(xs[:, :, :], x_src[:, GT:2 * GT, :]).then_inc(xs_in, 16)

            def latents(g):
                sp.wait_ge(ct_full, g * U)
                sp.dma_start(kvs[:, :, :], kv[:, bass.ds(g * GT, GT), :]).then_inc(kvs_in, 16)

            with sp.Fori(0, G - 2) as g:
                sp.wait_ge(pp_full, g * PER + (PRO + LAST_X + 1))
                sp.dma_start(xs[:, :, :], x_src[:, bass.ds((g + 2) * GT, GT), :]).then_inc(xs_in, 16)
                latents(g + 1)
            latents(G - 1)

        @block.gpsimd
        def _(pool):
            if half == 1:
                with pool.Fori(0, B // 2) as n:
                    for i in range(2):
                        pool.wait_ge(ve_done, n * 2 + (i + 1))
                        pool.tensor_tensor(out=st[i].rs[:, :], in0=st[i].ve[:, :], in1=S.mhalf[:, :],
                                           op=ALU.pow).then_inc(rs_done, 1)

        @block.scalar
        def _(act):
            act.wait_ge(kr_in, 16)
            act.activation(krh[:, :], kr[:, :], ACT.Copy).then_inc(kr_hi, 1)
            for q in range(G):
                act.wait_ge(kvt_full, q + 1)
                act.activation(kvh[:, q * N:(q + 1) * N], pp[q % 2][:, :], ACT.Copy).then_inc(kvt_hi, 1)
            with act.Fori(0, HH // 2) as n:
                for s in range(2):
                    act.wait_ge(fm_full, n * 2 + (s + 1))
                    act.activation(fm[:, s, :], sc[s][:, 0:XR], ACT.Copy).then_inc(fm_done, 1)
                    act.wait_ge(v_full, n * 2 + (s + 1))
                    act.activation(vh[:, bass.ds(n * 2 + s, 1), :], cb[s][:, :].unsqueeze(1),
                                   ACT.Copy).then_inc(v_hi, 1)
                    act.wait_ge(c_full, n * 2 + (s + 1))
                    act.activation(ch_[:, :, bass.ds(n * (2 * XR) + s * XR, XR)],
                                   tp[s][:, 0:C * XR].rearrange("p (c r) -> p c r", r=XR), ACT.Copy).then_inc(c_hi, 1)

            def hi_part(e, bank, k):
                if e[0] == "x":
                    act.wait_ge(pp_full, k + 1)
                    act.activation(xgh[:, :, e[1] * P:(e[1] + 1) * P], four(bank), ACT.Copy).then_inc(pp_hi, 1)

            for k, e in enumerate(head + proj):
                hi_part(e, pp[k % 2], k)

            def body(g, last):
                for i in range(STEPS):
                    u = i - 2
                    if 0 <= u < U:
                        act.wait_ge(pt_full, g * U + (u + 1))
                        if u >= 2:
                            act.wait_ge(ct_full, g * U + (u - 1))
                        act.activation(pt[:, u % 2, :, :], four(tp[u % 2]), ACT.Copy).then_inc(pt_done, 1)
                    if i < U:
                        act.wait_ge(max_done, g * U + (i + 1))
                        if i >= 2:
                            act.wait_ge(pt_full, g * U + (i - 1))
                        for j in range(4):
                            a = act.activation(pr[:, i % 2, j, :], sc[i % 2][:, j * P:(j + 1) * P], ACT.Exp,
                                               bias=nb[:, i % 2, j:j + 1], accum_out=sums[:, i % 2, j:j + 1])
                        a.then_inc(exp_done, 1)
                    u = i - 3
                    if 0 <= u < U:
                        act.wait_ge(ct_full, g * U + (u + 1))
                        act.activation(cth[:, u // 2 % 2, u % 2, :], cb[u % 2][:, :], ACT.Copy).then_inc(ct_hi, 1)
                    for e, k in at_step(i, last):
                        hi_part(e, pp[k % 2], g * PER + (PRO + k))

            over_groups(act, [], [], body)

        @block.vector
        def _(dve):
            ch = Chain(dve, dve_chain)
            dve.wait_ge(kv_in, 32)
            half_of = lambda t, s: t[:, :, :, s * (P // 2):(s + 1) * (P // 2)]
            for s in range(2):
                sn = kvr[:, 1, s * (P // 2):(s + 1) * (P // 2)].unsqueeze(1).unsqueeze(1)
                a = dve.tensor_tensor(half_of(t1, s), half_of(kv4, 1 - s), sn.broadcast_to((P, 2, 8, P // 2)), ALU.mult)
            ch.link(a)
            cs = kvr[:, 0, :].unsqueeze(1).unsqueeze(1).broadcast_to((P, 2, 8, P))
            ch.link(dve.tensor_tensor(t2, kv4, cs, ALU.mult))
            dve.tensor_tensor(kv4, t1, t2, ALU.add).then_inc(kv_rot, 1)
            dve.wait_ge(kr_hi, 1)
            dve.tensor_tensor(krl[:, :], kr[:, :], f32(krh[:, :]), ALU.subtract).then_inc(kr_lo, 1)
            for q in range(G):
                dve.wait_ge(kvt_hi, q + 1)
                cols = slice(q * N, (q + 1) * N)
                dve.tensor_tensor(kvl[:, cols], pp[q % 2][:, :], f32(kvh[:, cols]), ALU.subtract).then_inc(kvt_lo, 1)
            with dve.Fori(0, HH // 2) as n:
                for s in range(2):
                    dve.wait_ge(v_hi, n * 2 + (s + 1))
                    dve.tensor_tensor(vl[:, bass.ds(n * 2 + s, 1), :], cb[s][:, :].unsqueeze(1),
                                      f32(vh[:, bass.ds(n * 2 + s, 1), :]), ALU.subtract).then_inc(v_lo, 1)
                    dve.wait_ge(c_hi, n * 2 + (s + 1))
                    cols = bass.ds(n * (2 * XR) + s * XR, XR)
                    dve.tensor_tensor(cl_[:, :, cols], tp[s][:, 0:C * XR].rearrange("p (c r) -> p c r", r=XR),
                                      f32(ch_[:, :, cols]), ALU.subtract).then_inc(c_lo, 1)

            def lo_part(e, bank, k, hi_k, g):
                what, i = e
                dve.wait_ge(pp_full, k + 1)
                if what == "x":
                    dve.wait_ge(pp_hi, hi_k + 1)
                    cols = slice(i * P, (i + 1) * P)
                    a = dve.tensor_tensor(xgl[:, :, cols], four(bank), f32(xgh[:, :, cols]), ALU.subtract)
                elif what in "qk":
                    a = dve.tensor_copy((qt if what == "q" else kt)[:, i, :], bank[:, :])
                else:
                    row = S.X[:, g * GT + i, :]
                    a = dve.tensor_tensor(row, row, bank[:, :], ALU.add)
                a.then_inc(pp_free, 1)
                if what == "out" and half == 1:
                    dve.wait_ge(pp_free, k + 1)
                    norm_stats(dve, ch, S.X[:, g * GT + i, :], st[i % 2], S).then_inc(ve_done, 1)

            n_hi = 0
            for k, e in enumerate(head + proj):
                lo_part(e, pp[k % 2], k, n_hi, 0)
                n_hi += e[0] == "x"

            def normalize(b, g):
                s = st[b % 2]
                row = S.X[:, g * GT + b, :]
                dve.wait_ge(rs_done, g * GT + (b + 1))
                dve.tensor_scalar(row, row, s.mv[:, 0:1], s.rs[:, 0:1], ALU.subtract, ALU.mult)

            def body(g, last):
                for i in range(STEPS):
                    if i < U:
                        dve.wait_ge(sc_full, g * U + (i + 1))
                        ch.link(dve.tensor_reduce(nm[:, i % 2, :], four(sc[i % 2]), AX, ALU.max))
                        dve.tensor_scalar(nb[:, i % 2, :], nm[:, i % 2, :], -1.0, None, ALU.mult).then_inc(max_done, 1)
                    u = i - 1
                    if 0 <= u < U:
                        dve.wait_ge(exp_done, g * U + (u + 1))
                        ch.link(dve.reciprocal(rec[:, u % 2, :], sums[:, u % 2, :]))
                        for j in range(4):
                            row = pr[:, u % 2, j, :]
                            a = dve.tensor_scalar(row, row, rec[:, u % 2, j:j + 1], None, ALU.mult)
                        a.then_inc(p_norm, 1)
                    u = i - 3
                    if 0 <= u < U:
                        dve.wait_ge(ct_hi, g * U + (u + 1))
                        dve.tensor_tensor(ctl[:, u // 2 % 2, u % 2, :], cb[u % 2][:, :],
                                          f32(cth[:, u // 2 % 2, u % 2, :]), ALU.subtract).then_inc(ct_lo, 1)
                    for e, k in at_step(i, last):
                        if e[0] == "out" and e[1] > 0 and half == 1:
                            normalize(e[1] - 1, g)
                        lo_part(e, pp[k % 2], g * PER + (PRO + k), g * len(head) + (len(head) + his_before(k, last)), g)
                if half == 1:
                    normalize(GT - 1, g)

            if half == 0:
                dve.wait_ge(x_kept, 16)
            over_groups(dve, [ch], [2 * U + 2 * GT * half], body)

        @block.tensor
        def _(pe):
            pe.wait_ge(kv_rot, 1)
            for q in range(G):
                if q >= 2:
                    pe.wait_ge(kvt_lo, q - 1)
                for t in range(GT):
                    m = pe.transpose(pp[q % 2][:, t * P:(t + 1) * P], kv[:, GT * q + t, :], S.ident[:, :])
                m.then_inc(kvt_full, 1)

            def fold_head(n, s, first):
                wq, kcq, wqr, kckv, wo = folded(s)
                pe.wait_ge(fold_in[s], (n + 1) * 16)
                for c in range(3):
                    m = pe.matmul(sc[s][:, 0:XR], kcq[:, c * P:(c + 1) * P], wqr[:, c * XR:(c + 1) * XR],
                                  start=c == 0, stop=c == 2)
                m.then_inc(fm_full, 1)
                pe.wait_ge(fm_done, n * 2 + (s + 1))
                if not first:
                    pe.wait_ge(c_lo, n * 2 + (s - 1))
                for c in range(C):
                    m = pe.matmul(tp[s][:, c * XR:(c + 1) * XR], wq[:, c * P:(c + 1) * P], fm[:, s, :],
                                  start=True, stop=True)
                m.then_inc(c_full, 1)
                pe.matmul(cb[s][:, :], kckv, wo, start=True, stop=True).then_inc(v_full, 1)

            for s in range(2):
                fold_head(0, s, True)
            with pe.Fori(1, HH // 2) as n:
                for s in range(2):
                    fold_head(n, s, False)

            def pp_stage(e, bank, k, need, g):
                what, i = e
                if what == "x":
                    pe.wait_ge(xs_in, (g + 1) * 16)
                    for c in range(C):
                        m = pe.transpose(bank[:, c * P:(c + 1) * P], xs[:, i, c * P:(c + 1) * P], S.ident[:, :])
                elif what == "q":
                    if i == 0:
                        pe.wait_ge(pp_free, need)
                    cols = slice(i * P, (i + 1) * P)
                    for c in range(C):
                        m = products(pe, bank[:, :], ch_[:, c, cols], cl_[:, c, cols], xgh[:, c, :], xgl[:, c, :],
                                     c == 0, c == C - 1)
                elif what == "k":
                    cols = slice(i * P, (i + 1) * P)
                    toks = bass.ds(g * N, N)
                    m = products(pe, bank[:, :], krh[:, cols], krl[:, cols], kvh[:, toks], kvl[:, toks], True, True)
                else:
                    pe.wait_ge(ct_lo, need)
                    for u in range(2):
                        for j in range(4):
                            cols = slice(j * P, (j + 1) * P)
                            h = 2 * j + u
                            m = products(pe, bank[:, :], cth[:, i % 2, u, cols], ctl[:, i % 2, u, cols],
                                         vh[:, h, :], vl[:, h, :], u == 0 and j == 0, u == 1 and j == 3)
                m.then_inc(pp_full, 1)

            pe.wait_ge(kvt_lo, G)
            for k, e in enumerate(head + proj):
                if k >= 2:
                    pe.wait_ge(pp_free, k - 1)
                if k == len(head):
                    pe.wait_ge(c_lo, HH)
                    pe.wait_ge(kr_lo, 1)
                pp_stage(e, pp[k % 2], k, len(head), 0)
            pe.wait_ge(v_lo, HH)

            def body(g, last):
                base = g * PER + PRO
                for i in range(STEPS):
                    if i < U:
                        if i == 0:
                            pe.wait_ge(pp_free, base)
                        if i >= 2:
                            pe.wait_ge(exp_done, g * U + (i - 1))
                        tok = slice((i // 2) * P, (i // 2 + 1) * P)
                        rows = slice(XR * (i % 2), XR * (i % 2 + 1))
                        for j in range(4):
                            m = pe.matmul(sc[i % 2][:, j * P:(j + 1) * P], qt[rows, j, tok], kt[rows, j, tok],
                                          start=True, stop=True)
                        m.then_inc(sc_full, 1)
                    u = i - 2
                    if 0 <= u < U:
                        pe.wait_ge(p_norm, g * U + (u + 1))
                        if u >= 2:
                            pe.wait_ge(pt_done, g * U + (u - 1))
                        for j in range(4):
                            m = pe.transpose(tp[u % 2][:, j * P:(j + 1) * P], pr[:, u % 2, j, :], S.ident[:, :])
                        m.then_inc(pt_full, 1)
                    u = i - 3
                    if 0 <= u < U:
                        if u == 0:
                            pe.wait_ge(kvs_in, (g + 1) * 16)
                        pe.wait_ge(pt_done, g * U + (u + 1))
                        if u >= 2:
                            pe.wait_ge(ct_lo, g * U + (u - 1))
                        pe.matmul(cb[u % 2][:, :], kvs[:, u // 2, :],
                                  pt[:, u % 2, :, :].rearrange("p j t -> p (j t)"),
                                  start=True, stop=True).then_inc(ct_full, 1)
                    for e, k in at_step(i, last):
                        pe.wait_ge(pp_free, base + max(k - 1, 0))
                        if e[0] == "out":
                            pp_stage(e, pp[k % 2], base + k, g * U + (2 * e[1] + 2), g)
                        else:
                            pp_stage(e, pp[k % 2], base + k, base + (LAST_X + 1), g + 1)

            over_groups(pe, [], [], body)

        blocks.close()


def ternary_ffn_phase(nc, S, w):
    J = NF0
    with Phase(nc, "ternary") as phase:
        sb, sem = phase.sb, phase.sem

        xth, xtl = sb("xth", [P, C, B * P], F32R), sb("xtl", [P, C, B * P], F32R)
        RB = 3
        raw = sb("raw", [P, RB, 3, DM])
        wq = sb("wq", [P, J, 3, DM], F32R)
        below = sb("below", [P, 3, DM])
        tot, thr = sb("tot", [P, 3]), sb("thr", [P, 3, 2])
        sg, hf = sb("sg", [P, 2, N]), sb("hf", [P, 2, N])
        hh, hl = sb("hh", [P, 2, N], F32R), sb("hl", [P, 2, N], F32R)
        st = [Stats(sb, i) for i in range(GT)]
        gate, up, yb = S.bank[0:2], S.bank[2:4], S.bank[4:8]

        raw_in = [sem(f"raw_in{b}") for b in range(RB)]
        summed, total, thr_done = sem("summed"), sem("total"), sem("thr_done")
        below_done, quant = sem("below_done"), sem("quant")
        gate_full, up_full, sig_done = sem("gate_full"), sem("up_full"), sem("sig_done")
        hf_done, hh_done, hl_done = sem("hf_done"), sem("hh_done"), sem("hl_done")
        down_done, y_free = sem("down_done"), sem("y_free")
        ve_done, rs_done, dve_chain = sem("ve_done"), sem("rs_done"), sem("dve_chain")

        blocks = ExitStack()
        block = blocks.enter_context(nc.Block())
        xt = Transposer(S, xth, xtl, sem)

        def over_tokens(eng, body):
            body(0, True)
            with eng.Fori(1, G) as g:
                body(g, False)

        @block.sync
        def _(sp):
            for j in range(J):
                if j >= RB:
                    sp.wait_ge(quant, 3 * (j - RB + 1))
                sp.dma_start(raw[:, j % RB, :, :], S.ternary[:, j, :, :]).then_inc(raw_in[j % RB], 16)

        @block.gpsimd
        def _(pool):
            pool.wait_ge(thr_done, 6)
            for j in range(J):
                pool.wait_ge(raw_in[j % RB], 16 * (j // RB + 1))
                for m in range(3):
                    if j:
                        pool.wait_ge(quant, 3 * (j - 1) + m + 1)
                    pool.tensor_scalar(below[:, m, :], raw[:, j % RB, m, :], thr[:, m, 1:2], None,
                                       ALU.is_lt).then_inc(below_done, 1)
            with pool.Fori(0, G) as g:
                for i in range(GT):
                    pool.wait_ge(ve_done, g * GT + (i + 1))
                    pool.tensor_tensor(out=st[i].rs[:, :], in0=st[i].ve[:, :], in1=S.mhalf[:, :],
                                       op=ALU.pow).then_inc(rs_done, 1)

        @block.scalar
        def _(act):
            for t in range(B):
                xt.on_act(act, t)

            def body(g, first):
                for j in range(J + 1):
                    if j < J:
                        act.wait_ge(gate_full, g * J + (j + 1))
                        if j >= 2:
                            act.wait_ge(hf_done, g * J + (j - 1))
                        act.activation(sg[:, j % 2, :], gate[j % 2][:, :], ACT.Sigmoid).then_inc(sig_done, 1)
                    if j >= 1:
                        act.wait_ge(hf_done, g * J + j)
                        if j >= 3:
                            act.wait_ge(down_done, g * (J * GT) + (j - 2) * GT)
                        act.activation(hh[:, (j - 1) % 2, :], hf[:, (j - 1) % 2, :], ACT.Copy).then_inc(hh_done, 1)

            over_tokens(act, body)

        @block.vector
        def _(dve):
            ch = Chain(dve, dve_chain)
            dve.tensor_reduce(tot[:, :], S.tern_part[:, :].rearrange("p (g m) -> p m g", m=3), AX,
                              ALU.add).then_inc(summed, 1)
            dve.wait_ge(total, 1)
            for m in range(3):
                for s in range(2):
                    sign = 0.5 if s == 0 else -0.5
                    dve.tensor_scalar(thr[:, m, s:s + 1], yb[0][:, m:m + 1], sign / (F0 * DM), sign * 1e-8,
                                      ALU.mult, ALU.add).then_inc(thr_done, 1)
            dve.wait_ge(thr_done, 6)

            def compare(j):
                for m in range(3):
                    dve.wait_ge(below_done, 3 * j + m + 1)
                    dve.scalar_tensor_tensor(out=wq[:, j, m, :], in0=raw[:, j % RB, m, :], scalar=thr[:, m, 0:1],
                                             in1=below[:, m, :], op0=ALU.is_gt, op1=ALU.subtract).then_inc(quant, 1)

            for t in range(B):
                xt.on_dve(dve, t)
                if t in (B // 2, B - 1):
                    compare(0 if t < B - 1 else 1)

            def stats(g, i):
                norm_stats(dve, ch, S.X[:, g * GT + i, :], st[i], S).then_inc(ve_done, 1)

            def normalize(g, i):
                row = S.X[:, g * GT + i, :]
                dve.wait_ge(rs_done, g * GT + (i + 1))
                dve.tensor_scalar(row, row, st[i].mv[:, 0:1], st[i].rs[:, 0:1], ALU.subtract, ALU.mult)

            def body(g, first):
                if not first:
                    ch.turn(0, g - 1, 2 * GT)
                for j in range(J + 1):
                    if j < J:
                        dve.wait_ge(sig_done, g * J + (j + 1))
                        dve.wait_ge(up_full, g * J + (j + 1))
                        if j >= 2:
                            dve.wait_ge(hh_done, g * J + (j - 1))
                        dve.tensor_tensor(hf[:, j % 2, :], sg[:, j % 2, :], up[j % 2][:, :], ALU.mult).then_inc(hf_done, 1)
                    if j >= 1:
                        q = (j - 1) % 2
                        dve.wait_ge(hh_done, g * J + j)
                        dve.tensor_tensor(hl[:, q, :], hf[:, q, :], f32(hh[:, q, :]), ALU.subtract).then_inc(hl_done, 1)
                    if first and j + 2 < J:
                        compare(j + 2)
                    if not first and 1 <= j <= GT:
                        stats(g - 1, j - 1)
                    if not first and GT < j <= 2 * GT:
                        normalize(g - 1, j - GT - 1)
                for i in range(GT):
                    row = S.X[:, g * GT + i, :]
                    dve.wait_ge(down_done, g * (J * GT) + ((J - 1) * GT + i + 1))
                    dve.tensor_tensor(row, row, yb[i][:, :], ALU.add).then_inc(y_free, 1)
                dve.wait_ge(y_free, g * GT + GT)

            over_tokens(dve, body)
            ch.turn(0, G - 1, 2 * GT)
            for i in range(GT):
                stats(G - 1, i)
            for i in range(GT):
                normalize(G - 1, i)

        @block.tensor
        def _(pe):
            pe.wait_ge(summed, 1)
            pe.matmul(yb[0][:, 0:3], S.ones_f[:, :], tot[:, :], start=True, stop=True).then_inc(total, 1)
            xt.on_pe(pe)
            pe.wait_ge(xt.lo, B)
            pe.wait_ge(thr_done, 6)

            def body(g, first):
                toks = bass.ds(g * N, N)

                def ups(dst, m, j):
                    if first:
                        pe.wait_ge(quant, 3 * j + m + 1)
                    for c in range(C):
                        for n, x in enumerate((xth, xtl)):
                            a = pe.matmul(dst[:, :], wq[:, j, m, c * P:(c + 1) * P], x[:, c, toks],
                                          start=c == 0 and n == 0, stop=c == C - 1 and n == 1)
                    return a

                def down(j):
                    pe.wait_ge(hl_done, g * J + (j + 1))
                    if first:
                        pe.wait_ge(quant, 3 * j + 3)
                    for i in range(GT):
                        for n, h in enumerate((hh, hl)):
                            a = pe.matmul(yb[i][:, :], h[:, j % 2, i * P:(i + 1) * P], wq[:, j, 2, :],
                                          start=j == 0 and n == 0, stop=j == J - 1 and n == 1)
                        a.then_inc(down_done, 1)

                for j in range(J):
                    if j >= 2:
                        pe.wait_ge(sig_done, g * J + (j - 1))
                    ups(gate[j % 2], 0, j).then_inc(gate_full, 1)
                    if j >= 2:
                        pe.wait_ge(hf_done, g * J + (j - 1))
                    if j >= 2:
                        down(j - 2)
                    ups(up[j % 2], 1, j).then_inc(up_full, 1)
                down(J - 2)
                down(J - 1)

            over_tokens(pe, body)

        blocks.close()


def shared_ffn_phase(nc, S, w):
    WU, WD = 2 * F1 * C, len(FT) * DM
    WE = WU + WD
    J = len(FT)
    Q = 2 * J
    with Phase(nc, "shared") as phase:
        sb, sem = phase.sb, phase.sem

        xth, xtl = sb("xth", [P, C, B * P], F32R), sb("xtl", [P, C, B * P], F32R)
        raw, weh, wel = S.raw, S.weh, S.wel
        sg, hf = sb("sg", [P, 2, N]), sb("hf", [P, 2, N])
        hh, hl = sb("hh", [P, 2, N], F32R), sb("hl", [P, 2, N], F32R)
        gw = sb("gw", [P, C, E])
        gwh, gwl = (t[:, 0, 0:C * P].rearrange("p (c n) -> p c n", c=C) for t in (hh, hl))
        lg, ex, m8, eq = (sb(n, [P, B, E]) for n in ("lg", "ex", "m8", "eq"))
        ix, ixf = sb("ix", [P, B, E], U32), sb("ixf", [P, B, E])
        mx, rec = sb("mx", [P, B]), sb("rec", [P, B])
        route = sb("route", [P, E + E * E + TILES + 1])
        before, given = sb("before", [P, P]), sb("given", [P, B, E])
        count, tiles, start, end = (sb(n, [P, E]) for n in ("count", "tiles", "start", "end"))
        pairs, slot = sb("pairs", [P, E, E]), sb("slot", [P, B, E])
        posf, past, owner = sb("posf", [P, 2, B]), sb("past", [P, TILES, E]), sb("owner", [P, TILES])
        gate, up, yb = S.bank[0:2], S.bank[2:4], S.bank[4:8]

        raw_in, w_hi, w_lo = sem("raw_in"), sem("w_hi"), sem("w_lo")
        route_in, given_done, ranked = sem("route_in"), sem("given_done"), sem("ranked")
        tile_in = sem("tile_in")
        slots_done, rows_done, scattered = sem("slots_done"), sem("rows_done"), sem("scattered")
        gw_in, gw_zero, gw_hi, gw_lo = sem("gw_in"), sem("gw_zero"), sem("gw_hi"), sem("gw_lo")
        rt_full, rt_copied, lg_full = sem("rt_full"), sem("rt_copied"), sem("lg_full")
        diff_done, ex_done, router_chain = sem("diff_done"), sem("ex_done"), sem("router_chain")
        gate_full, up_full, sig_done = sem("gate_full"), sem("up_full"), sem("sig_done")
        hf_done, hh_done, hl_done = sem("hf_done"), sem("hh_done"), sem("hl_done")
        down_done, y_free = sem("down_done"), sem("y_free")

        blocks = ExitStack()
        block = blocks.enter_context(nc.Block())
        xt = Transposer(S, xth, xtl, sem)

        def up_w(t, s, c, col, width):
            return t[:, s, c * 2 * F1 + col:c * 2 * F1 + col + width]

        def down_w(t, s, j):
            return t[0:FT[j], s, WU + j * DM:WU + (j + 1) * DM]

        def over_experts(eng, body):
            for s in range(2):
                body(s, s == 1)

        @block.sync
        def _(sp):
            sp.dma_start(gw[:, :, :], w["router"]).then_inc(gw_in, 16)
            sp.dma_start(route[:, :], w["route"]).then_inc(route_in, 16)
            sp.dma_start(raw[:, :], w["experts"][E * P:(E + 1) * P, :]).then_inc(raw_in, 16)
            sp.wait_ge(w_lo, 1)
            sp.dma_start(raw[:, :], w["experts"][(E + 1) * P:(E + 2) * P, :]).then_inc(raw_in, 16)

        @block.gpsimd
        def _(pool):
            pool.wait_ge(slots_done, 1)
            for t in range(B):
                for k in range(2):
                    at = bass.IndirectOffsetOnAxis(ap=S.pos[:, k * B + t:k * B + t + 1], axis=0)
                    pool.indirect_dma_start(S.x_slots, at, S.X[:, t, :], None).then_inc(scattered, 16)
                if t % GT == GT - 1:
                    pool.wait_ge(scattered, 16 * 2 * (t + 1))
            pool.wait_ge(rows_done, 1)
            for i in range(2):
                pool.wait_ge(w_lo, i + 2)
                rows = bass.IndirectOffsetOnAxis(ap=S.weight_rows[:, i:i + 1], axis=0)
                pool.indirect_dma_start(raw[:, :], None, w["experts"], rows).then_inc(tile_in, 16)
                pool.wait_ge(tile_in, 16 * (i + 1))

        @block.scalar
        def _(act):
            act.wait_ge(gw_in, 16)
            act.wait_ge(gw_zero, 2)
            act.activation(gwh[:, :, 0:E], gw[:, :, :], ACT.Copy).then_inc(gw_hi, 1)
            for t in range(B):
                xt.on_act(act, t)
            act.wait_ge(raw_in, 16)
            act.activation(weh[:, 0, :], raw[:, :], ACT.Copy).then_inc(w_hi, 1)
            act.wait_ge(diff_done, 1)
            act.activation(ex[:, :, :], lg[:, :, :], ACT.Exp).then_inc(ex_done, 1)

            def body(s, last):
                if s == 0:
                    act.wait_ge(raw_in, 32)
                else:
                    act.wait_ge(tile_in, 16)
                act.wait_ge(gate_full, 2 * Q * s + 1)
                act.activation(weh[:, 1 - s, :], raw[:, :], ACT.Copy).then_inc(w_hi, 1)
                with act.Fori(0, G // 2) as m:
                    t = m * Q
                    for q in range(Q + 1):
                        if q >= 1:
                            act.wait_ge(hf_done, t + (2 * Q * s + q))
                            if q >= 3:
                                act.wait_ge(down_done, t * GT + GT * (2 * Q * s + q - 2))
                            b, r = (q - 1) % 2, FT[(q - 1) % J]
                            act.activation(hh[0:r, b, :], hf[0:r, b, :], ACT.Copy).then_inc(hh_done, 1)
                        if q < Q:
                            act.wait_ge(gate_full, t + (2 * Q * s + q + 1))
                            if q >= 2:
                                act.wait_ge(hf_done, t + (2 * Q * s + q - 1))
                            r = FT[q % J]
                            act.activation(sg[0:r, q % 2, :], gate[q % 2][0:r, :], ACT.Silu).then_inc(sig_done, 1)

            over_experts(act, body)

        @block.vector
        def _(dve):
            rc = Chain(dve, router_chain)
            for t in (gwh, gwl):
                dve.memset(f32(t), 0.0).then_inc(gw_zero, 1)
            dve.wait_ge(gw_hi, 1)
            dve.tensor_tensor(gwl[:, :, 0:E], gw[:, :, :], f32(gwh[:, :, 0:E]), ALU.subtract).then_inc(gw_lo, 1)
            for t in range(B):
                xt.on_dve(dve, t)
            for g in range(G):
                dve.wait_ge(rt_full, g + 1)
                dve.tensor_copy(sg[0:E, g % 2, :], gate[g % 2][0:E, :]).then_inc(rt_copied, 1)
            dve.wait_ge(lg_full, 1)
            b8 = lambda t: t.unsqueeze(2).broadcast_to((P, B, E))
            rc.link(dve.tensor_copy(lg[:, :, :], yb[-1][:, 0:B * E].rearrange("p (t e) -> p t e", e=E)))
            rc.link(dve.tensor_reduce(mx[:, :], lg[:, :, :], AX, ALU.max))
            dve.tensor_tensor(lg[:, :, :], lg[:, :, :], b8(mx[:, :]), ALU.subtract).then_inc(diff_done, 1)
            dve.wait_ge(ex_done, 1)
            rc.link(dve.tensor_reduce(mx[:, :], ex[:, :, :], AX, ALU.add))
            rc.link(dve.reciprocal(rec[:, :], mx[:, :]))
            rc.link(dve.tensor_tensor(ex[:, :, :], ex[:, :, :], b8(rec[:, :]), ALU.mult))
            for t in range(B):
                a = dve.max(out=m8[:, t, :], in_=ex[:, t, :])
            rc.link(a)
            for t in range(B):
                a = dve.max_index(ix[:, t, :], m8[:, t, :], ex[:, t, :])
            rc.link(a)
            rc.link(dve.tensor_copy(ixf[:, :, :], ix[:, :, :]))
            io = S.iota[:, :].unsqueeze(1).broadcast_to((P, B, E))
            for dst, k in ((eq, 0), (lg, 1)):
                rc.link(dve.tensor_tensor(dst[:, :, :], io, b8(ixf[:, :, k]), ALU.is_equal))
            dve.tensor_scalar(before[:, :], S.dist[:, :], 0.0, None, ALU.is_gt)
            rc.link(dve.tensor_tensor(given[:, :, :], eq[:, :, :], lg[:, :, :], ALU.add))
            dve.tensor_copy(S.score[:, :], m8[:, :, 0:2])
            dve.tensor_reduce(count[:, :], given[:, :, :].rearrange("p t e -> p e t"), AX, ALU.add).then_inc(given_done, 1)
            dve.wait_ge(w_hi, 1)
            dve.tensor_tensor(wel[:, 0, :], raw[:, :], f32(weh[:, 0, :]), ALU.subtract).then_inc(w_lo, 1)
            dve.wait_ge(route_in, 16)
            steps = route[:, 0:E].unsqueeze(1).broadcast_to((P, E, E))
            earlier = route[:, E:E + E * E].rearrange("p (a b) -> p a b", b=E)
            tile_ids = route[:, E + E * E:E + E * E + TILES]
            e8 = lambda t: t[:, :].unsqueeze(2).broadcast_to((P, E, E))
            dve.wait_ge(ranked, 1)
            rc.link(dve.tensor_copy(end[:, :], yb[1][:, 0:E]))
            rc.link(dve.tensor_tensor(pairs[:, :, :], e8(end), steps, ALU.is_gt))
            rc.link(dve.tensor_reduce(tiles[:, :], pairs[:, :, :], AX, ALU.add))
            rc.link(dve.tensor_tensor(pairs[:, :, :], earlier, tiles[:, :].unsqueeze(1).broadcast_to((P, E, E)), ALU.mult))
            rc.link(dve.tensor_reduce(start[:, :], pairs[:, :, :], AX, ALU.add))
            rc.link(dve.scalar_tensor_tensor(out=slot[:, :, :], in0=start[:, :].unsqueeze(1).broadcast_to((P, B, E)),
                                             scalar=float(SN), in1=yb[0][:, 0:B * E].rearrange("p (t e) -> p t e", e=E),
                                             op0=ALU.mult, op1=ALU.add))
            for k, own in ((0, eq), (1, lg)):
                a = dve.tensor_tensor(own[:, :, :], own[:, :, :], slot[:, :, :], ALU.mult)
            rc.link(a)
            for k, own in ((0, eq), (1, lg)):
                a = dve.tensor_reduce(posf[:, k, :], own[:, :, :], AX, ALU.add)
            rc.link(a)
            dve.tensor_copy(S.pos[:, :], posf[:, :, :].rearrange("p k t -> p (k t)")).then_inc(slots_done, 1)
            rc.link(dve.tensor_tensor(end[:, :], start[:, :], tiles[:, :], ALU.add))
            rc.link(dve.tensor_tensor(past[:, :, :], tile_ids.unsqueeze(2).broadcast_to((P, TILES, E)),
                                      end[:, :].unsqueeze(1).broadcast_to((P, TILES, E)), ALU.is_ge))
            rc.link(dve.tensor_reduce(owner[:, :], past[:, :, :], AX, ALU.add))
            rc.link(dve.tensor_scalar(owner[:, :], owner[:, :], E - 1.0, float(P), ALU.min, ALU.mult))
            p_id = route[:, E + E * E + TILES:E + E * E + TILES + 1]
            dve.tensor_scalar(S.weight_rows[:, :], owner[:, :], p_id, None, ALU.add).then_inc(rows_done, 1)

            def body(s, last):
                dve.wait_ge(w_hi, s + 2)
                dve.tensor_tensor(wel[:, 1 - s, :], raw[:, :], f32(weh[:, 1 - s, :]), ALU.subtract).then_inc(w_lo, 1)
                with dve.Fori(0, G // 2) as m:
                    t = m * Q

                    def sums(gg):
                        if s == 0:
                            dve.wait_ge(scattered, m * (2 * 16 * 2 * GT) + (gg + 1) * 16 * 2 * GT)
                        for i in range(GT):
                            row = S.X[:, bass.ds(m * (2 * GT) + (gg * GT + i), 1), :].rearrange("p a n -> p (a n)")
                            dve.wait_ge(down_done, t * GT + GT * (2 * Q * s) + (gg * J * GT + (J - 1) * GT + i + 1))
                            dve.tensor_tensor(row, row, yb[i][:, :], ALU.add).then_inc(y_free, 1)

                    for q in range(Q + 1):
                        if q >= 1:
                            b, r = (q - 1) % 2, FT[(q - 1) % J]
                            dve.wait_ge(hh_done, t + (2 * Q * s + q))
                            dve.tensor_tensor(hl[0:r, b, :], hf[0:r, b, :], f32(hh[0:r, b, :]),
                                              ALU.subtract).then_inc(hl_done, 1)
                        if q == J + 1:
                            sums(0)
                        if q < Q:
                            r = FT[q % J]
                            dve.wait_ge(sig_done, t + (2 * Q * s + q + 1))
                            dve.wait_ge(up_full, t + (2 * Q * s + q + 1))
                            if q >= 2:
                                dve.wait_ge(hh_done, t + (2 * Q * s + q - 1))
                            dve.tensor_tensor(hf[0:r, q % 2, :], sg[0:r, q % 2, :], up[q % 2][0:r, :],
                                              ALU.mult).then_inc(hf_done, 1)
                        if q == Q:
                            sums(1)

            over_experts(dve, body)

        @block.tensor
        def _(pe):
            def router_rows(g):
                pe.wait_ge(rt_copied, g + 1)
                for i in range(GT):
                    t = g * GT + i
                    m = pe.transpose(yb[-1][:, t * E:(t + 1) * E], sg[0:E, g % 2, i * P:(i + 1) * P], S.ident[0:E, 0:E])
                return m

            xt.on_pe(pe)
            pe.wait_ge(xt.lo, B)
            pe.wait_ge(gw_lo, 1)
            for g in range(G):
                if g >= 2:
                    pe.wait_ge(rt_copied, g - 1)
                cols = slice(g * N, (g + 1) * N)
                for c in range(C):
                    m = products(pe, gate[g % 2][:, :], gwh[:, c, :], gwl[:, c, :], xth[:, c, cols], xtl[:, c, cols],
                                 c == 0, c == C - 1)
                m.then_inc(rt_full, 1)
                if g >= 1:
                    router_rows(g - 1)
            router_rows(G - 1).then_inc(lg_full, 1)
            pe.wait_ge(given_done, 1)
            pe.matmul(yb[0][:, 0:B * E], before[:, :], given[:, :, :].rearrange("p t e -> p (t e)"), start=True, stop=False)
            for t in range(B - 1):
                n = B - 1 - t
                pe.matmul(yb[0][:, (t + 1) * E:B * E].rearrange("p (t e) -> p t e", e=E), S.ones_f[:, :],
                          given[:, t:t + 1, :].broadcast_to((P, n, E)), start=False, stop=t == B - 2)
            pe.matmul(yb[1][:, 0:E], S.ones_f[:, :], count[:, :], start=True, stop=True).then_inc(ranked, 1)

            def ups(dst, s, col, r, toks):
                for c in range(C):
                    m = products(pe, dst[0:r, :], up_w(weh, s, c, col, r), up_w(wel, s, c, col, r),
                                 xth[:, c, toks], xtl[:, c, toks], c == 0, c == C - 1)
                return m

            def body(s, last):
                with pe.Fori(0, G // 2) as m:
                    pe.wait_ge(w_lo, s + 1)
                    t = m * Q

                    def down(q):
                        j, r = q % J, FT[q % J]
                        pe.wait_ge(hl_done, t + (2 * Q * s + q + 1))
                        if j == 0 and q:
                            pe.wait_ge(y_free, m * (2 * GT) + (B * s + (q // J) * GT))
                        for i in range(GT):
                            cols = slice(i * P, (i + 1) * P)
                            ins = products(pe, yb[i][:, :], hh[0:r, q % 2, cols], hl[0:r, q % 2, cols],
                                           down_w(weh, s, j), down_w(wel, s, j), j == 0, j == J - 1)
                            ins.then_inc(down_done, 1)

                    for q in range(Q):
                        j = q % J
                        toks = bass.ds(m * (2 * N) + (q // J) * N, N)
                        if q >= 2:
                            pe.wait_ge(sig_done, t + (2 * Q * s + q - 1))
                        ups(gate[q % 2], s, j * P, FT[j], toks).then_inc(gate_full, 1)
                        if q >= 2:
                            pe.wait_ge(hf_done, t + (2 * Q * s + q - 1))
                        ups(up[q % 2], s, F1 + j * P, FT[j], toks).then_inc(up_full, 1)
                        if q >= 1:
                            down(q - 1)
                    down(Q - 1)

            over_experts(pe, body)

        blocks.close()


def expert_ffn_phase(nc, S, w):
    WU, WD = 2 * F1 * C, len(FT) * DM
    WE = WU + WD
    J = len(FT)
    PIECES = [slice(0, WU // 2), slice(WU // 2, WU), slice(WU, WE)]
    NP = len(PIECES)
    GB = 4
    with Phase(nc, "expert") as phase:
        sb, sem = phase.sb, phase.sem

        raw = [sb("raw", [P, WE]), S.raw]
        weh, wel = S.weh, S.wel
        xin = sb("xin", [P, 2, ST * DM])
        xgh, xgl = sb("xgh", [P, 2, C, SN], F32R), sb("xgl", [P, 2, C, SN], F32R)
        sg, hf = sb("sg", [P, 2, SN]), sb("hf", [P, 2, SN])
        hh, hl = sb("hh", [P, 2, SN], F32R), sb("hl", [P, 2, SN], F32R)
        ys = sb("ys", [P, 2, ST, DM])
        yg = sb("yg", [P, GB, DM])
        st = [Stats(sb, i) for i in range(2)]
        shift = sb("shift", [P, 2])
        gate, up, yb, tr = S.bank[0:2], S.bank[2:4], S.bank[4:6], S.bank[6:8]

        raw_in = [sem(f"raw_in{b}") for b in range(2)]
        x_in = [sem(f"x_in{b}") for b in range(2)]
        y_out = [sem(f"y_out{b}") for b in range(2)]
        yg_in = [sem(f"yg_in{b}") for b in range(GB)]
        w_hi, w_lo = sem("w_hi"), sem("w_lo")
        tr_full, tr_hi, tr_lo = sem("tr_full"), sem("tr_hi"), sem("tr_lo")
        gate_full, up_full, sig_done = sem("gate_full"), sem("up_full"), sem("sig_done")
        hf_done, hh_done, hl_done = sem("hf_done"), sem("hh_done"), sem("hl_done")
        down_done, y_copied, yg_used = sem("down_done"), sem("y_copied"), sem("yg_used")
        ve_done, rs_done, dve_chain = sem("ve_done"), sem("rs_done"), sem("dve_chain")
        shift_done, x_done, stored = sem("shift_done"), sem("x_done"), sem("stored")

        def over_tiles(eng, body):
            assert TILES % 2 == 1
            for i in range(3):
                body(i, i % 2, i == 0, False)
            with eng.Fori(0, (TILES - 5) // 2) as n:
                for s in range(2):
                    body(n * 2 + (s + 3), (s + 3) % 2, False, False)
            body(TILES - 2, 1, False, False)
            body(TILES - 1, 0, False, True)

        def at_rows(t, i):
            v = t.rearrange("(i a p) n -> i p a n", a=ST, p=P)
            return v[i] if isinstance(i, int) else v[bass.ds(i, 1)].rearrange("o p a n -> (o p) a n")

        blocks = ExitStack()
        block = blocks.enter_context(nc.Block())

        @block.sync
        def _(sp):
            def load(i, b):
                sp.dma_start(xin[:, b, :].rearrange("p (a n) -> p a n", a=ST), at_rows(S.x_slots, i)).then_inc(x_in[b], 16)

            load(0, 0)
            load(1, 1)

            def body(i, b, first, last):
                if not last and not (isinstance(i, int) and i == TILES - 2):
                    sp.wait_ge(tr_full, i * ST + ST)
                    load(i + 2, b)
                sp.wait_ge(y_copied, i * ST + ST)
                sp.dma_start(at_rows(S.y_slots, i), ys[:, b, :, :]).then_inc(y_out[b], 16)

            over_tiles(sp, body)
            with sp.Fori(0, G) as g:
                sp.wait_ge(x_done, g * GT + GT)
                sp.dma_start(S.out_dram[:, bass.ds(g * GT, GT), :], S.X[:, bass.ds(g * GT, GT), :]).then_inc(stored, 16)
            sp.wait_ge(stored, 16 * G)

        @block.gpsimd
        def _(pool):
            for i in range(2, TILES):
                if i >= 3:
                    pool.wait_ge(w_lo, (i - 2) * NP)
                rows = bass.IndirectOffsetOnAxis(ap=S.weight_rows[:, i:i + 1], axis=0)
                pool.indirect_dma_start(raw[i % 2][:, :], None, w["experts"], rows).then_inc(raw_in[i % 2], 16)
            for b in range(2):
                pool.wait_ge(y_out[b], 16 * ((TILES + 1 - b) // 2))

            def norm(t):
                pool.wait_ge(ve_done, t + 1)
                if t >= 2:
                    pool.wait_ge(x_done, t - 1)
                pool.tensor_tensor(out=st[t % 2].rs[:, :], in0=st[t % 2].ve[:, :], in1=S.mhalf[:, :],
                                   op=ALU.pow).then_inc(rs_done, 1)

            for n in range(2 * B):
                t, k = n // 2, n % 2
                if n >= GB:
                    pool.wait_ge(yg_used, n - GB + 1)
                at = bass.IndirectOffsetOnAxis(ap=S.pos[:, k * B + t:k * B + t + 1], axis=0)
                pool.indirect_dma_start(yg[:, n % GB, :], None, S.y_slots, at).then_inc(yg_in[n % GB], 16)
                if k == 1 and n >= GB:
                    norm(t - 2)
            norm(B - 2)
            norm(B - 1)

        @block.scalar
        def _(act):
            def split(i, b, p):
                if p == 0 and not (isinstance(i, int) and i == 1):
                    act.wait_ge(raw_in[b], i * 8 + (-8 if b else 0))
                act.activation(weh[:, b, PIECES[p]], raw[b][:, PIECES[p]], ACT.Copy).then_inc(w_hi, 1)

            def tokens(i, b):
                for a in range(ST):
                    act.wait_ge(tr_full, i * ST + (a + 1))
                    act.activation(xgh[:, b, :, a * P:(a + 1) * P], four(tr[a]), ACT.Copy).then_inc(tr_hi, 1)

            def sums(i, b, fills):
                for a in range(ST):
                    act.wait_ge(down_done, i * (J * ST) + ((J - 1) * ST + a + 1))
                    if a == 0 and fills is not None:
                        act.wait_ge(y_out[b], fills)
                    act.activation(ys[:, b, a, :], yb[a][:, :], ACT.Copy).then_inc(y_copied, 1)

            tokens(0, 0)

            def body(i, b, first, last):
                for j in range(J):
                    q = (b + j) % 2
                    if not first or j >= 1:
                        hidden(i, j - 1, 1 - q, first)
                    if not first and j == 1:
                        early = isinstance(i, int) and i < 3
                        sums(i + -1, 1 - b, None if early else i * 8 + (-8 if b else -16))
                    act.wait_ge(gate_full, i * J + (j + 1))
                    if not first or j >= 2:
                        act.wait_ge(hf_done, i * J + (j - 1))
                    r = FT[j]
                    act.activation(sg[0:r, q, :], gate[q][0:r, 0:SN], ACT.Silu).then_inc(sig_done, 1)
                    if not last and j == 0:
                        tokens(i + 1, 1 - b)
                    if not last and j == 1:
                        if not first:
                            act.wait_ge(down_done, i * (J * ST))
                        split(i + 1, 1 - b, 0)
                        split(i + 1, 1 - b, 1)
                    if not last and j == 2:
                        split(i + 1, 1 - b, 2)

            def hidden(i, j, q, first):
                act.wait_ge(hf_done, i * J + (j + 1))
                if not first or j >= 2:
                    act.wait_ge(down_done, i * (J * ST) + (j - 1) * ST)
                r = FT[j % J]
                act.activation(hh[0:r, q, :], hf[0:r, q, :], ACT.Copy).then_inc(hh_done, 1)

            over_tiles(act, body)
            hidden(TILES - 1, J - 1, (J - 1) % 2, False)
            sums(TILES - 1, 0, 16 * (TILES // 2))
            for t in range(B):
                act.wait_ge(shift_done, t + 1)
                act.activation(S.X[:, t, :], S.X[:, t, :], ACT.Identity, scale=st[t % 2].rs[:, :],
                               bias=shift[:, t % 2:t % 2 + 1]).then_inc(x_done, 1)

        @block.vector
        def _(dve):
            ch = Chain(dve, dve_chain)

            def split(i, b, p):
                dve.wait_ge(w_hi, i * NP + (p + 1 - NP))
                dve.tensor_tensor(wel[:, b, PIECES[p]], raw[b][:, PIECES[p]], f32(weh[:, b, PIECES[p]]),
                                  ALU.subtract).then_inc(w_lo, 1)

            def tokens(i, b):
                for a in range(ST):
                    dve.wait_ge(tr_hi, i * ST + (a + 1))
                    cols = slice(a * P, (a + 1) * P)
                    dve.tensor_tensor(xgl[:, b, :, cols], four(tr[a]), f32(xgh[:, b, :, cols]),
                                      ALU.subtract).then_inc(tr_lo, 1)

            def hidden(i, j, q):
                r = FT[j % J]
                dve.wait_ge(hh_done, i * J + (j + 1))
                dve.tensor_tensor(hl[0:r, q, :], hf[0:r, q, :], f32(hh[0:r, q, :]), ALU.subtract).then_inc(hl_done, 1)

            tokens(0, 0)

            def body(i, b, first, last):
                for j in range(J):
                    q = (b + j) % 2
                    r = FT[j]
                    if not first or j >= 1:
                        hidden(i, j - 1, 1 - q)
                    dve.wait_ge(sig_done, i * J + (j + 1))
                    dve.wait_ge(up_full, i * J + (j + 1))
                    if not first or j >= 2:
                        dve.wait_ge(hh_done, i * J + (j - 1))
                    dve.tensor_tensor(hf[0:r, q, :], sg[0:r, q, :], up[q][0:r, 0:SN], ALU.mult).then_inc(hf_done, 1)
                    if not last:
                        if j == 0:
                            tokens(i + 1, 1 - b)
                        if j == 1:
                            split(i + 1, 1 - b, 0)
                            split(i + 1, 1 - b, 1)
                        if j == 2:
                            split(i + 1, 1 - b, 2)

            over_tiles(dve, body)
            hidden(TILES - 1, J - 1, (J - 1) % 2)

            def shifts(t):
                dve.wait_ge(rs_done, t + 1)
                if t >= 2:
                    dve.wait_ge(x_done, t - 1)
                dve.scalar_tensor_tensor(out=shift[:, t % 2:t % 2 + 1], in0=st[t % 2].mv[:, 0:1], scalar=-1.0,
                                         in1=st[t % 2].rs[:, :], op0=ALU.mult, op1=ALU.mult).then_inc(shift_done, 1)

            for t in range(B):
                for k in range(2):
                    n = 2 * t + k
                    dve.wait_ge(yg_in[n % GB], 16 * (n // GB + 1))
                    if k:
                        dve.wait_ge(yg_used, n)
                    dve.scalar_tensor_tensor(out=S.X[:, t, :], in0=yg[:, n % GB, :], scalar=S.score[:, 2 * t + k:2 * t + k + 1],
                                             in1=S.X[:, t, :], op0=ALU.mult, op1=ALU.add).then_inc(yg_used, 1)
                if t >= 1:
                    shifts(t - 1)
                dve.wait_ge(yg_used, 2 * t + 2)
                norm_stats(dve, ch, S.X[:, t, :], st[t % 2], S).then_inc(ve_done, 1)
            shifts(B - 1)

        @block.tensor
        def _(pe):
            def transposes(i, b, first):
                pe.wait_ge(x_in[b], i * 8 + (8 if b else 16))
                for a in range(ST):
                    if not first:
                        pe.wait_ge(tr_lo, i * ST + (a - ST + 1))
                    for c in range(C):
                        m = pe.transpose(tr[a][:, c * P:(c + 1) * P], xin[:, b, a * DM + c * P:a * DM + (c + 1) * P],
                                         S.ident[:, :])
                    m.then_inc(tr_full, 1)

            def ups(dst, b, col, r):
                for c in range(C):
                    at = slice(c * 2 * F1 + col, c * 2 * F1 + col + r)
                    m = products(pe, dst[0:r, 0:SN], weh[:, b, at], wel[:, b, at], xgh[:, b, c, :], xgl[:, b, c, :],
                                 c == 0, c == C - 1)
                return m

            def down(i, j, q, b, first):
                pe.wait_ge(hl_done, i * J + (j + 1))
                if j == 0 and not first:
                    pe.wait_ge(y_copied, i * ST)
                r = FT[j]
                for a in range(ST):
                    cols = slice(a * P, (a + 1) * P)
                    at = slice(WU + j * DM, WU + (j + 1) * DM)
                    products(pe, yb[a][:, :], hh[0:r, q, cols], hl[0:r, q, cols], weh[0:r, b, at], wel[0:r, b, at],
                             j == 0, j == J - 1).then_inc(down_done, 1)

            transposes(0, 0, True)

            def body(i, b, first, last):
                for j in range(J):
                    q = (b + j) % 2
                    if j == 0:
                        pe.wait_ge(tr_lo, i * ST + ST)
                        if not first:
                            pe.wait_ge(w_lo, i * NP + (2 - NP))
                    if not first or j >= 2:
                        pe.wait_ge(sig_done, i * J + (j - 1))
                    ups(gate[q], b, j * P, FT[j]).then_inc(gate_full, 1)
                    if not first or j >= 2:
                        pe.wait_ge(hf_done, i * J + (j - 1))
                    ups(up[q], b, F1 + j * P, FT[j]).then_inc(up_full, 1)
                    if j == 0 and not first:
                        down(i + -1, J - 1, 1 - q, 1 - b, False)
                    if j == 1 and not first:
                        pe.wait_ge(w_lo, i * NP)
                    if j >= 1:
                        down(i, j - 1, 1 - q, b, first)
                    if j == 0 and not last:
                        transposes(i + 1, 1 - b, False)

            over_tiles(pe, body)
            down(TILES - 1, J - 1, (J - 1) % 2, 0, False)

        blocks.close()


def build(nc, a, out, phases=6):
    with ExitStack() as ctx:
        S = Shared()

        def sb(n, shape, dt=F32):
            return ctx.enter_context(nc.sbuf_tensor(n, shape, dt))

        S.bank = [ctx.enter_context(nc.psum_tensor(f"bank{i}", [P, N], F32)) for i in range(8)]
        S.X = sb("X", [P, B, DM])
        S.ident, S.ones_f = sb("ident", [P, P]), sb("ones_f", [P, P])
        S.ones = sb("ones", [1, P], F32R)
        S.mhalf, S.iota = sb("mhalf", [P, 1]), sb("iota", [P, E])
        S.tern_part = sb("tern_part", [P, 3 * G])
        lower, upper, causal = sb("lower", [P, P]), sb("upper", [P, P]), sb("causal", [P, P])
        S.dist = sb("dist", [P, P])
        S.lower4, S.upper4, S.causal4 = (t[:, :].unsqueeze(1).broadcast_to((P, 4, P)) for t in (lower, upper, causal))
        S.x_dram = a[""]["x"].rearrange("b p n -> p b n")
        S.ctx_dram = a[""]["ctx"].rearrange("b p n -> p b n")
        S.out_dram = out.rearrange("b p n -> p b n")
        S.x_slots, S.y_slots = (nc.dram_tensor(n, (SLOTS, DM), F32).ap() for n in ("x_slots", "y_slots"))
        S.pos, S.weight_rows = sb("pos", [P, 2 * B], U32), sb("weight_rows", [P, TILES], U32)
        S.score = sb("score", [P, 2 * B])
        S.x_kept = nc.dram_tensor("x_kept", (P, B, DM), F32).ap()
        S.ternary = a["ternary"]["w"]
        S.rope_rows, S.rope_cols, S.kv_rope = a[""]["rope_rows"], a[""]["rope_cols"], a[""]["kv_rope"]
        loaded, S.ones_set = ctx.enter_context(nc.semaphore("tables_in")), ctx.enter_context(nc.semaphore("ones_set"))
        tables = [(S.ident, a[""]["ident"]), (lower, a[""]["lower"]), (upper, a[""]["upper"]), (causal, a[""]["causal"]), (S.dist, a[""]["dist"]), (S.iota, a[""]["iota"])]
        with nc.Block() as block:
            @block.sync
            def _(sp):
                for dst, src in tables:
                    sp.dma_start(dst[:, :], src).then_inc(loaded, 16)
                sp.wait_ge(loaded, 16 * len(tables))

            @block.vector
            def _(dve):
                for t, v in ((S.ones_f[:, :], 1.0), (f32(S.ones[:, :]), 1.0), (S.mhalf[:, :], -0.5)):
                    dve.memset(t, v).then_inc(S.ones_set, 1)
                dve.wait_ge(S.ones_set, 3)

        if phases >= 1:
            attention_phase(nc, S, "gqa", a["attn0"])
        if phases >= 2:
            latent_phase(nc, S, a["latent"], 0)
            latent_phase(nc, S, a["latent"], 1)
        if phases >= 3:
            ternary_ffn_phase(nc, S, a["ternary"])
        if phases >= 4:
            attention_phase(nc, S, "decay", a["attn1"])
        if phases >= 5:
            attention_phase(nc, S, "causal", a["cross1"])
        if phases >= 6:
            WE = 2 * F1 * C + len(FT) * DM
            S.raw = sb("weights_raw", [P, WE])
            S.weh, S.wel = sb("weh", [P, 2, WE], F32R), sb("wel", [P, 2, WE], F32R)
            shared_ffn_phase(nc, S, a["expert"])
            expert_ffn_phase(nc, S, a["expert"])
        else:
            with nc.Block() as block:
                dbg = ctx.enter_context(nc.semaphore("dbg"))

                @block.sync
                def _(sp):
                    sp.dma_start(S.out_dram, S.X[:, :, :]).then_inc(dbg, 16)
                    sp.wait_ge(dbg, 16)


def layouts(i):
    import numpy as np

    def lay(t):
        return np.ascontiguousarray(t.reshape(-1, P, t.shape[1]).transpose(1, 0, 2))

    def rows(t):
        return np.ascontiguousarray(np.broadcast_to(t.reshape(1, -1), (P, t.size)))

    def cols(*ts):
        t = np.concatenate([t.reshape(-1, P) for t in ts]).T
        return np.ascontiguousarray(np.concatenate([t, np.zeros((P, 8 - t.shape[1]), t.dtype)], 1))

    o = {"x": i["x"], "ctx": i["ctx_512"]}
    turn = lambda t: t.reshape(KV, H // KV, D, -1).transpose(1, 0, 2, 3).reshape(DM, -1)
    swap = lambda t: t.reshape(-1, 2, D // 2)[:, ::-1].reshape(-1)
    bq, bk = turn(i["L0_attn_bq"]).reshape(-1), i["L0_attn_bk"]
    o |= {"attn0.q": lay(turn(i["L0_attn_wq"]).T), "attn0.k": lay(i["L0_attn_wk"].T), "attn0.v": lay(i["L0_attn_wv"].T),
          "attn0.o": lay(i["L0_attn_wo"].T), "attn0.bqk": cols(bq, bk), "attn0.bqk_swapped": cols(swap(bq), swap(bk)),
          "attn0.bv": rows(i["L0_attn_bv"]), "attn0.bo": i["L0_attn_bo"].reshape(1, -1)}
    w = i["L1_attn_Wqkv"]
    b = i["L1_attn_bqkv"]
    o |= {"attn1.q": lay(w[:, :DM]), "attn1.k": lay(w[:, DM:2 * DM]), "attn1.v": lay(w[:, 2 * DM:]),
          "attn1.o": lay(i["L1_attn_Wout"]), "attn1.bqk": cols(b[:2 * DM]), "attn1.bv": rows(b[2 * DM:]),
          "attn1.bo": i["L1_attn_bout"].reshape(1, -1), "attn1.slopes": rows(i["L1_attn_slopes"])}
    w = i["L1_xattn_Wkv_expand"].T
    o |= {"cross1.q": lay(i["L1_xattn_Wq"].T), "cross1.k": lay(w[:, :DM]), "cross1.v": lay(w[:, DM:]),
          "cross1.o": lay(i["L1_xattn_Wout"].T)}
    o["latent.fold"] = np.concatenate([
        i["L0_xattn_Wq"].reshape(XH, P, DM),
        i["L0_xattn_w_kc_q"].reshape(XH, P, 3, P).transpose(0, 3, 2, 1).reshape(XH, P, 3 * P),
        i["L0_xattn_W_qr"].reshape(XH, 3, P, XR).transpose(0, 2, 1, 3).reshape(XH, P, 3 * XR),
        i["L0_xattn_w_kc_kv"],
        i["L0_xattn_Wo"].T.reshape(XH, P, DM)], 2)
    o["latent.kr"] = np.ascontiguousarray(i["L0_xattn_W_kr"].transpose(1, 0, 2)).reshape(P, -1)
    up = [lay(i[f"L0_ffn_{k}"].T).reshape(P, C, NF0, P).transpose(0, 2, 1, 3).reshape(P, NF0, DM) for k in ("w1", "w2")]
    o["ternary.w"] = np.stack(up + [lay(i["L0_ffn_w3"].T)], 2)
    gu, dn = i["L1_ffn_gate_up_weights"], i["L1_ffn_down_weights"]
    sg, sd = i["L1_ffn_shared_gate_up"].reshape(2, 2, F1, DM), i["L1_ffn_shared_down"].reshape(DM, 2, F1)
    ex = []
    for e in range(NE):
        u = gu[e] if e < E else sg[:, e - E].reshape(2 * F1, DM)
        d = (dn[e] if e < E else sd[:, e - E]).T
        d = np.concatenate([d, np.zeros((len(FT) * P - F1, DM), d.dtype)])
        ex.append(np.concatenate([lay(u.T).reshape(P, -1), lay(d).reshape(P, -1)], 1))
    o["expert.experts"] = np.concatenate(ex)
    o["expert.router"] = lay(i["L1_ffn_gate_weight"].T)
    return {k: np.ascontiguousarray(v) for k, v in o.items()}


def tables():
    import numpy as np
    f = np.float32
    t = np.arange(P)
    inv = (1.0 / f(10000.0) ** (np.arange(0, D, 2, dtype=f) / f(D))).astype(f)

    def rope(pos, inv, repeat):
        fr = pos[:, None].astype(f) * inv[None, :]
        e = np.repeat(fr, 2, -1) if repeat else np.concatenate([fr, fr], -1)
        sn = np.sin(e)
        sn[:, :e.shape[1] // 2] *= -1
        return np.stack([np.cos(e), sn])

    r = rope(np.arange(H), inv, False)
    q = r.reshape(2, KV, H // KV, D).transpose(0, 2, 1, 3).reshape(2, DM)
    qk = np.concatenate([q, r[:, :KV].reshape(2, P)], 1)
    cols = np.concatenate([qk.reshape(2, 5, P), np.zeros((2, 3, P), f)], 1).transpose(2, 0, 1)
    invk = (1.0 / f(10000.0) ** (np.arange(0, P, 2, dtype=f) / f(P))).astype(f)
    d = t[:, None] - t[None, :]
    earlier = np.arange(E)[:, None] > np.arange(E)[None, :]
    route = np.concatenate([np.arange(E) * SN, earlier.reshape(-1), np.arange(TILES)])
    route = np.concatenate([np.tile(route, (P, 1)), t[:, None]], 1)
    o = {"expert.route": route, "ident": np.eye(P), "lower": np.where(d <= 0, np.exp(1.0), 1.0), "upper": np.where(d <= 0, 1.0, 0.0),
         "causal": np.where(d >= 0, 0.0, -1e38), "dist": np.maximum(-d, 0), "iota": np.tile(np.arange(E), (P, 1)),
         "rope_rows": np.broadcast_to(qk, (P, 2, DM + P)), "rope_cols": cols,
         "kv_rope": rope(t, invk, True).transpose(1, 0, 2)}
    return {k: np.ascontiguousarray(v.astype(f)) for k, v in o.items()}


def kernel(**inputs):
    import concourse.bacc as bacc
    import numpy as np
    from concourse.bass_utils import run_bass_kernel_spmd

    arrays = layouts({k: np.asarray(v) for k, v in inputs.items()}) | tables()
    nc = bacc.Bacc("TRN2", target_bir_lowering=False, num_devices=1)
    a = {g: {} for g in ("", "attn0", "latent", "ternary", "attn1", "cross1", "expert")}
    for name, v in arrays.items():
        group, _, key = name.rpartition(".")
        a[group][key] = nc.dram_tensor("in_" + name.replace(".", "_"), v.shape, F32, kind="ExternalInput").ap()
    out = nc.dram_tensor("out", (B, P, DM), F32, kind="ExternalOutput").ap()
    build(nc, a, out)
    r = run_bass_kernel_spmd(nc, [{"in_" + k.replace(".", "_"): v for k, v in arrays.items()}], core_ids=[0])
    return r.results[0]["out"]
```
